# Optimizing a Trainium2 kernel written in Bass

```python
import numpy as np
import jax
import jax.numpy as jnp

def _softmax(x, axis=-1):
    return jax.nn.softmax(x, axis=axis)

def _gelu(x):
    return jax.nn.gelu(x, approximate=True)

def _silu(x):
    return jax.nn.silu(x)

def _sigmoid(x):
    return jax.nn.sigmoid(x)

def _layernorm(x, axis=-1, eps=1e-05):
    m = jnp.mean(x, axis=axis, keepdims=True)
    v = jnp.var(x, axis=axis, keepdims=True)
    return (x - m) / jnp.sqrt(v + eps)

def _scatter_add(tgt, idx, src, axis=0):
    return tgt.at[idx].add(src)

def _segment_sum(src, seg, n):
    return jax.ops.segment_sum(src, seg, n)
kernel_name = 'mk_adaln_d1_jaxref_r8_dfd153'

def setup_inputs(seed: int=0):
    np.random.seed(seed)
    _w = jnp.asarray

    def _L0_attn_setup():
        import jax, jax.numpy as jnp
        import numpy as np
        B, N, D = (4, 256, 128)
        THRESHOLD_FACTOR = 1.25

        def _linear(x, W, b):
            return x @ W.T + b
        key = jax.random.key(seed)
        ks = jax.random.split(key, 8)
        s = 0.02
        return {'hidden_states': jax.random.normal(ks[0], (B, N, D), jnp.float32), 'Wq': jax.random.normal(ks[1], (D, D), jnp.float32) * s, 'bq': jnp.zeros((D,), jnp.float32), 'Wk': jax.random.normal(ks[2], (D, D), jnp.float32) * s, 'bk': jnp.zeros((D,), jnp.float32), 'Wv': jax.random.normal(ks[3], (D, D), jnp.float32) * s, 'bv': jnp.zeros((D,), jnp.float32), 'Wo': jax.random.normal(ks[4], (D, D), jnp.float32) * s, 'bo': jnp.zeros((D,), jnp.float32), 'Wtq': jax.random.normal(ks[5], (2, D), jnp.float32) * s, 'btq': jnp.zeros((2,), jnp.float32), 'Wfq': jax.random.normal(ks[6], (D, 2), jnp.float32) * s, 'bfq': jnp.zeros((D,), jnp.float32)}
    _L0_attn_in = _L0_attn_setup()

    def _L0_ffn_setup():
        import jax, jax.numpy as jnp
        import numpy as np
        B, S, D = (1, 256, 128)
        E, F = (16, 128)
        NG, TKG, K = (4, 2, 4)
        NSH = 2
        SCALE = 2.5
        STD = 0.02
        EPG = E // NG

        def _route(x_flat, router_w, bias):
            logits = x_flat.astype(jnp.float32) @ router_w.T
            scores = jax.nn.sigmoid(logits)
            s = scores + bias[None, :]
            sg = s.reshape(-1, NG, EPG)
            group_score = jax.lax.top_k(sg, 2)[0].sum(-1)
            gidx = jax.lax.top_k(group_score, TKG)[1]
            gmask = jnp.sum(jax.nn.one_hot(gidx, NG, dtype=jnp.float32), axis=1) > 0
            emask = jnp.repeat(gmask, EPG, axis=1)
            masked = jnp.where(emask, s, -1.0)
            topk_idx = jax.lax.top_k(masked, K)[1]
            tw = jnp.take_along_axis(scores, topk_idx, axis=1)
            tw = tw / (tw.sum(-1, keepdims=True) + 1e-20)
            tw = tw * SCALE
            return (topk_idx, tw)
        key = jax.random.key(seed)
        ks = jax.random.split(key, 8)
        return {'hidden_states': jax.random.normal(ks[0], (B, S, D), jnp.float32), 'router_w': jax.random.normal(ks[1], (E, D), jnp.float32) * STD, 'bias': jnp.zeros((E,), jnp.float32), 'gate_w': jax.random.normal(ks[2], (E, D, F), jnp.float32) * STD, 'up_w': jax.random.normal(ks[3], (E, D, F), jnp.float32) * STD, 'down_w': jax.random.normal(ks[4], (E, F, D), jnp.float32) * STD, 'sh_gate_w': jax.random.normal(ks[5], (D, NSH * F), jnp.float32) * STD, 'sh_up_w': jax.random.normal(ks[6], (D, NSH * F), jnp.float32) * STD, 'sh_down_w': jax.random.normal(ks[7], (NSH * F, D), jnp.float32) * STD}
    _L0_ffn_in = _L0_ffn_setup()
    _L0_c = _w((lambda *s: np.random.randn(*s).astype(np.float32) * 0.05)(2, 128))
    _L0_wmod = _w((lambda *s: np.random.randn(*s).astype(np.float32) * 0.05)(128, 6 * 128) * 128 ** (-0.5))
    _d = {'L0_attn_hidden_states': _L0_attn_in['hidden_states'], 'L0_attn_Wq': _L0_attn_in['Wq'], 'L0_attn_bq': _L0_attn_in['bq'], 'L0_attn_Wk': _L0_attn_in['Wk'], 'L0_attn_bk': _L0_attn_in['bk'], 'L0_attn_Wv': _L0_attn_in['Wv'], 'L0_attn_bv': _L0_attn_in['bv'], 'L0_attn_Wo': _L0_attn_in['Wo'], 'L0_attn_bo': _L0_attn_in['bo'], 'L0_attn_Wtq': _L0_attn_in['Wtq'], 'L0_attn_btq': _L0_attn_in['btq'], 'L0_attn_Wfq': _L0_attn_in['Wfq'], 'L0_attn_bfq': _L0_attn_in['bfq'], 'L0_ffn_router_w': _L0_ffn_in['router_w'], 'L0_ffn_bias': _L0_ffn_in['bias'], 'L0_ffn_gate_w': _L0_ffn_in['gate_w'], 'L0_ffn_up_w': _L0_ffn_in['up_w'], 'L0_ffn_down_w': _L0_ffn_in['down_w'], 'L0_ffn_sh_gate_w': _L0_ffn_in['sh_gate_w'], 'L0_ffn_sh_up_w': _L0_ffn_in['sh_up_w'], 'L0_ffn_sh_down_w': _L0_ffn_in['sh_down_w'], 'L0_c': _L0_c, 'L0_wmod': _L0_wmod}
    _x0 = _d['L0_attn_hidden_states']
    _d['L0_attn_hidden_states'] = jax.random.normal(jax.random.fold_in(jax.random.key(seed), 1), (2, 2048, 128), dtype=_x0.dtype)
    del _x0
    return _d

def reference(L0_attn_hidden_states, L0_attn_Wq, L0_attn_bq, L0_attn_Wk, L0_attn_bk, L0_attn_Wv, L0_attn_bv, L0_attn_Wo, L0_attn_bo, L0_attn_Wtq, L0_attn_btq, L0_attn_Wfq, L0_attn_bfq, L0_ffn_router_w, L0_ffn_bias, L0_ffn_gate_w, L0_ffn_up_w, L0_ffn_down_w, L0_ffn_sh_gate_w, L0_ffn_sh_up_w, L0_ffn_sh_down_w, L0_c, L0_wmod):

    def _L0_attn_ref(hidden_states, Wq, bq, Wk, bk, Wv, bv, Wo, bo, Wtq, btq, Wfq, bfq):
        import jax, jax.numpy as jnp
        import numpy as np
        B, N, D = (4, 256, 128)
        THRESHOLD_FACTOR = 1.25

        def _linear(x, W, b):
            return x @ W.T + b
        d = hidden_states.shape[-1]
        q = _linear(hidden_states, Wq, bq)
        k = _linear(hidden_states, Wk, bk)
        v = _linear(hidden_states, Wv, bv)
        scores = jnp.einsum('bid,bjd->bij', q, k) / jnp.sqrt(jnp.asarray(d, (scores_dtype := q.dtype)))
        qp = _linear(hidden_states, Wtq, btq)
        diff = qp[:, :, None, :] - qp[:, None, :, :]
        dist_sq = jnp.sum(diff * diff, axis=-1)
        phase_diff = jnp.arctan2(diff[..., 1], diff[..., 0])
        forward_bias = 0.5 * (1.0 + jnp.cos(phase_diff))
        mean_dist = jnp.mean(dist_sq, axis=(-1, -2), keepdims=True)
        std_dist = jnp.std(dist_sq, axis=(-1, -2), keepdims=True, ddof=1)
        threshold = mean_dist + THRESHOLD_FACTOR * std_dist
        n = dist_sq.shape[-1]
        causal = jnp.tril(jnp.ones((n, n), bool))
        valid = (dist_sq <= threshold) & causal[None]
        binary_attn = valid.astype(scores.dtype) * forward_bias
        masked = jnp.where(binary_attn == 0, -jnp.inf, scores)
        weights = jax.nn.softmax(masked, axis=-1)
        context = jnp.einsum('bij,bjd->bid', weights, v)
        output = _linear(context, Wo, bo)
        r_embed = qp / jnp.maximum(jnp.linalg.norm(qp, axis=-1, keepdims=True), 1e-12)
        quantum_output = _linear(r_embed, Wfq, bfq)
        return hidden_states + output + 0.1 * quantum_output

    def _L0_ffn_ref(hidden_states, router_w, bias, gate_w, up_w, down_w, sh_gate_w, sh_up_w, sh_down_w):
        import jax, jax.numpy as jnp
        import numpy as np
        B, S, D = (1, 256, 128)
        E, F = (16, 128)
        NG, TKG, K = (4, 2, 4)
        NSH = 2
        SCALE = 2.5
        STD = 0.02
        EPG = E // NG

        def _route(x_flat, router_w, bias):
            logits = x_flat.astype(jnp.float32) @ router_w.T
            scores = jax.nn.sigmoid(logits)
            s = scores + bias[None, :]
            sg = s.reshape(-1, NG, EPG)
            group_score = jax.lax.top_k(sg, 2)[0].sum(-1)
            gidx = jax.lax.top_k(group_score, TKG)[1]
            gmask = jnp.sum(jax.nn.one_hot(gidx, NG, dtype=jnp.float32), axis=1) > 0
            emask = jnp.repeat(gmask, EPG, axis=1)
            masked = jnp.where(emask, s, -1.0)
            topk_idx = jax.lax.top_k(masked, K)[1]
            tw = jnp.take_along_axis(scores, topk_idx, axis=1)
            tw = tw / (tw.sum(-1, keepdims=True) + 1e-20)
            tw = tw * SCALE
            return (topk_idx, tw)
        x = hidden_states.reshape(-1, D)
        topk_idx, tw = _route(x, router_w, bias)
        combine = (jax.nn.one_hot(topk_idx, E, dtype=tw.dtype) * tw[..., None]).sum(1)
        h = jnp.einsum('td,edf->etf', x, gate_w)
        u = jnp.einsum('td,edf->etf', x, up_w)
        y = jnp.einsum('etf,efd->etd', jax.nn.silu(h) * u, down_w)
        routed = jnp.einsum('etd,te->td', y, combine)
        sh = jax.nn.silu(x @ sh_gate_w) * (x @ sh_up_w) @ sh_down_w
        return (routed + sh).reshape(hidden_states.shape)
    x = L0_attn_hidden_states
    mod = (_silu(L0_c) @ L0_wmod).reshape(L0_c.shape[0], 6, 1, -1)
    sa, ca, ga, sb, cb, gb = (mod[:, 0], mod[:, 1], mod[:, 2], mod[:, 3], mod[:, 4], mod[:, 5])
    ga = (2 * (ga >= 0) - 1) * jnp.maximum(jnp.abs(ga), 0.25)
    gb = (2 * (gb >= 0) - 1) * jnp.maximum(jnp.abs(gb), 0.25)
    h = _layernorm(x, axis=-1) * (1 + ca) + sa
    x = x + ga * _L0_attn_ref(h, L0_attn_Wq, L0_attn_bq, L0_attn_Wk, L0_attn_bk, L0_attn_Wv, L0_attn_bv, L0_attn_Wo, L0_attn_bo, L0_attn_Wtq, L0_attn_btq, L0_attn_Wfq, L0_attn_bfq)
    h = _layernorm(x, axis=-1) * (1 + cb) + sb
    x = x + gb * _L0_ffn_ref(h, L0_ffn_router_w, L0_ffn_bias, L0_ffn_gate_w, L0_ffn_up_w, L0_ffn_down_w, L0_ffn_sh_gate_w, L0_ffn_sh_up_w, L0_ffn_sh_down_w)
    return x

_drawn_inputs = setup_inputs


def setup_inputs(seed=0):
    import zlib

    import numpy as np

    out = dict(_drawn_inputs(seed))
    spreads = {'L0_attn_bq': (0.0, 0.8),
     'L0_attn_bk': (0.0, 0.8),
     'L0_attn_bv': (0.0, 0.8),
     'L0_attn_bo': (0.0, 0.329),
     'L0_attn_btq': (0.0, 0.8),
     'L0_attn_bfq': (0.0, 0.8),
     'L0_ffn_bias': (0.0, 0.8)}
    factors = {'L0_attn_Wq': 8.0,
     'L0_attn_Wk': 8.0,
     'L0_attn_Wv': 8.0,
     'L0_attn_Wo': 8.0,
     'L0_attn_Wtq': 8.0,
     'L0_attn_Wfq': 8.0,
     'L0_ffn_router_w': 8.0,
     'L0_ffn_gate_w': 8.0,
     'L0_ffn_up_w': 8.0,
     'L0_ffn_down_w': 8.0,
     'L0_ffn_sh_gate_w': 8.0,
     'L0_ffn_sh_up_w': 8.0,
     'L0_ffn_sh_down_w': 8.0}
    for name, (base, spread) in spreads.items():
        noise = np.random.default_rng([zlib.crc32(name.encode()), seed]).standard_normal(out[name].shape)
        drawn = base * np.exp(spread * noise) if base else spread * noise
        out[name] = jnp.asarray(drawn.astype(out[name].dtype))
    for name, factor in factors.items():
        out[name] = (out[name] * factor).astype(out[name].dtype)
    return out
```

```python
from contextlib import ExitStack

import numpy as np

import concourse.bass as bass
from concourse import mybir

F32 = mybir.dt.float32
BF16 = mybir.dt.bfloat16
U32 = mybir.dt.uint32
ALU = mybir.AluOpType
ACT = mybir.ActivationFunctionType
X = mybir.AxisListType.X

P = 128
NB = 2
N = 2048
BLK = N // P
W = 512
CH = N // W
PER = W // P
E = 16
NS = 2
EX = E + NS
GRP = 4
EPG = E // GRP
TOP = 4
SCALE = 2.5
EPS = 1e-5
NEAR = 0.25

WEDGE = 2.4417243e-4
HUGE = float(2.0 ** 90)
HUGER = float(2.0 ** 110)
FEAT = 27
TINY = 1e-30

CHUNKS_ROW = [(i + PER) // PER for i in range(BLK)]
CHUNKS_BEFORE = [sum(CHUNKS_ROW[:i]) for i in range(BLK + 1)]


class Chain:

    def __init__(self, engine, semaphore):
        self.engine, self.semaphore, self.n = engine, semaphore, 0

    def step(self, instruction):
        instruction.then_inc(self.semaphore, 1)
        self.n += 1

    def settle(self):
        self.engine.wait_ge(self.semaphore, self.n)


def build(nc, hs, Wq, bq, Wk, bk, Wv, bv, Wo, bo, Wtq, btq, Wfq, bfq, router_w, router_b,
          gate_w, up_w, down_w, sh_gate_w, sh_up_w, sh_down_w, cvec, wmod, out):
    ctx = ExitStack()
    with ctx:
        def sb(name, shape, dt=F32):
            return ctx.enter_context(nc.sbuf_tensor(name, shape, dt))

        def sem(name):
            return ctx.enter_context(nc.semaphore(name))

        bank = [ctx.enter_context(nc.psum_tensor(f"bank{i}", [P, W], F32)) for i in range(8)]

        wq = sb("wq", [P, P]); wk = sb("wk", [P, P]); wv = sb("wv", [P, P]); wo = sb("wo", [P, P])
        wT = sb("wT", [P, 3, P])
        rw = sb("rw", [E, P]); rT = sb("rT", [P, E])
        wtq = sb("wtq", [2, P]); tqT = sb("tqT", [P, 2])
        wfq = sb("wfq", [P, 2])
        cols = sb("cols", [P, 5])
        btq_bc = sb("btq_bc", [P, 2])
        rb_bc = sb("rb_bc", [P, E])
        c2 = sb("c2", [NB, P]); sc2 = sb("sc2", [NB, P]); sc = sb("sc", [P, NB]); scb = sb("scb", [P, NB, P])
        wm = sb("wm", [P, 6 * P])
        md = sb("md", [P, 6, NB])
        gbc = sb("gbc", [P, NB, 2, P])
        vh = sb("vh", [P, NB, 2, P])
        x3 = sb("x3", [P, 3]); qw = sb("qw", [3, NB, P])
        wg = sb("wg", [P, EX, P]); wu = sb("wu", [P, EX, P]); wd = sb("wd", [P, EX, P])
        ident = sb("ident", [P, P]); identb = sb("identb", [P, P], BF16)
        minus = sb("minus", [P, P], BF16)
        causal = sb("causal", [P, P], BF16)
        ones = sb("ones", [P, P])
        selw = sb("selw", [3 * E, E, P], BF16)
        selx = sb("selx", [FEAT, P], BF16); sely = sb("sely", [FEAT, P], BF16)
        vw = sb("vw", [P, 5])

        x = sb("x", [P, NB * BLK, P])
        x1 = sb("x1", [P, BLK, P])
        hT = sb("hT", [P, N]); qT = sb("qT", [P, N]); kT = sb("kT", [P, N])
        v = sb("v", [P, BLK, P])
        xb = sb("xb", [P, N]); yb = sb("yb", [P, N])
        off = sb("off", [P, 2, N])
        pen = sb("pen", [P, 2, W], BF16)
        sm = sb("sm", [P, 2, N])
        pr = sb("pr", [P, 2, N])
        gsgn, gmag, graw = (sm[:, 0, k * W:(k + 1) * W] for k in range(3))
        xn = pr[:, 0, :].rearrange("p (i d) -> p i d", d=P)
        ptr = sb("ptr", [P, 2, W])
        st = sb("st", [P, BLK, 6]); mv = sb("mv", [P, BLK, 2])
        ve = sb("ve", [P, BLK]); sd = sb("sd", [P, BLK]); rs = sb("rs", [P, BLK]); tt = sb("tt", [P, BLK])
        qp = sb("qp", [P, BLK, 2]); qc = sb("qc", [P, BLK, 2]); sq = sb("sq", [P, BLK, 2])
        nrm = sb("nrm", [P, BLK]); rea = sb("rea", [P, BLK, 3]); reT = sb("reT", [3, N])
        part = sb("part", [P, 2]); mean = sb("mean", [P, 2])
        mom = sb("mom", [P, 5, BLK]); mpart = sb("mpart", [P, 5]); msum = sb("msum", [P, 5])
        m2 = sb("m2", [P, 5]); var = sb("var", [P, 1]); sdv = sb("sdv", [P, 1]); tv = sb("tv", [P, 1])
        thr = sb("thr", [P, 1])
        quant = sb("quant", [P, BLK, 5])
        rest = sb("rest", [P, BLK, 5])
        parts = sb("parts", [P, 3, BLK, 5], BF16)
        fl = sb("fl", [P, BLK, FEAT], BF16); fr = sb("fr", [P, BLK, FEAT], BF16)
        flT = sb("flT", [FEAT, N], BF16); frT = sb("frT", [FEAT, N], BF16)
        xi = sb("xi", [P, BLK]); nyi = sb("nyi", [P, BLK])
        mx = sb("mx", [P, BLK, CH]); nmx = sb("nmx", [P, BLK])
        rsum = sb("rsum", [P, BLK]); rinv = sb("rinv", [P, BLK])
        sig = sb("sig", [P, BLK, E]); score = sb("score", [P, BLK, E])
        pm = sb("pm", [P, BLK, GRP, 2, 2]); ps2 = sb("ps2", [P, BLK, GRP, 2]); ps3 = sb("ps3", [P, BLK, GRP, 2])
        gs = sb("gs", [P, BLK, GRP])
        gcmp, geq = (off[:, 0, k * BLK * E:(k + 1) * BLK * E].rearrange("p (i g o) -> p i g o", i=BLK, g=GRP)
                     for k in range(2))
        hit, hits, crest = (off[:, 0, k * BLK * E:(k + 1) * BLK * E].rearrange("p (i e) -> p i e", i=BLK)
                            for k in range(2, 5))
        tri = sb("tri", [P, GRP, GRP])
        grank = sb("grank", [P, BLK, GRP]); gsel = sb("gsel", [P, BLK, GRP])
        best = sb("best", [P, BLK, 8]); bidx = sb("bidx", [P, BLK, 8], U32); bf = sb("bf", [P, BLK, 8])
        iota = sb("iota", [P, E]); iotai = sb("iotai", [P, E], mybir.dt.int32)
        wsum = sb("wsum", [P, BLK]); comb = sb("comb", [P, BLK, E])
        cpart = sb("cpart", [P, BLK, 3, E], BF16); combT = kT[0:3 * E, 0:N // 2].bitcast(BF16)
        sg = sm[:, 0, 0:2 * W].rearrange("p (n w) -> p n w", n=2)
        sw = sm[:, 0, 2 * W:4 * W].rearrange("p (n w) -> p n w", n=2)
        act_g = sm[:, 1, 0:2 * W].rearrange("p (n w) -> p n w", n=2)
        ysb = sm[:, 1, 2 * W:3 * W]

        small_loaded = sem("small_loaded"); x_loaded = sem("x_loaded"); experts_loaded = sem("experts_loaded")
        consts_ready = sem("consts_ready"); pool_step = sem("pool_step")
        set_pe = sem("set_pe")
        set_act = sem("set_act")
        set_dve = sem("set_dve")
        dve_step = sem("dve_step")
        root_asked = sem("root_asked"); root_ready = sem("root_ready")
        norm_ready = sem("norm_ready"); norm_turned = sem("norm_turned"); h_ready = sem("h_ready")
        pos_ready = sem("pos_ready")
        part_ready = sem("part_ready"); part_summed = sem("part_summed")
        q_made = sem("q_made"); q_ready = sem("q_ready")
        unit_ready = sem("unit_ready"); unit_turned = sem("unit_turned"); unit_copied = sem("unit_copied")
        feat_ready = sem("feat_ready"); feat_turned = sem("feat_turned"); feat_copied = sem("feat_copied")
        v_made = sem("v_made"); base_made = sem("base_made"); v_ready = sem("v_ready"); base_ready = sem("base_ready")
        spread_made = sem("spread_made"); spread_ready = sem("spread_ready")
        dist_made = sem("dist_made"); dist_used = sem("dist_used")
        scores_made = sem("scores_made"); scores_masked = sem("scores_masked")
        rise_ready = sem("rise_ready")
        max_ready = sem("max_ready"); probs_ready = sem("probs_ready")
        probs_turned = sem("probs_turned"); turned_copied = sem("turned_copied")
        turned_used = sem("turned_used"); row_made = sem("row_made"); row_ready = sem("row_ready")
        logits_made = sem("logits_made"); sig_ready = sem("sig_ready")
        comb_ready = sem("comb_ready"); comb_turned = sem("comb_turned"); comb_copied = sem("comb_copied")
        gate_made = sem("gate_made"); up_made = sem("up_made"); silu_ready = sem("silu_ready")
        silu_weighted = sem("silu_weighted"); act_ready = sem("act_ready"); down_made = sem("down_made")
        y_copied = sem("y_copied"); y_turned = sem("y_turned"); out_scaled = sem("out_scaled")
        out_ready = sem("out_ready"); stored = sem("stored")

        block = ctx.enter_context(nc.Block())
        SMALL = 16

        def batch_view(t):
            return t.rearrange("b (n p) d -> p (b n) d", p=P)

        @block.sync
        def _(sp):
            sp.dma_start(x[:, 0:BLK, :], batch_view(hs)[:, 0:BLK, :]).then_inc(x_loaded, 16)
            sp.dma_start(c2[:, :], cvec).then_inc(small_loaded, 16)
            sp.dma_start(wm[:, :], wmod).then_inc(small_loaded, 16)
            for dst, src in ((wq, Wq), (wk, Wk), (wv, Wv), (wo, Wo), (rw, router_w), (wtq, Wtq), (wfq, Wfq)):
                sp.dma_start(dst[:, :], src).then_inc(small_loaded, 16)
            for n, src in enumerate((bq, bk, bv, bo, bfq)):
                sp.dma_start(cols[:, n:n + 1], src.rearrange("(d o) -> d o", o=1)).then_inc(small_loaded, 16)
            sp.dma_start(btq_bc[:, :], btq.rearrange("(o d) -> o d", o=1).broadcast_to([P, 2])).then_inc(small_loaded, 16)
            sp.dma_start(rb_bc[:, :], router_b.rearrange("(o d) -> o d", o=1).broadcast_to([P, E])).then_inc(small_loaded, 16)
            sp.wait_ge(x_loaded, 16)
            sp.dma_start(x[:, BLK:, :], batch_view(hs)[:, BLK:NB * BLK, :]).then_inc(x_loaded, 16)
            sp.dma_start(wg[:, 0:E, :], gate_w.rearrange("e d f -> d e f")).then_inc(experts_loaded, 16)
            sp.dma_start(wu[:, 0:E, :], up_w.rearrange("e d f -> d e f")).then_inc(experts_loaded, 16)
            sp.dma_start(wd[:, 0:E, :], down_w.rearrange("e f d -> f e d")).then_inc(experts_loaded, 16)
            sp.dma_start(wg[:, E:EX, :], sh_gate_w.rearrange("d (s f) -> d s f", s=NS)).then_inc(experts_loaded, 16)
            sp.dma_start(wu[:, E:EX, :], sh_up_w.rearrange("d (s f) -> d s f", s=NS)).then_inc(experts_loaded, 16)
            sp.dma_start(wd[:, E:EX, :], sh_down_w.rearrange("(s f) d -> f s d", s=NS)).then_inc(experts_loaded, 16)
            with sp.Fori(0, NB * CH) as it:
                sp.wait_ge(out_ready, it + 1)
                sp.dma_start(batch_view(out)[:, bass.ds(it * PER, PER), :],
                             x[:, bass.ds(it * PER, PER), :]).then_inc(stored, 16)
            sp.wait_ge(stored, 16 * NB * CH)

        @block.gpsimd
        def _(pool):
            chain = Chain(pool, pool_step)
            chain.step(pool.memset(ident[:, :], 0.0))
            chain.step(pool.memset(ones[:, :], 1.0))
            chain.step(pool.memset(causal[:, :], 0.0))
            chain.step(pool.memset(selw[:, :, :], 0.0))
            chain.step(pool.memset(selx[:, :], 0.0))
            chain.step(pool.memset(sely[:, :], HUGE))
            chain.step(pool.memset(tri[:, :, :], 0.0))
            chain.step(pool.memset(fl[:, :, :], 0.0))
            chain.step(pool.memset(fr[:, :, :], 0.0))
            chain.step(pool.memset(rea[:, :, :], 1.0))
            chain.step(pool.memset(minus[:, :], 0.0))
            chain.step(pool.memset(identb[:, :], 0.0))
            chain.step(pool.iota(iotai[:, :], pattern=[[1, E]], base=0, channel_multiplier=0))
            w_den = float(N) * N - 1
            for n, wgt in enumerate((4.0, 8.0, 4.0, -2.0, 2.0 * N)):
                chain.step(pool.memset(vw[:, n:n + 1], wgt / w_den))
            chain.settle()
            chain.step(pool.affine_select(out=ident[:, :], in_=ident[:, :], compare_op=ALU.not_equal, fill=1.0,
                                          base=0, pattern=[[-1, P]], channel_multiplier=1))
            chain.step(pool.affine_select(out=identb[:, :], in_=identb[:, :], compare_op=ALU.not_equal, fill=1.0,
                                          base=0, pattern=[[-1, P]], channel_multiplier=1))
            chain.step(pool.affine_select(out=minus[:, :], in_=minus[:, :], compare_op=ALU.not_equal, fill=-HUGER,
                                          base=0, pattern=[[-1, P]], channel_multiplier=1))
            chain.step(pool.affine_select(out=causal[:, :], in_=causal[:, :], compare_op=ALU.is_ge, fill=1.0,
                                          base=0, pattern=[[-1, P]], channel_multiplier=1))
            for k in range(3):
                chain.settle()
                chain.step(pool.affine_select(out=selw[:, :, :], in_=selw[:, :, :], compare_op=ALU.not_equal,
                                              fill=1.0, base=-E * k, pattern=[[-1, E], [0, P]],
                                              channel_multiplier=1))
            chain.step(pool.affine_select(out=tri[:, :, :], in_=tri[:, :, :], compare_op=ALU.is_ge, fill=1.0,
                                          base=0, pattern=[[-1, GRP], [1, GRP]], channel_multiplier=0))
            chain.step(pool.memset(selx[0:3, :], HUGE))
            chain.step(pool.affine_select(out=sely[:, :], in_=sely[:, :], compare_op=ALU.is_ge, fill=0.0,
                                          base=-(FEAT - 3), pattern=[[0, P]], channel_multiplier=1))
            chain.step(pool.tensor_copy(iota[:, :], iotai[:, :]))
            chain.step(pool.memset(fr[:, :, 18:21], 1.0))
            chain.step(pool.memset(fl[:, :, 21:24], HUGE))
            chain.settle()
            pool.sem_inc(consts_ready, 1)

        @block.scalar
        def _(act):
            act.wait_ge(small_loaded, 16 * (SMALL))
            act.activation(sc2[:, :], c2[:, :], ACT.Silu).then_inc(set_act, 1)
            act.wait_ge(set_dve, 2)
            for b in range(NB):
                def layer(which):
                    n = 4 * b + (1 if which == 0 else 4)
                    act.wait_ge(root_asked, n)
                    act.activation(sd[:, :], ve[:, :], ACT.Sqrt).then_inc(root_ready, 1)
                    for g in range(CH):
                        act.wait_ge(norm_turned, 2 * CH * b + which * CH + g + 1)
                        act.activation(hT[:, g * W:(g + 1) * W], bank[g][:, :], ACT.Identity,
                                       bias=md[:, 3 * which, b:b + 1],
                                       scale=md[:, 3 * which + 1, b:b + 1]).then_inc(h_ready, 1)

                layer(0)
                for n in range(2 * CH):
                    dst, g = (qT, kT)[n // CH], n % CH
                    act.wait_ge(q_made, 2 * CH * b + n + 1)
                    act.activation(dst[:, g * W:(g + 1) * W], bank[g][:, :], ACT.Identity,
                                   bias=cols[:, n // CH:n // CH + 1]).then_inc(q_ready, 1)
                    if n == 2:
                        act.wait_ge(root_asked, 4 * b + 2)
                        act.activation(sd[:, :], nrm[:, :], ACT.Sqrt).then_inc(root_ready, 1)
                    if n == 5:
                        act.wait_ge(root_asked, 4 * b + 3)
                        act.activation(sdv[:, :], var[:, :], ACT.Sqrt).then_inc(root_ready, 1)
                for i in range(BLK):
                    act.wait_ge(v_made, BLK * b + i + 1)
                    act.copy(v[:, i, :], bank[4 + i % 2][:, 0:P]).then_inc(v_ready, 1)
                for n in range(2 * CH):
                    dst, g = (xb, yb)[n // CH], n % CH
                    act.wait_ge(spread_made, 2 * CH * b + n + 1)
                    act.copy(dst[:, g * W:(g + 1) * W], bank[g][:, :]).then_inc(spread_ready, 1)
                def rise(i):
                    if i >= 2:
                        act.wait_ge(dist_used, CHUNKS_BEFORE[BLK] * b + CHUNKS_BEFORE[i - 1])
                    L = (i + 1) * P
                    act.activation(off[:, i % 2, 0:L], yb[:, 0:L], ACT.Abs, bias=nyi[:, i:i + 1])\
                       .then_inc(rise_ready, 1)

                act.wait_ge(spread_ready, 2 * CH * (b + 1))
                rise(0)
                for i in range(BLK):
                    L = (i + 1) * P
                    if i + 1 < BLK:
                        rise(i + 1)
                    act.wait_ge(max_ready, BLK * b + i + 1)
                    if i >= 2:
                        act.wait_ge(probs_turned, CHUNKS_BEFORE[BLK] * b + CHUNKS_BEFORE[i - 1])
                    act.activation(pr[:, i % 2, 0:L], sm[:, i % 2, 0:L], ACT.Exp, bias=nmx[:, i:i + 1],
                                   accum_out=rsum[:, i:i + 1]).then_inc(probs_ready, 1)
                    for g in range(CHUNKS_ROW[i]):
                        n = CHUNKS_BEFORE[i] + g
                        w = min(W, L - g * W)
                        act.wait_ge(probs_turned, CHUNKS_BEFORE[BLK] * b + n + 1)
                        if n >= 2:
                            act.wait_ge(turned_used, CHUNKS_BEFORE[BLK] * b + n - 1)
                        act.copy(ptr[:, n % 2, 0:w], bank[4 + n % 2][:, 0:w]).then_inc(turned_copied, 1)
                layer(1)
                act.wait_ge(logits_made, b + 1)
                act.activation(sig[:, :, :], bank[4][:, 0:BLK * E], ACT.Sigmoid).then_inc(sig_ready, 1)
                with act.Fori(0, CH) as c:
                    it = b * CH + c
                    for e in range(EX):
                        act.wait_ge(gate_made, EX * it + e + 1)
                        if e >= 2:
                            act.wait_ge(act_ready, EX * it + e - 1)
                        act.activation(sg[:, e % 2, :], bank[e % 2][:, :], ACT.Silu).then_inc(silu_ready, 1)
                    act.wait_ge(down_made, EX * (it + 1))
                    act.copy(ysb[:, :], bank[6][:, :]).then_inc(y_copied, 1)

        @block.tensor
        def _(pe):
            mm = pe.matmul
            pe.wait_ge(small_loaded, 16 * (SMALL))
            pe.wait_ge(consts_ready, 1)
            for n, w in enumerate((wq, wk, wo)):
                pe.transpose(bank[0][:, n * P:(n + 1) * P], w[:, :], ident[:, :])
            pe.transpose(bank[1][:, 0:E], rw[:, :], ident[0:E, 0:E])
            pe.transpose(bank[1][:, E:E + 2], wtq[:, :], ident[0:2, 0:2])
            pe.wait_ge(set_act, 1)
            pe.transpose(bank[1][:, E + 2:E + 2 + NB], sc2[:, :], ident[0:NB, 0:NB]).then_inc(set_pe, 1)
            pe.wait_ge(set_dve, 1)
            for j in range(6):
                last = mm(bank[2][:, NB * j:NB * (j + 1)], wm[:, j * P:(j + 1) * P], sc[:, :], start=True, stop=True)
            last.then_inc(set_pe, 1)
            for b in range(NB):
                for n, j in enumerate((2, 5)):
                    o = (2 * b + n) * P
                    last = mm(bank[3][:, o:o + P], scb[:, b, :], wm[:, j * P:(j + 1) * P], start=True, stop=True)
            last.then_inc(set_pe, 1)
            pe.wait_ge(set_dve, 2)
            mm(bank[4][:, 0:P], wv[:, :], wT[:, 2, :], start=True, stop=True)
            mm(bank[4][:, P:P + 1], wT[:, 2, :], cols[:, 2:3], start=True, stop=True).then_inc(set_pe, 1)
            pe.wait_ge(set_dve, 3)
            pe.transpose(bank[5][0:3, 0:P], x3[:, :], ident[:, :]).then_inc(set_pe, 1)
            pe.wait_ge(set_dve, 4)

            for b in range(NB):
                def layer(which):
                    for g in range(CH):
                        for k in range(PER):
                            i = g * PER + k
                            pe.wait_ge(norm_ready, 2 * BLK * b + which * BLK + i + 1)
                            last = pe.transpose(bank[g][:, k * P:(k + 1) * P], xn[:, i, :], ident[:, :])
                        last.then_inc(norm_turned, 1)

                layer(0)
                pe.wait_ge(h_ready, 2 * CH * b + CH)
                for i in range(BLK):
                    last = mm(bank[4][:, 2 * i:2 * i + 2], hT[:, i * P:(i + 1) * P], tqT[:, :], start=True, stop=True)
                last.then_inc(pos_ready, 1)
                for n in range(2 * CH):
                    g = n % CH
                    if n >= CH:
                        pe.wait_ge(q_ready, 2 * CH * b + g + 1)
                    mm(bank[g][:, :], wT[:, n // CH, :], hT[:, g * W:(g + 1) * W], start=True, stop=True)\
                        .then_inc(q_made, 1)
                    if n == 1:
                        pe.wait_ge(part_ready, 2 * b + 1)
                        mm(bank[5][:, 0:2], ones[:, :], part[:, :], start=True, stop=True).then_inc(part_summed, 1)
                    if n == 4:
                        pe.wait_ge(part_ready, 2 * b + 2)
                        mm(bank[5][:, 8:13], ones[:, :], mpart[:, :], start=True, stop=True).then_inc(part_summed, 1)
                pe.wait_ge(unit_ready, b + 1)
                pe.wait_ge(feat_ready, b + 1)
                for g in range(CH):
                    for k in range(PER):
                        i = g * PER + k
                        last = pe.transpose(bank[4 + g][0:3, k * P:(k + 1) * P], rea[:, i, :], ident[:, :])
                    last.then_inc(unit_turned, 1)
                for n in range(4):
                    src = (fl, fr)[n // 2]
                    pe.wait_ge(unit_copied, CH * b + n + 1)
                    for k in range(8):
                        i = (n % 2) * 8 + k
                        last = pe.transpose(bank[4 + n][0:FEAT, :].bitcast(BF16)[:, k * P:(k + 1) * P],
                                            src[:, i, :], identb[:, :])
                    last.then_inc(feat_turned, 1)
                for i in range(BLK):
                    if i < 2:
                        pe.wait_ge(feat_copied, 4 * b + i + 3)
                    else:
                        pe.wait_ge(v_ready, BLK * b + i - 1)
                    h = hT[:, i * P:(i + 1) * P]
                    mm(bank[4 + i % 2][:, 0:P], h, vh[:, b, 0, :], start=True, stop=True).then_inc(v_made, 1)
                    if i >= 2:
                        pe.wait_ge(base_ready, BLK * b + i - 1)
                    o = bank[6 + i % 2][:, 0:P]
                    mm(o, h, vh[:, b, 1, :], start=True, stop=False)
                    mm(o, reT[:, i * P:(i + 1) * P], qw[:, b, :], start=False, stop=True).then_inc(base_made, 1)
                for n in range(2 * CH):
                    g = n % CH
                    if n < CH:
                        pe.wait_ge(q_ready, 2 * CH * b + CH + g + 1)
                    else:
                        pe.wait_ge(spread_ready, 2 * CH * b + g + 1)
                    mm(bank[g][:, :], (selx, sely)[n // CH][:, :], frT[:, g * W:(g + 1) * W], start=True, stop=True)\
                        .then_inc(spread_made, 1)
                pe.wait_ge(spread_ready, 2 * CH * (b + 1))
                pe.wait_ge(v_ready, BLK * (b + 1))
                pe.wait_ge(base_ready, BLK * (b + 1))

                def scores(i):
                    for c in range(CHUNKS_ROW[i]):
                        n = CHUNKS_BEFORE[i] + c
                        w = min(W, (i + 1) * P - c * W)
                        if n >= 2:
                            pe.wait_ge(dist_used, CHUNKS_BEFORE[BLK] * b + n - 1)
                        d = bank[2 + n % 2]
                        diag = c == CHUNKS_ROW[i] - 1
                        last = mm(d[:, 0:w], flT[:, i * P:(i + 1) * P], frT[:, c * W:c * W + w],
                                  start=True, stop=not diag)
                        if diag:
                            last = mm(d[:, w - P:w], minus[:, :], causal[:, :], start=False, stop=True)
                        last.then_inc(dist_made, 1)
                        if n >= 2:
                            pe.wait_ge(scores_masked, CHUNKS_BEFORE[BLK] * b + n - 1)
                        mm(bank[n % 2][:, 0:w], qT[:, i * P:(i + 1) * P], kT[:, c * W:c * W + w],
                           start=True, stop=True).then_inc(scores_made, 1)

                def values(i):
                    def product(g):
                        n = CHUNKS_BEFORE[i] + g
                        pe.wait_ge(turned_copied, CHUNKS_BEFORE[BLK] * b + n + 1)
                        if g == 0 and i >= 2:
                            pe.wait_ge(row_ready, BLK * b + i - 1)
                        for k in range(min(PER, i + 1 - g * PER)):
                            j = g * PER + k
                            last = mm(bank[6 + i % 2][:, 0:P], ptr[:, n % 2, k * P:(k + 1) * P], v[:, j, :],
                                      start=(j == 0), stop=(j == i))
                        last.then_inc(turned_used, 1)
                        if g == CHUNKS_ROW[i] - 1:
                            pe.wait_ge(turned_used, CHUNKS_BEFORE[BLK] * b + n + 1)
                            pe.sem_inc(row_made, 1)

                    pe.wait_ge(probs_ready, BLK * b + i + 1)
                    for g in range(CHUNKS_ROW[i]):
                        n = CHUNKS_BEFORE[i] + g
                        if n >= 2:
                            pe.wait_ge(turned_copied, CHUNKS_BEFORE[BLK] * b + n - 1)
                        for k in range(min(PER, i + 1 - g * PER)):
                            j = g * PER + k
                            last = pe.transpose(bank[4 + n % 2][:, k * P:(k + 1) * P],
                                                pr[:, i % 2, j * P:(j + 1) * P], ident[:, :])
                        last.then_inc(probs_turned, 1)
                        if g:
                            product(g - 1)
                    product(CHUNKS_ROW[i] - 1)

                for i in range(BLK + 1):
                    if i < BLK:
                        scores(i)
                    if i:
                        values(i - 1)
                layer(1)
                pe.wait_ge(h_ready, 2 * CH * (b + 1))
                for i in range(BLK):
                    last = mm(bank[4][:, i * E:(i + 1) * E], hT[:, i * P:(i + 1) * P], rT[:, :], start=True, stop=True)
                last.then_inc(logits_made, 1)
                pe.wait_ge(comb_ready, b + 1)
                for n in range(2):
                    for k in range(8):
                        last = pe.transpose(bank[5 + n][0:3 * E, :].bitcast(BF16)[:, k * P:(k + 1) * P],
                                            cpart[:, n * 8 + k, :, :], identb[:, :])
                    last.then_inc(comb_turned, 1)
                pe.wait_ge(comb_copied, 2 * (b + 1))
                pe.wait_ge(experts_loaded, 16 * 6)
                with pe.Fori(0, CH) as c:
                    it = b * CH + c
                    hc = hT[:, bass.ds(c * W, W)]

                    def up(e):
                        if e >= 2:
                            pe.wait_ge(silu_ready, EX * it + e - 1)
                        mm(bank[e % 2][:, :], wg[:, e, :], hc, start=True, stop=True).then_inc(gate_made, 1)
                        if e >= 2:
                            pe.wait_ge(act_ready, EX * it + e - 1)
                        last = mm(bank[2 + e % 2][:, :], wu[:, e, :], hc, start=True, stop=True)
                        if e < E:
                            last = mm(bank[4 + e % 2][:, :], selw[:, e, :], combT[:, bass.ds(c * W, W)],
                                      start=True, stop=True)
                        last.then_inc(up_made, 1)

                    def down(e):
                        pe.wait_ge(act_ready, EX * it + e + 1)
                        mm(bank[6][:, :], wd[:, e, :], act_g[:, e % 2, :], start=(e == 0), stop=(e == EX - 1))\
                            .then_inc(down_made, 1)

                    for e in range(EX + 1):
                        if e < EX:
                            up(e)
                        if e:
                            down(e - 1)
                    pe.wait_ge(y_copied, it + 1)
                    for k in range(PER):
                        last = pe.transpose(bank[7][:, k * P:(k + 1) * P], ysb[:, k * P:(k + 1) * P], ident[:, :])
                    last.then_inc(y_turned, 1)

        @block.vector
        def _(dve):
            chain = Chain(dve, dve_step)
            step, settle = chain.step, chain.settle
            dve.wait_ge(consts_ready, 1)
            dve.wait_ge(set_pe, 1)
            step(dve.tensor_copy(sc[:, :], bank[1][:, E + 2:E + 2 + NB]))
            settle()
            for b in range(NB):
                last = dve.tensor_scalar(scb[:, b, :], ones[:, :], sc[:, b:b + 1], None, ALU.mult)
            last.then_inc(set_dve, 1)
            dve.wait_ge(small_loaded, 16 * (SMALL))
            dve.wait_ge(set_pe, 2)
            step(dve.tensor_copy(wT[:, :, :], bank[0][:, 0:3 * P]))
            step(dve.tensor_copy(rT[:, :], bank[1][:, 0:E]))
            step(dve.tensor_copy(tqT[:, :], bank[1][:, E:E + 2]))
            step(dve.tensor_copy(md[:, :, :], bank[2][:, 0:6 * NB]))
            settle()
            step(dve.tensor_scalar(md[:, 1, :], md[:, 1, :], 1.0, None, ALU.add))
            step(dve.tensor_scalar(md[:, 4, :], md[:, 4, :], 1.0, None, ALU.add))
            settle()
            dve.sem_inc(set_dve, 1)
            dve.wait_ge(set_pe, 3)
            step(dve.tensor_scalar(gsgn, bank[3][:, :], 0.0, 2.0, ALU.is_ge, ALU.mult))
            step(dve.tensor_copy(graw, bank[3][:, :]))
            settle()
            step(dve.scalar_tensor_tensor(out=gmag, in0=graw, scalar=-1.0, in1=graw, op0=ALU.mult, op1=ALU.max))
            settle()
            step(dve.tensor_scalar(gmag, gmag, NEAR, None, ALU.max))
            settle()
            step(dve.scalar_tensor_tensor(out=gbc[:, :, :, :].rearrange("p b g d -> p (b g d)"),
                                          in0=gsgn, scalar=-1.0, in1=gmag,
                                          op0=ALU.add, op1=ALU.mult))
            settle()
            dve.wait_ge(set_pe, 4)
            for b in range(NB):
                step(dve.tensor_tensor(vh[:, b, 0, :], bank[4][:, 0:P], gbc[:, b, 0, :], ALU.mult))
                step(dve.tensor_tensor(vh[:, b, 1, :], ident[:, :], gbc[:, b, 0, :], ALU.mult))
            step(dve.tensor_scalar(x3[:, 0:2], wfq[:, :], 0.1, None, ALU.mult))
            step(dve.scalar_tensor_tensor(out=x3[:, 2:3], in0=cols[:, 4:5], scalar=0.1, in1=cols[:, 3:4],
                                          op0=ALU.mult, op1=ALU.add))
            settle()
            step(dve.tensor_tensor(x3[:, 2:3], bank[4][:, P:P + 1], x3[:, 2:3], ALU.add))
            settle()
            dve.sem_inc(set_dve, 1)
            dve.wait_ge(set_pe, 5)
            for b in range(NB):
                step(dve.tensor_tensor(qw[:, b, :], bank[5][0:3, 0:P], gbc[0:3, b, 0, :], ALU.mult))
            settle()
            dve.sem_inc(set_dve, 1)

            def refine(root, square, helper, times):
                step(dve.reciprocal(helper, root)); settle()
                step(dve.tensor_tensor(helper, helper, square, ALU.mult)); settle()
                step(dve.tensor_tensor(helper, helper, root, ALU.add)); settle()

            for b in range(NB):
                def layer(which, block_of):
                    for i in range(BLK):
                        if which:
                            pass
                        step(dve.bn_stats(st[:, i, :], block_of(i)))
                    settle()
                    for i in range(BLK):
                        step(dve.bn_aggr(mv[:, i, :], st[:, i, :]))
                    settle()
                    dve.tensor_scalar(ve[:, :], mv[:, :, 1], EPS, None, ALU.add).then_inc(root_asked, 1)
                    k = 1 if which == 0 else 4
                    dve.wait_ge(root_ready, 4 * b + k)
                    dve.wait_ge(root_asked, 4 * b + k)
                    refine(sd[:, :], ve[:, :], tt[:, :], 1)
                    step(dve.reciprocal(rs[:, :], tt[:, :])); settle()
                    step(dve.tensor_scalar(rs[:, :], rs[:, :], 2.0, None, ALU.mult)); settle()
                    for i in range(BLK):
                        dve.tensor_scalar(xn[:, i, :], block_of(i), mv[:, i, 0:1], rs[:, i:i + 1],
                                          ALU.subtract, ALU.mult).then_inc(norm_ready, 1)

                dve.wait_ge(x_loaded, 16 * (b + 1))
                layer(0, lambda i: x[:, b * BLK + i, :])

                dve.wait_ge(pos_ready, b + 1)
                step(dve.tensor_tensor(qp[:, :, :], bank[4][:, 0:2 * BLK].rearrange("p (i k) -> p i k", k=2),
                                       btq_bc[:, :].unsqueeze(1).broadcast_to([P, BLK, 2]), ALU.add))
                settle()
                step(dve.tensor_tensor(sq[:, :, :], qp[:, :, :], qp[:, :, :], ALU.mult))
                dve.tensor_reduce(part[:, :], qp[:, :, :].rearrange("p i k -> p k i"), X, ALU.add)\
                   .then_inc(part_ready, 1)
                settle()
                step(dve.tensor_tensor(nrm[:, :], sq[:, :, 0], sq[:, :, 1], ALU.add)); settle()
                dve.tensor_scalar(nrm[:, :], nrm[:, :], TINY, None, ALU.max).then_inc(root_asked, 1)
                dve.wait_ge(part_summed, 2 * b + 1)
                step(dve.tensor_scalar(mean[:, :], bank[5][:, 0:2], 1.0 / N, None, ALU.mult)); settle()
                step(dve.tensor_tensor(qc[:, :, :], qp[:, :, :],
                                       mean[:, :].unsqueeze(1).broadcast_to([P, BLK, 2]), ALU.subtract))
                settle()
                step(dve.tensor_tensor(mom[:, 0, :], qc[:, :, 0], qc[:, :, 0], ALU.mult))
                step(dve.tensor_tensor(mom[:, 1, :], qc[:, :, 0], qc[:, :, 1], ALU.mult))
                step(dve.tensor_tensor(mom[:, 2, :], qc[:, :, 1], qc[:, :, 1], ALU.mult))
                settle()
                step(dve.tensor_tensor(mom[:, 3, :], mom[:, 0, :], mom[:, 2, :], ALU.add)); settle()
                step(dve.tensor_tensor(mom[:, 4, :], mom[:, 3, :], mom[:, 3, :], ALU.mult)); settle()
                dve.tensor_reduce(mpart[:, :], mom[:, :, :], X, ALU.add).then_inc(part_ready, 1)
                dve.wait_ge(root_ready, 4 * b + 2)
                refine(sd[:, :], nrm[:, :], tt[:, :], 1)
                step(dve.tensor_scalar(tt[:, :], tt[:, :], 0.5, 1e-12, ALU.mult, ALU.max)); settle()
                step(dve.reciprocal(rs[:, :], tt[:, :])); settle()
                dve.tensor_tensor(rea[:, :, 0:2], qp[:, :, :], rs[:, :].unsqueeze(2).broadcast_to([P, BLK, 2]),
                                  ALU.mult).then_inc(unit_ready, 1)
                dve.wait_ge(part_summed, 2 * b + 2)
                step(dve.tensor_copy(msum[:, :], bank[5][:, 8:13])); settle()
                step(dve.tensor_tensor(m2[:, 0:4], msum[:, 0:4], msum[:, 0:4], ALU.mult))
                step(dve.tensor_copy(m2[:, 4:5], msum[:, 4:5])); settle()
                step(dve.tensor_tensor(m2[:, :], m2[:, :], vw[:, :], ALU.mult)); settle()
                step(dve.tensor_reduce(var[:, :], m2[:, :], X, ALU.add)); settle()
                dve.tensor_scalar(var[:, :], var[:, :], TINY, None, ALU.max).then_inc(root_asked, 1)
                step(dve.tensor_copy(quant[:, :, 0:2], qc[:, :, :]))
                step(dve.tensor_scalar(quant[:, :, 2], qc[:, :, 1], 1.0 / WEDGE, None, ALU.mult))
                step(dve.tensor_scalar(quant[:, :, 3], mom[:, 3, :], -1.0, None, ALU.mult))
                settle()
                step(dve.tensor_scalar(xi[:, :], quant[:, :, 0], HUGE, None, ALU.mult))
                step(dve.tensor_scalar(nyi[:, :], quant[:, :, 2], -HUGE, None, ALU.mult))
                dve.wait_ge(root_ready, 4 * b + 3)
                refine(sdv[:, :], var[:, :], tv[:, :], 1)
                step(dve.tensor_scalar(tv[:, :], tv[:, :], 0.5 * 1.25, None, ALU.mult)); settle()
                step(dve.scalar_tensor_tensor(out=thr[:, :], in0=msum[:, 3:4], scalar=2.0 / N, in1=tv[:, :],
                                              op0=ALU.mult, op1=ALU.add))
                settle()
                step(dve.tensor_scalar(quant[:, :, 4], quant[:, :, 3], thr[:, 0:1], None, ALU.add)); settle()
                step(dve.tensor_copy(parts[:, 0, :, :], quant[:, :, :])); settle()
                step(dve.tensor_tensor(rest[:, :, :], quant[:, :, :], parts[:, 0, :, :], ALU.subtract)); settle()
                step(dve.tensor_copy(parts[:, 1, :, :], rest[:, :, :])); settle()
                step(dve.tensor_tensor(rest[:, :, :], rest[:, :, :], parts[:, 1, :, :], ALU.subtract)); settle()
                step(dve.tensor_copy(parts[:, 2, :, :], rest[:, :, :])); settle()

                def by_part(k):
                    return parts[:, :, :, k].rearrange("p s i -> p i s")

                for k in range(2):
                    o = 9 * k
                    step(dve.tensor_scalar(fl[:, :, o:o + 9].rearrange("p i (s t) -> p i s t", t=3),
                                           by_part(k).unsqueeze(3).broadcast_to([P, BLK, 3, 3]),
                                           2 * HUGE, None, ALU.mult))
                    step(dve.tensor_copy(fr[:, :, o:o + 9].rearrange("p i (s t) -> p i s t", s=3),
                                         by_part(k).unsqueeze(2).broadcast_to([P, BLK, 3, 3])))
                step(dve.tensor_scalar(fl[:, :, 18:21], by_part(4), HUGE, None, ALU.mult))
                step(dve.tensor_copy(fr[:, :, 21:24], by_part(3)))
                step(dve.tensor_copy(fr[:, :, 24:27], by_part(2)))
                settle()
                dve.sem_inc(feat_ready, 1)
                for g in range(CH):
                    dve.wait_ge(unit_turned, CH * b + g + 1)
                    dve.tensor_copy(reT[:, g * W:(g + 1) * W], bank[4 + g][0:3, :]).then_inc(unit_copied, 1)
                for n in range(4):
                    dve.wait_ge(feat_turned, 4 * b + n + 1)
                    dve.tensor_copy((flT, frT)[n // 2][:, (n % 2) * 8 * P:(n % 2 + 1) * 8 * P],
                                    bank[4 + n][0:FEAT, :].bitcast(BF16)).then_inc(feat_copied, 1)
                for i in range(BLK):
                    dve.wait_ge(base_made, BLK * b + i + 1)
                    dve.tensor_tensor(x1[:, i, :], bank[6 + i % 2][:, 0:P], x[:, b * BLK + i, :],
                                      ALU.add).then_inc(base_ready, 1)
                dve.wait_ge(spread_ready, 2 * CH * (b + 1))

                def finish(i):
                    dve.wait_ge(probs_ready, BLK * b + i + 1)
                    step(dve.reciprocal(rinv[:, i:i + 1], rsum[:, i:i + 1])); settle()
                    dve.wait_ge(row_made, BLK * b + i + 1)
                    dve.scalar_tensor_tensor(out=x1[:, i, :], in0=bank[6 + i % 2][:, 0:P], scalar=rinv[:, i:i + 1],
                                             in1=x1[:, i, :], op0=ALU.mult, op1=ALU.add).then_inc(row_ready, 1)

                for i in range(BLK):
                    L = (i + 1) * P
                    o = off[:, i % 2, :]
                    dve.wait_ge(rise_ready, BLK * b + i + 1)
                    step(dve.scalar_tensor_tensor(out=o[:, 0:L], in0=xb[:, 0:L], scalar=xi[:, i:i + 1],
                                                  in1=o[:, 0:L], op0=ALU.subtract, op1=ALU.subtract, reverse1=True))
                    settle()
                    if i >= 2:
                        dve.wait_ge(probs_ready, BLK * b + i - 1)
                    for c in range(CHUNKS_ROW[i]):
                        n = CHUNKS_BEFORE[i] + c
                        w = min(W, L - c * W)
                        dve.wait_ge(dist_made, CHUNKS_BEFORE[BLK] * b + n + 1)
                        dve.scalar_tensor_tensor(out=pen[:, n % 2, 0:w], in0=bank[2 + n % 2][:, 0:w], scalar=0.0,
                                                 in1=o[:, c * W:c * W + w], op0=ALU.min, op1=ALU.min)\
                           .then_inc(dist_used, 1)
                        dve.wait_ge(dist_used, CHUNKS_BEFORE[BLK] * b + n + 1)
                        dve.wait_ge(scores_made, CHUNKS_BEFORE[BLK] * b + n + 1)
                        dve.tensor_tensor_reduce(sm[:, i % 2, c * W:c * W + w], bank[n % 2][:, 0:w],
                                                 pen[:, n % 2, 0:w], float(P) ** -0.5, -3.0e38, ALU.add, ALU.max,
                                                 mx[:, i, c:c + 1]).then_inc(scores_masked, 1)
                    dve.wait_ge(scores_masked, CHUNKS_BEFORE[BLK] * b + CHUNKS_BEFORE[i + 1])
                    dve.tensor_reduce(nmx[:, i:i + 1], mx[:, i, 0:CHUNKS_ROW[i]], X, ALU.max, negate=True)\
                       .then_inc(max_ready, 1)
                    if i:
                        finish(i - 1)
                finish(BLK - 1)
                dve.wait_ge(row_ready, BLK * (b + 1))
                layer(1, lambda i: x1[:, i, :])

                dve.wait_ge(sig_ready, b + 1)
                step(dve.tensor_tensor(score[:, :, :], sig[:, :, :],
                                       rb_bc[:, :].unsqueeze(1).broadcast_to([P, BLK, E]), ALU.add))
                settle()
                pair = score[:, :, :].rearrange("p i (g a c) -> p (i g) a c", g=GRP, a=2)
                for n, op in enumerate((ALU.max, ALU.min)):
                    step(dve.tensor_tensor(pm[:, :, :, :, n].rearrange("p i g a -> p (i g) a"),
                                           pair[:, :, :, 0], pair[:, :, :, 1], op))
                settle()
                step(dve.tensor_tensor(ps2[:, :, :, 0], pm[:, :, :, 0, 0], pm[:, :, :, 1, 0], ALU.max))
                step(dve.tensor_tensor(ps3[:, :, :, 0], pm[:, :, :, 0, 0], pm[:, :, :, 1, 0], ALU.min))
                step(dve.tensor_tensor(ps3[:, :, :, 1], pm[:, :, :, 0, 1], pm[:, :, :, 1, 1], ALU.max))
                settle()
                step(dve.tensor_tensor(ps2[:, :, :, 1], ps3[:, :, :, 0], ps3[:, :, :, 1], ALU.max)); settle()
                step(dve.tensor_tensor(gs[:, :, :], ps2[:, :, :, 0], ps2[:, :, :, 1], ALU.add)); settle()
                mine = gs[:, :, :].unsqueeze(3).broadcast_to([P, BLK, GRP, GRP])
                other = gs[:, :, :].unsqueeze(2).broadcast_to([P, BLK, GRP, GRP])
                step(dve.tensor_tensor(gcmp[:, :, :, :], other, mine, ALU.is_gt))
                step(dve.tensor_tensor(geq[:, :, :, :], other, mine, ALU.is_equal))
                settle()
                step(dve.tensor_tensor(geq[:, :, :, :].rearrange("p i g o -> p i (g o)"),
                                       geq[:, :, :, :].rearrange("p i g o -> p i (g o)"),
                                       tri[:, :, :].rearrange("p g o -> p (g o)").unsqueeze(1)
                                       .broadcast_to([P, BLK, GRP * GRP]), ALU.mult))
                settle()
                step(dve.tensor_tensor(gcmp[:, :, :, :], gcmp[:, :, :, :], geq[:, :, :, :], ALU.add)); settle()
                step(dve.tensor_reduce(grank[:, :, :], gcmp[:, :, :, :], X, ALU.add)); settle()
                step(dve.tensor_scalar(gsel[:, :, :], grank[:, :, :], 2.0, None, ALU.is_lt)); settle()
                chosen = gsel[:, :, :].unsqueeze(3).broadcast_to([P, BLK, GRP, EPG])
                wide = lambda t: t[:, :, :].rearrange("p i (g m) -> p i g m", g=GRP)
                step(dve.tensor_tensor(wide(score), wide(score), chosen, ALU.mult)); settle()
                step(dve.tensor_tensor(wide(score), wide(score), chosen, ALU.add)); settle()
                step(dve.tensor_scalar(score[:, :, :], score[:, :, :], -1.0, None, ALU.add)); settle()
                for i in range(BLK):
                    step(dve.max(best[:, i, :], score[:, i, :]))
                settle()
                for i in range(BLK):
                    step(dve.max_index(bidx[:, i, :], best[:, i, :], score[:, i, :]))
                settle()
                step(dve.tensor_copy(bf[:, :, :], bidx[:, :, :])); settle()
                every = iota[:, :].unsqueeze(1).broadcast_to([P, BLK, E])
                for k in range(TOP):
                    step(dve.tensor_tensor((hit if k else hits)[:, :, :], every,
                                           bf[:, :, k:k + 1].broadcast_to([P, BLK, E]), ALU.is_equal))
                    settle()
                    if k:
                        step(dve.tensor_tensor(hits[:, :, :], hits[:, :, :], hit[:, :, :], ALU.add)); settle()
                step(dve.tensor_tensor(comb[:, :, :], hits[:, :, :], sig[:, :, :], ALU.mult)); settle()
                step(dve.tensor_reduce(wsum[:, :], comb[:, :, :], X, ALU.add)); settle()
                step(dve.tensor_scalar(wsum[:, :], wsum[:, :], 1e-20, None, ALU.add)); settle()
                step(dve.reciprocal(wsum[:, :], wsum[:, :])); settle()
                step(dve.tensor_scalar(wsum[:, :], wsum[:, :], SCALE, None, ALU.mult)); settle()
                step(dve.tensor_tensor(comb[:, :, :], comb[:, :, :],
                                       wsum[:, :].unsqueeze(2).broadcast_to([P, BLK, E]), ALU.mult))
                settle()
                step(dve.tensor_copy(cpart[:, :, 0, :], comb[:, :, :])); settle()
                step(dve.tensor_tensor(crest[:, :, :], comb[:, :, :], cpart[:, :, 0, :], ALU.subtract)); settle()
                step(dve.tensor_copy(cpart[:, :, 1, :], crest[:, :, :])); settle()
                step(dve.tensor_tensor(crest[:, :, :], crest[:, :, :], cpart[:, :, 1, :], ALU.subtract)); settle()
                dve.tensor_copy(cpart[:, :, 2, :], crest[:, :, :]).then_inc(comb_ready, 1)
                for n in range(2):
                    dve.wait_ge(comb_turned, 2 * b + n + 1)
                    dve.tensor_copy(combT[:, n * 8 * P:(n + 1) * 8 * P],
                                    bank[5 + n][0:3 * E, :].bitcast(BF16)).then_inc(comb_copied, 1)

                with dve.Fori(0, CH) as c:
                    it = b * CH + c
                    for e in range(EX):
                        dve.wait_ge(silu_ready, EX * it + e + 1)
                        dve.wait_ge(up_made, EX * it + e + 1)
                        if e >= 2:
                            dve.wait_ge(down_made, EX * it + e - 1)
                        src = sg[:, e % 2, :]
                        if e < E:
                            dve.tensor_tensor(sw[:, e % 2, :], bank[4 + e % 2][:, :], sg[:, e % 2, :], ALU.mult)\
                               .then_inc(silu_weighted, 1)
                            dve.wait_ge(silu_weighted, E * it + e + 1)
                            src = sw[:, e % 2, :]
                        dve.tensor_tensor(act_g[:, e % 2, :], bank[2 + e % 2][:, :], src, ALU.mult)\
                           .then_inc(act_ready, 1)
                    dve.wait_ge(y_turned, it + 1)
                    o = x[:, bass.ds(it * PER, PER), :]
                    dve.tensor_tensor(o, bank[7][:, :].rearrange("p (k d) -> p k d", d=P),
                                      gbc[:, b, 1:2, :].broadcast_to([P, PER, P]), ALU.mult)\
                       .then_inc(out_scaled, 1)
                    dve.wait_ge(out_scaled, it + 1)
                    dve.tensor_tensor(o, o, x1[:, bass.ds(c * PER, PER), :], ALU.add).then_inc(out_ready, 1)


_INS = ["L0_attn_hidden_states", "L0_attn_Wq", "L0_attn_bq", "L0_attn_Wk", "L0_attn_bk", "L0_attn_Wv",
        "L0_attn_bv", "L0_attn_Wo", "L0_attn_bo", "L0_attn_Wtq", "L0_attn_btq", "L0_attn_Wfq", "L0_attn_bfq",
        "L0_ffn_router_w", "L0_ffn_bias", "L0_ffn_gate_w", "L0_ffn_up_w", "L0_ffn_down_w", "L0_ffn_sh_gate_w",
        "L0_ffn_sh_up_w", "L0_ffn_sh_down_w", "L0_c", "L0_wmod"]


def kernel(**inputs):
    import concourse.bacc as _bacc
    from concourse.bass_utils import run_bass_kernel_spmd as _run

    nc = _bacc.Bacc("TRN2", target_bir_lowering=False, num_devices=1)
    arrays, args = {}, []
    for name in _INS:
        a = np.ascontiguousarray(inputs[name])
        arrays[f"in_{name}"] = a
        args.append(nc.dram_tensor(f"in_{name}", a.shape, mybir.dt.from_np(a.dtype), kind="ExternalInput").ap())
    args.append(nc.dram_tensor("out_x", (NB, N, P), F32, kind="ExternalOutput").ap())
    build(nc, *args)
    r = _run(nc, [arrays], core_ids=[0])
    return r.results[0]["out_x"]
```

```python
from contextlib import ExitStack

import numpy as np

import concourse.bass as bass
from concourse import mybir

F32 = mybir.dt.float32
BF16 = mybir.dt.bfloat16
F16 = mybir.dt.float16
U32 = mybir.dt.uint32
ALU = mybir.AluOpType
ACT = mybir.ActivationFunctionType
X = mybir.AxisListType.X

P = 128
NB = 2
N = 2048
BLK = N // P
W = 512
CH = N // W
PER = W // P
E = 16
NS = 2
EX = E + NS
GRP = 4
EPG = E // GRP
TOP = 4
SCALE = 2.5
EPS = 1e-5
NEAR = 0.25

WEDGE = 2.4417243e-4
HUGE = float(2.0 ** 90)
HUGER = float(2.0 ** 110)
FEAT = 27
TINY = 1e-30

QK_UP = 16.0
H_UP = 32.0
W_UP = 64.0
G_UP = 32.0
ROWS = 3
PIECE = EX // 2
STEPS = EX * CH
PIECES = 14
PIECE_EVERY = 2

CHUNKS_ROW = [i // PER + 1 for i in range(BLK)]
CHUNKS_BEFORE = [sum(CHUNKS_ROW[:i]) for i in range(BLK + 1)]
NCH = CHUNKS_BEFORE[BLK]
CHUNKS = [(i, c) for i in range(BLK) for c in range(CHUNKS_ROW[i])]
EXP_AT = {CHUNKS_BEFORE[i + 1]: i for i in range(BLK)}
RISE_AT = {max(CHUNKS_BEFORE[i] - 1, 0): i for i in range(1, BLK)}
TURN_AT = {n + CHUNKS_ROW[i] + 1: n for n, (i, c) in enumerate(CHUNKS)}
PRODUCT_AT = {slot + 1: n for slot, n in TURN_AT.items()}
FINISH_AT = {slot: CHUNKS[n][0] for slot, n in PRODUCT_AT.items() if CHUNKS[n][1] == CHUNKS_ROW[CHUNKS[n][0]] - 1}
SLOTS = max(PRODUCT_AT) + 1
ROOT_AT = {slot: i // PER for slot, i in FINISH_AT.items() if i % PER == PER - 1}
NORM_AT = {slot + 1: g for slot, g in ROOT_AT.items()}
SHIFT_AT = {slot + 2: g for slot, g in ROOT_AT.items()}
SPLIT_AT = {slot + 3: g for slot, g in ROOT_AT.items()}
ROOTS = 3 + CH
LATE = [g for slot, g in ROOT_AT.items() if slot + 3 >= SLOTS]


class Chain:

    def __init__(self, engine, semaphore):
        self.engine, self.semaphore, self.n = engine, semaphore, 0

    def step(self, instruction):
        instruction.then_inc(self.semaphore, 1)
        self.n += 1

    def settle(self):
        self.engine.wait_ge(self.semaphore, self.n)


def build(nc, hs, Wq, bq, Wk, bk, Wv, bv, Wo, bo, Wtq, btq, Wfq, bfq, router_w, router_b,
          gate_w, up_w, down_w, sh_gate_w, sh_up_w, sh_down_w, cvec, wmod, out):
    ctx = ExitStack()
    with ctx:
        def sb(name, shape, dt=F32):
            return ctx.enter_context(nc.sbuf_tensor(name, shape, dt))

        def sem(name):
            return ctx.enter_context(nc.semaphore(name))

        bank = [ctx.enter_context(nc.psum_tensor(f"bank{i}", [P, W], F32)) for i in range(8)]

        wq = sb("wq", [P, P]); wk = sb("wk", [P, P]); wv = sb("wv", [P, P]); wo = sb("wo", [P, P])
        wT = sb("wT", [P, 3, P])
        rw = sb("rw", [E, P]); rT = sb("rT", [P, E]); colu = sb("colu", [P, 2])
        wtq = sb("wtq", [2, P]); tqT = sb("tqT", [P, 2])
        wfq = sb("wfq", [P, 2])
        cols = sb("cols", [P, 5])
        btq_bc = sb("btq_bc", [P, 2])
        rb_bc = sb("rb_bc", [P, E])
        c2 = sb("c2", [NB, P]); sc2 = sb("sc2", [NB, P]); sc = sb("sc", [P, NB]); scb = sb("scb", [P, NB, P])
        wm = sb("wm", [P, 6 * P])
        md = sb("md", [P, 6, NB])
        gbc = sb("gbc", [P, NB, 2, P])
        vh = sb("vh", [P, NB, 2, P])
        x3 = sb("x3", [P, 3]); qw = sb("qw", [3, NB, P])
        stage = sb("stage", [P, 2, PIECE, P])
        wg = sb("wg", [P, 2, EX, P], F16); wu = sb("wu", [P, 2, EX, P], F16); wd = sb("wd", [P, 2, EX, P], F16)
        ident = sb("ident", [P, P]); identb = sb("identb", [P, P], BF16)
        minus = sb("minus", [P, P], BF16)
        causal = sb("causal", [P, P], BF16)
        ones = sb("ones", [P, P])
        selw = sb("selw", [3 * E, E, P], BF16)
        selx = sb("selx", [FEAT, P], BF16); sely = sb("sely", [FEAT, P], BF16)
        vw = sb("vw", [P, 5])

        x = sb("x", [P, NB * BLK, P])
        hT = sb("hT", [P, N])
        qT = sb("qT", [P, 2, N], F16); kT = sb("kT", [P, 2, N], F16)
        h2 = sb("h2", [P, 2, N], F16)
        v = sb("v", [P, BLK, P])
        xb = sb("xb", [P, N]); yb = sb("yb", [P, N])
        pen = sb("pen", [P, 2, W], BF16)
        row = sb("row", [P, ROWS, N])
        gsgn, gmag, graw = (row[:, 0, k * W:(k + 1) * W] for k in range(3))
        reT = row[0:3, 2, :]
        xn = sb("xn", [P, 2 * PER, P])
        ptr = sb("ptr", [P, 2, W])
        st = sb("st", [P, BLK, 6]); mv = sb("mv", [P, BLK, 2])
        ve = sb("ve", [P, BLK]); rs = sb("rs", [P, BLK]); runit = sb("runit", [P, BLK])
        minus_half = sb("minus_half", [P, BLK]); half = sb("half", [P, 1])
        qp = sb("qp", [P, BLK, 2]); qc = sb("qc", [P, BLK, 2]); sq = sb("sq", [P, BLK, 2])
        nrm = sb("nrm", [P, BLK]); rea = sb("rea", [P, BLK, 3])
        part = sb("part", [P, 2]); mean = sb("mean", [P, 2])
        mom = sb("mom", [P, 5, BLK]); mpart = sb("mpart", [P, 5]); msum = sb("msum", [P, 5])
        m2 = sb("m2", [P, 5]); var = sb("var", [P, 1]); sdv = sb("sdv", [P, 1])
        thr = sb("thr", [P, 1])
        quant = sb("quant", [P, BLK, 5])
        rest = sb("rest", [P, BLK, 5])
        parts = sb("parts", [P, 3, BLK, 5], BF16)
        fl = sb("fl", [P, BLK, FEAT], BF16); fr = sb("fr", [P, BLK, FEAT], BF16)
        flT = sb("flT", [FEAT, N], BF16); frT = sb("frT", [FEAT, N], BF16)
        xi = sb("xi", [P, BLK]); nyi = sb("nyi", [P, BLK])
        mx = sb("mx", [P, BLK, CH]); nmx = sb("nmx", [P, BLK])
        rsum = sb("rsum", [P, BLK]); rinv = sb("rinv", [P, BLK])
        sig = sb("sig", [P, BLK, E]); score = sb("score", [P, BLK, E])
        pm = sb("pm", [P, BLK, GRP, 2, 2]); ps2 = sb("ps2", [P, BLK, GRP, 2]); ps3 = sb("ps3", [P, BLK, GRP, 2])
        gs = sb("gs", [P, BLK, GRP])
        gcmp, geq = (row[:, 0, k * BLK * E:(k + 1) * BLK * E].rearrange("p (i g o) -> p i g o", i=BLK, g=GRP)
                     for k in range(2))
        hit, hits, crest = (row[:, 0, k * BLK * E:(k + 1) * BLK * E].rearrange("p (i e) -> p i e", i=BLK)
                            for k in range(2, 5))
        tri = sb("tri", [P, GRP, GRP])
        grank = sb("grank", [P, BLK, GRP]); gsel = sb("gsel", [P, BLK, GRP])
        best = sb("best", [P, BLK, 8]); bidx = sb("bidx", [P, BLK, 8], U32); bf = sb("bf", [P, BLK, 8])
        iota = sb("iota", [P, E]); iotai = sb("iotai", [P, E], mybir.dt.int32)
        wsum = sb("wsum", [P, BLK]); comb = sb("comb", [P, BLK, E])
        cpart = sb("cpart", [P, BLK, 3, E], BF16); combT = sb("combT", [3 * E, N], BF16)
        sg = stage[:, 0, 0:2 * PER, :].rearrange("p (n k) d -> p n (k d)", n=2)
        act_g = stage[:, 1, 0:2 * PER, :].rearrange("p (n k) d -> p n (k d)", n=2)
        sw = sb("sw", [P, 2, W]); hid = sb("hid", [P, 2, W])
        gp = sb("gp", [P, 3, 2, W], F16)
        ysb = sb("ysb", [P, W]); scaled = sb("scaled", [P, PER, P])

        small_loaded = sem("small_loaded"); x_loaded = sem("x_loaded")
        consts_ready = sem("consts_ready"); pool_step = sem("pool_step")
        set_pe = sem("set_pe")
        set_act = sem("set_act")
        set_dve = sem("set_dve")
        dve_step = sem("dve_step")
        root_asked = sem("root_asked"); root_ready = sem("root_ready")
        stage_loaded = [sem(f"stage_loaded{n}") for n in range(2)]; stage_used = sem("stage_used")
        experts_ready = sem("experts_ready")
        high_ready = sem("high_ready")
        mix_high = sem("mix_high"); mix_split = sem("mix_split")
        act_high = sem("act_high"); act_split = sem("act_split")
        norm_ready = sem("norm_ready"); norm_turned = sem("norm_turned"); h_ready = sem("h_ready")
        pos_ready = sem("pos_ready")
        part_ready = sem("part_ready"); part_summed = sem("part_summed")
        q_made = sem("q_made"); q_ready = sem("q_ready")
        unit_ready = sem("unit_ready"); unit_turned = sem("unit_turned"); unit_copied = sem("unit_copied")
        feat_ready = sem("feat_ready"); feat_turned = sem("feat_turned"); feat_copied = sem("feat_copied")
        v_made = sem("v_made"); base_made = sem("base_made"); v_ready = sem("v_ready"); base_ready = sem("base_ready")
        spread_made = sem("spread_made"); spread_ready = sem("spread_ready")
        dist_made = sem("dist_made"); dist_used = sem("dist_used")
        scores_made = sem("scores_made"); scores_masked = sem("scores_masked")
        rise_ready = sem("rise_ready")
        max_ready = sem("max_ready"); probs_ready = sem("probs_ready")
        probs_turned = sem("probs_turned"); turned_copied = sem("turned_copied")
        turned_used = sem("turned_used"); row_made = sem("row_made"); row_ready = sem("row_ready")
        logits_made = sem("logits_made"); sig_ready = sem("sig_ready")
        comb_ready = sem("comb_ready"); comb_turned = sem("comb_turned"); comb_copied = sem("comb_copied")
        hidden_ready = sem("hidden_ready"); gate_made = sem("gate_made"); up_made = sem("up_made"); silu_ready = sem("silu_ready")
        silu_weighted = sem("silu_weighted"); act_ready = sem("act_ready"); down_made = sem("down_made"); weight_made = sem("weight_made")
        y_copied = sem("y_copied"); y_turned = sem("y_turned"); out_scaled = sem("out_scaled")
        out_ready = sem("out_ready"); stored = sem("stored")

        block = ctx.enter_context(nc.Block())
        SMALL = 16

        def batch_view(t):
            return t.rearrange("b (n p) d -> p (b n) d", p=P)

        def run(inputs, attention, route, step):
            for k in range(PIECES):
                inputs(0, k)
            for n in range(SLOTS):
                attention(0, n)
            for b in range(NB):
                route(b)
                for t in range(STEPS + 3):
                    step(b, t)
                    if b + 1 < NB:
                        k, n = divmod(t, PIECE_EVERY)[0], t - PIECE_EVERY * PIECES
                        if n < 0 and t % PIECE_EVERY == 0:
                            inputs(b + 1, k)
                        if 0 <= n < SLOTS:
                            attention(b + 1, n)

        def ring(b, which, n):
            first, second = ((0, 3), (1, 4), (2, 5), (7, 6))[which]
            return bank[second if b == 0 and n % 2 else first]

        def behind(b):
            return 2 if b == 0 else 1

        def smooth(b):
            return b + 1 < NB

        def ends_chunk(t, lag):
            return t >= lag and (t - lag) % EX == EX - 1

        @block.sync
        def _(sp):
            sp.dma_start(x[:, 0:BLK, :], batch_view(hs)[:, 0:BLK, :]).then_inc(x_loaded, 16)
            sp.dma_start(c2[:, :], cvec).then_inc(small_loaded, 16)
            sp.dma_start(wm[:, :], wmod).then_inc(small_loaded, 16)
            for dst, src in ((wq, Wq), (wk, Wk), (wv, Wv), (wo, Wo), (rw, router_w), (wtq, Wtq), (wfq, Wfq)):
                sp.dma_start(dst[:, :], src).then_inc(small_loaded, 16)
            for n, src in enumerate((bq, bk, bv, bo, bfq)):
                sp.dma_start(cols[:, n:n + 1], src.rearrange("(d o) -> d o", o=1)).then_inc(small_loaded, 16)
            sp.dma_start(btq_bc[:, :], btq.rearrange("(o d) -> o d", o=1).broadcast_to([P, 2])).then_inc(small_loaded, 16)
            sp.dma_start(rb_bc[:, :], router_b.rearrange("(o d) -> o d", o=1).broadcast_to([P, E])).then_inc(small_loaded, 16)
            sp.wait_ge(x_loaded, 16)
            sp.dma_start(x[:, BLK:, :], batch_view(hs)[:, BLK:NB * BLK, :]).then_inc(x_loaded, 16)
            for n in range(6):
                routed, shared = ((gate_w.rearrange("e d f -> d e f"), sh_gate_w.rearrange("d (s f) -> d s f", s=NS)),
                                  (up_w.rearrange("e d f -> d e f"), sh_up_w.rearrange("d (s f) -> d s f", s=NS)),
                                  (down_w.rearrange("e f d -> f e d"),
                                   sh_down_w.rearrange("(s f) d -> f s d", s=NS)))[n // 2]
                if n >= 2:
                    sp.wait_ge(stage_used, n - 1)
                dst = stage[:, n % 2, :, :]
                if n % 2 == 0:
                    sp.dma_start(dst, routed[:, 0:PIECE, :]).then_inc(stage_loaded[0], 16)
                else:
                    sp.dma_start(dst[:, 0:E - PIECE, :], routed[:, PIECE:E, :]).then_inc(stage_loaded[1], 16)
                    sp.dma_start(dst[:, E - PIECE:PIECE, :], shared).then_inc(stage_loaded[1], 16)
            with sp.Fori(0, NB * CH) as it:
                sp.wait_ge(out_ready, it + 1)
                sp.dma_start(batch_view(out)[:, bass.ds(it * PER, PER), :],
                             x[:, bass.ds(it * PER, PER), :]).then_inc(stored, 16)
            sp.wait_ge(stored, 16 * NB * CH)

        @block.gpsimd
        def _(pool):
            chain = Chain(pool, pool_step)
            chain.step(pool.memset(ident[:, :], 0.0))
            chain.step(pool.memset(ones[:, :], 1.0))
            chain.step(pool.memset(causal[:, :], 0.0))
            chain.step(pool.memset(selw[:, :, :], 0.0))
            chain.step(pool.memset(selx[:, :], 0.0))
            chain.step(pool.memset(sely[:, :], HUGE))
            chain.step(pool.memset(tri[:, :, :], 0.0))
            chain.step(pool.memset(fl[:, :, :], 0.0))
            chain.step(pool.memset(minus_half[:, :], -0.5))
            chain.step(pool.memset(half[:, :], 0.5))
            chain.step(pool.memset(fr[:, :, :], 0.0))
            chain.step(pool.memset(rea[:, :, :], 1.0))
            chain.step(pool.memset(minus[:, :], 0.0))
            chain.step(pool.memset(identb[:, :], 0.0))
            chain.step(pool.iota(iotai[:, :], pattern=[[1, E]], base=0, channel_multiplier=0))
            w_den = float(N) * N - 1
            for n, wgt in enumerate((4.0, 8.0, 4.0, -2.0, 2.0 * N)):
                chain.step(pool.memset(vw[:, n:n + 1], wgt / w_den))
            chain.settle()
            chain.step(pool.affine_select(out=ident[:, :], in_=ident[:, :], compare_op=ALU.not_equal, fill=1.0,
                                          base=0, pattern=[[-1, P]], channel_multiplier=1))
            chain.step(pool.affine_select(out=identb[:, :], in_=identb[:, :], compare_op=ALU.not_equal, fill=1.0,
                                          base=0, pattern=[[-1, P]], channel_multiplier=1))
            chain.step(pool.affine_select(out=minus[:, :], in_=minus[:, :], compare_op=ALU.not_equal, fill=-HUGER,
                                          base=0, pattern=[[-1, P]], channel_multiplier=1))
            chain.step(pool.affine_select(out=causal[:, :], in_=causal[:, :], compare_op=ALU.is_ge, fill=1.0,
                                          base=0, pattern=[[-1, P]], channel_multiplier=1))
            for k in range(3):
                chain.settle()
                chain.step(pool.affine_select(out=selw[:, :, :], in_=selw[:, :, :], compare_op=ALU.not_equal,
                                              fill=G_UP / (H_UP * W_UP) ** 2 / 2, base=-E * k, pattern=[[-1, E], [0, P]],
                                              channel_multiplier=1))
            chain.step(pool.affine_select(out=tri[:, :, :], in_=tri[:, :, :], compare_op=ALU.is_ge, fill=1.0,
                                          base=0, pattern=[[-1, GRP], [1, GRP]], channel_multiplier=0))
            chain.step(pool.memset(selx[0:3, :], HUGE))
            chain.step(pool.affine_select(out=sely[:, :], in_=sely[:, :], compare_op=ALU.is_ge, fill=0.0,
                                          base=-(FEAT - 3), pattern=[[0, P]], channel_multiplier=1))
            chain.step(pool.tensor_copy(iota[:, :], iotai[:, :]))
            chain.step(pool.memset(fr[:, :, 18:21], 1.0))
            chain.step(pool.memset(fl[:, :, 21:24], HUGE))
            chain.settle()
            pool.sem_inc(consts_ready, 1)

            def power(dst, src, exponent, count):
                pool.wait_ge(root_asked, count)
                pool.tensor_tensor(dst, src, exponent, ALU.pow).then_inc(root_ready, 1)

            def split(n):
                pool.wait_ge(stage_loaded[n % 2], (n // 2 + 1) * (16, 32)[n % 2])
                w, dst = stage[:, n % 2, :, :], (wg, wu, wd)[n // 2]
                lot = slice(n % 2 * PIECE, (n % 2 + 1) * PIECE)
                chain.step(pool.tensor_scalar(w, w, W_UP, None, ALU.mult)); chain.settle()
                chain.step(pool.tensor_copy(dst[:, 0, lot, :], w)); chain.settle()
                pool.tensor_tensor(dst[:, 1, lot, :], w, dst[:, 0, lot, :], ALU.subtract).then_inc(stage_used, 1)

            def inputs(b, k):
                if k == 0:
                    power(rs[:, :], ve[:, :], minus_half[:, :], ROOTS * b + 1)
                if k == 5:
                    power(runit[:, :], nrm[:, :], minus_half[:, :], ROOTS * b + 2)
                if k == 7:
                    power(sdv[:, :], var[:, :], half[:, :], ROOTS * b + 3)

            def attention(b, n):
                if n in ROOT_AT and ROOT_AT[n] not in LATE:
                    g = ROOT_AT[n]
                    lot = slice(g * PER, (g + 1) * PER)
                    power(rs[:, lot], ve[:, lot], minus_half[:, lot], ROOTS * b + 4 + g)
                if b == 0 and n % 7 == 0 and n // 7 < 6:
                    split(n // 7)

            def route(b):
                for g in LATE:
                    lot = slice(g * PER, (g + 1) * PER)
                    power(rs[:, lot], ve[:, lot], minus_half[:, lot], ROOTS * b + 4 + g)

            def step(b, t):
                if t < STEPS:
                    s = STEPS * b + t
                    pool.wait_ge(act_high, s + 1)
                    if s >= 3:
                        pool.wait_ge(down_made, s - 2)
                    pool.tensor_tensor(gp[:, s % 3, 1, :], act_g[:, s % 2, :], gp[:, s % 3, 0, :], ALU.subtract)\
                        .then_inc(act_split, 1)

            run(inputs, attention, route, step)

        @block.scalar
        def _(act):
            act.wait_ge(small_loaded, 16 * SMALL)
            act.activation(sc2[:, :], c2[:, :], ACT.Silu).then_inc(set_act, 1)
            act.wait_ge(set_dve, 2)

            def shift(b, which, g):
                act.wait_ge(norm_turned, 2 * CH * b + which * CH + g + 1)
                src = bank[2] if which else bank[g % 2]
                act.activation(hT[:, g * W:(g + 1) * W], src[:, :], ACT.Identity,
                               bias=md[:, 3 * which, b:b + 1], scale=md[:, 3 * which + 1, b:b + 1])\
                   .then_inc(h_ready, 1)

            def mixture_input(b, g):
                shift(b, 1, g)
                act.wait_ge(h_ready, 2 * CH * b + CH + g + 1)
                if b:
                    act.wait_ge(up_made, STEPS * (b - 1) + EX * (g + 1))
                lot = slice(g * W, (g + 1) * W)
                act.mul(h2[:, 0, lot], hT[:, lot], H_UP).then_inc(mix_high, 1)

            def inputs(b, k):
                if 1 <= k <= CH:
                    shift(b, 0, k - 1)
                elif 5 <= k <= 8:
                    for m in (2 * (k - 5), 2 * (k - 5) + 1):
                        act.wait_ge(q_made, 2 * CH * b + m + 1)
                        act.activation((qT, kT)[m // CH][:, 0, m % CH * W:(m % CH + 1) * W], bank[m % 2][:, :],
                                       ACT.Identity, bias=colu[:, m // CH:m // CH + 1]).then_inc(high_ready, 1)
                elif k in (10, 11):
                    for g in (2 * (k - 10), 2 * (k - 10) + 1):
                        act.wait_ge(v_made, CH * b + g + 1)
                        act.copy(v[:, g * PER:(g + 1) * PER, :], bank[g % 2][:, :]).then_inc(v_ready, 1)
                elif k >= 12:
                    for g in range(CH):
                        act.wait_ge(spread_made, 2 * CH * b + (k - 12) * CH + g + 1)
                        act.copy((xb, yb)[k - 12][:, g * W:(g + 1) * W], bank[g % 2][:, :]).then_inc(spread_ready, 1)

            def rise(b, i):
                if i >= ROWS:
                    act.wait_ge(probs_turned, NCH * b + CHUNKS_BEFORE[i - ROWS + 1])
                L = (i + 1) * P
                act.activation(row[:, i % ROWS, 0:L], yb[:, 0:L], ACT.Abs, bias=nyi[:, i:i + 1])\
                   .then_inc(rise_ready, 1)

            def attention(b, n):
                if n == 0:
                    act.wait_ge(spread_ready, 2 * CH * (b + 1))
                    rise(b, 0)
                if n in TURN_AT:
                    m = TURN_AT[n]
                    i, g = CHUNKS[m]
                    w = min(W, (i + 1) * P - g * W)
                    act.wait_ge(probs_turned, NCH * b + m + 1)
                    if m >= 2:
                        act.wait_ge(turned_used, NCH * b + m - 1)
                    act.copy(ptr[:, m % 2, 0:w], ring(b, 2, m)[:, 0:w]).then_inc(turned_copied, 1)
                if n in EXP_AT:
                    i = EXP_AT[n]
                    L = (i + 1) * P
                    act.wait_ge(max_ready, BLK * b + i + 1)
                    act.activation(row[:, i % ROWS, 0:L], row[:, i % ROWS, 0:L], ACT.Exp, bias=nmx[:, i:i + 1],
                                   accum_out=rsum[:, i:i + 1]).then_inc(probs_ready, 1)
                if n in RISE_AT:
                    rise(b, RISE_AT[n])
                if n in SHIFT_AT:
                    mixture_input(b, SHIFT_AT[n])

            def route(b):
                for g in LATE:
                    mixture_input(b, g)
                act.wait_ge(logits_made, b + 1)
                act.activation(sig[:, :, :], bank[0][:, 0:BLK * E], ACT.Tanh, scale=0.5).then_inc(sig_ready, 1)

            def step(b, t):
                s = STEPS * b + t
                if t < STEPS:
                    act.wait_ge(gate_made, s + 1)
                    if s >= 2:
                        act.wait_ge(act_ready, s - 1)
                    func, half_of = (ACT.Tanh, 0.5) if smooth(b) else (ACT.Silu, 1.0)
                    act.activation(sg[:, s % 2, :], bank[3][:, :], func, scale=half_of / (H_UP * W_UP))\
                       .then_inc(silu_ready, 1)
                if 1 <= t <= STEPS:
                    act.wait_ge(act_ready, s)
                    if s >= 4:
                        act.wait_ge(down_made, s - 3)
                    act.copy(gp[:, (s - 1) % 3, 0, :], act_g[:, (s - 1) % 2, :]).then_inc(act_high, 1)
                if ends_chunk(t, 2):
                    f = (s - 2) // EX
                    act.wait_ge(down_made, EX * (f + 1))
                    act.mul(ysb[:, :], bank[6][:, :], 1 / (G_UP * W_UP)).then_inc(y_copied, 1)

            run(inputs, attention, route, step)

        @block.tensor
        def _(pe):
            mm = pe.matmul
            pe.wait_ge(small_loaded, 16 * SMALL)
            pe.wait_ge(consts_ready, 1)
            for n, w in enumerate((wq, wk, wo)):
                pe.transpose(bank[0][:, n * P:(n + 1) * P], w[:, :], ident[:, :])
            pe.transpose(bank[1][:, 0:E], rw[:, :], ident[0:E, 0:E])
            pe.transpose(bank[1][:, E:E + 2], wtq[:, :], ident[0:2, 0:2])
            pe.wait_ge(set_act, 1)
            pe.transpose(bank[1][:, E + 2:E + 2 + NB], sc2[:, :], ident[0:NB, 0:NB]).then_inc(set_pe, 1)
            pe.wait_ge(set_dve, 1)
            for j in range(6):
                last = mm(bank[2][:, NB * j:NB * (j + 1)], wm[:, j * P:(j + 1) * P], sc[:, :], start=True, stop=True)
            last.then_inc(set_pe, 1)
            for b in range(NB):
                for n, j in enumerate((2, 5)):
                    o = (2 * b + n) * P
                    last = mm(bank[3][:, o:o + P], scb[:, b, :], wm[:, j * P:(j + 1) * P], start=True, stop=True)
            last.then_inc(set_pe, 1)
            pe.wait_ge(set_dve, 2)
            mm(bank[4][:, 0:P], wv[:, :], wT[:, 2, :], start=True, stop=True)
            mm(bank[4][:, P:P + 1], wT[:, 2, :], cols[:, 2:3], start=True, stop=True).then_inc(set_pe, 1)
            pe.wait_ge(set_dve, 3)
            pe.transpose(bank[5][0:3, 0:P], x3[:, :], ident[:, :]).then_inc(set_pe, 1)
            pe.wait_ge(set_dve, 4)

            def pair(out_bank, weights, data, start=True, stop=True):
                mm(out_bank, weights[0], data[0], start=start, stop=False)
                mm(out_bank, weights[0], data[1], start=False, stop=False)
                return mm(out_bank, weights[1], data[0], start=False, stop=stop)

            def turn_norm(b, which, g):
                if which == 0 and g >= 2:
                    pe.wait_ge(h_ready, 2 * CH * b + g - 1)
                pe.wait_ge(norm_ready, 2 * BLK * b + which * BLK + (g + 1) * PER)
                dst = bank[2] if which else bank[g % 2]
                for k in range(PER):
                    last = pe.transpose(dst[:, k * P:(k + 1) * P], xn[:, g % 2 * PER + k, :], ident[:, :])
                last.then_inc(norm_turned, 1)

            def inputs(b, k):
                if 1 <= k <= CH:
                    turn_norm(b, 0, k - 1)
                if k == 5:
                    pe.wait_ge(h_ready, 2 * CH * b + CH)
                    for i in range(BLK):
                        last = mm(bank[2][:, 2 * i:2 * i + 2], hT[:, i * P:(i + 1) * P], tqT[:, :],
                                  start=True, stop=True)
                    last.then_inc(pos_ready, 1)
                if k == 6:
                    pe.wait_ge(part_ready, 2 * b + 1)
                    mm(bank[2][:, 0:2], ones[:, :], part[:, :], start=True, stop=True).then_inc(part_summed, 1)
                if k == 7:
                    pe.wait_ge(part_ready, 2 * b + 2)
                    mm(bank[2][:, 0:5], ones[:, :], mpart[:, :], start=True, stop=True).then_inc(part_summed, 1)
                if 5 <= k <= 8:
                    for m in (2 * (k - 5), 2 * (k - 5) + 1):
                        if m >= 2:
                            pe.wait_ge(q_ready, 2 * CH * b + m - 1)
                        mm(bank[m % 2][:, :], wT[:, m // CH, :], hT[:, m % CH * W:(m % CH + 1) * W],
                           start=True, stop=True).then_inc(q_made, 1)
                if k == 9:
                    pe.wait_ge(unit_ready, b + 1)
                    for g in range(CH):
                        if g < 2:
                            pe.wait_ge(q_ready, 2 * CH * b + 2 * CH - 1 + g)
                        else:
                            pe.wait_ge(unit_copied, CH * b + g - 1)
                        for j in range(PER):
                            last = pe.transpose(bank[g % 2][0:3, j * P:(j + 1) * P], rea[:, g * PER + j, :], ident[:, :])
                        last.then_inc(unit_turned, 1)
                    pe.wait_ge(feat_ready, b + 1)
                    for n in range(4):
                        if n < 2:
                            pe.wait_ge(unit_copied, CH * b + 3 + n)
                        else:
                            pe.wait_ge(feat_copied, 4 * b + n - 1)
                        for j in range(8):
                            last = pe.transpose(bank[n % 2][0:FEAT, :].bitcast(BF16)[:, j * P:(j + 1) * P],
                                                (fl, fr)[n // 2][:, (n % 2) * 8 + j, :], identb[:, :])
                        last.then_inc(feat_turned, 1)
                if k in (10, 11):
                    for g in (2 * (k - 10), 2 * (k - 10) + 1):
                        if g < 2:
                            pe.wait_ge(feat_copied, 4 * b + 3 + g)
                        else:
                            pe.wait_ge(v_ready, CH * b + g - 1)
                        blocks = range(g * PER, (g + 1) * PER)
                        for j, i in enumerate(blocks):
                            last = mm(bank[g % 2][:, j * P:(j + 1) * P], hT[:, i * P:(i + 1) * P], vh[:, b, 0, :],
                                      start=True, stop=True)
                        last.then_inc(v_made, 1)
                        if g:
                            pe.wait_ge(base_ready, CH * b + g)
                        for j, i in enumerate(blocks):
                            o = bank[2][:, j * P:(j + 1) * P]
                            mm(o, hT[:, i * P:(i + 1) * P], vh[:, b, 1, :], start=True, stop=False)
                            last = mm(o, reT[:, i * P:(i + 1) * P], qw[:, b, :], start=False, stop=True)
                        last.then_inc(base_made, 1)
                if k >= 12:
                    for g in range(CH):
                        n = (k - 12) * CH + g
                        if n < 2:
                            pe.wait_ge(v_ready, CH * b + 3 + n)
                        else:
                            pe.wait_ge(spread_ready, 2 * CH * b + n - 1)
                        mm(bank[g % 2][:, :], (selx, sely)[k - 12][:, :], frT[:, g * W:(g + 1) * W],
                           start=True, stop=True).then_inc(spread_made, 1)

            def attention(b, n):
                lag = behind(b)
                if n == 0:
                    pe.wait_ge(spread_ready, 2 * CH * (b + 1))
                    pe.wait_ge(base_ready, CH * (b + 1))
                    pe.wait_ge(q_ready, 2 * CH * (b + 1))
                if n < NCH:
                    i, c = CHUNKS[n]
                    w = min(W, (i + 1) * P - c * W)
                    if n >= lag:
                        pe.wait_ge(dist_used, NCH * b + n - lag + 1)
                    d = ring(b, 1, n)
                    diag = c == CHUNKS_ROW[i] - 1
                    last = mm(d[:, 0:w], flT[:, i * P:(i + 1) * P], frT[:, c * W:c * W + w], start=True, stop=not diag)
                    if diag:
                        last = mm(d[:, w - P:w], minus[:, :], causal[:, :], start=False, stop=True)
                    last.then_inc(dist_made, 1)
                    if n >= lag:
                        pe.wait_ge(scores_masked, NCH * b + n - lag + 1)
                    pair(ring(b, 0, n)[:, 0:w], [qT[:, h, i * P:(i + 1) * P] for h in range(2)],
                         [kT[:, h, c * W:c * W + w] for h in range(2)]).then_inc(scores_made, 1)
                if n in TURN_AT:
                    m = TURN_AT[n]
                    i, g = CHUNKS[m]
                    pe.wait_ge(probs_ready, BLK * b + i + 1)
                    if m >= lag:
                        pe.wait_ge(turned_copied, NCH * b + m - lag + 1)
                    norms = sum(at < n for at in SHIFT_AT)
                    if norms:
                        pe.wait_ge(h_ready, 2 * CH * b + CH + norms)
                    for k in range(min(PER, i + 1 - g * PER)):
                        j = g * PER + k
                        last = pe.transpose(ring(b, 2, m)[:, k * P:(k + 1) * P],
                                            row[:, i % ROWS, j * P:(j + 1) * P], ident[:, :])
                    last.then_inc(probs_turned, 1)
                if n in PRODUCT_AT:
                    m = PRODUCT_AT[n]
                    i, g = CHUNKS[m]
                    pe.wait_ge(turned_copied, NCH * b + m + 1)
                    if g == 0 and i >= lag:
                        pe.wait_ge(row_ready, BLK * b + i - lag + 1)
                    for k in range(min(PER, i + 1 - g * PER)):
                        j = g * PER + k
                        last = mm(ring(b, 3, i)[:, 0:P], ptr[:, m % 2, k * P:(k + 1) * P], v[:, j, :],
                                  start=(j == 0), stop=(j == i))
                    last.then_inc(turned_used, 1)
                if n in SHIFT_AT:
                    turned = sum(at <= n for at in TURN_AT)
                    pe.wait_ge(turned_copied, NCH * b + turned)
                    turn_norm(b, 1, SHIFT_AT[n])

            def route(b):
                pe.wait_ge(scores_masked, NCH * (b + 1))
                pe.wait_ge(turned_copied, NCH * (b + 1))
                pe.wait_ge(row_ready, BLK * (b + 1))
                for n, g in enumerate(LATE):
                    if n:
                        pe.wait_ge(h_ready, 2 * CH * b + CH + g)
                    turn_norm(b, 1, g)
                pe.wait_ge(h_ready, 2 * CH * (b + 1))
                for i in range(BLK):
                    last = mm(bank[0][:, i * E:(i + 1) * E], hT[:, i * P:(i + 1) * P], rT[:, :], start=True, stop=True)
                last.then_inc(logits_made, 1)
                pe.wait_ge(comb_ready, b + 1)
                for n in range(2):
                    for k in range(8):
                        last = pe.transpose(bank[1 + n][0:3 * E, :].bitcast(BF16)[:, k * P:(k + 1) * P],
                                            cpart[:, n * 8 + k, :, :], identb[:, :])
                    last.then_inc(comb_turned, 1)
                pe.wait_ge(comb_copied, 2 * (b + 1))
                pe.wait_ge(mix_split, CH * (b + 1))
                pe.wait_ge(stage_used, 6)

            def step(b, t):
                s = STEPS * b + t
                e, c = t % EX, min(t // EX, CH - 1)
                data = [h2[:, h, c * W:(c + 1) * W] for h in range(2)]
                if t < STEPS:
                    if s:
                        if s <= STEPS * (NB - 1):
                            pe.wait_ge(hidden_ready, s)
                        else:
                            pe.wait_ge(silu_ready, s)
                    pair(bank[3][:, :], [wg[:, h, e, :] for h in range(2)], data).then_inc(gate_made, 1)
                    if e < E:
                        if E * (s // EX) + e:
                            pe.wait_ge(silu_weighted, E * (s // EX) + e)
                        mm(bank[5][:, :], selw[:, e, :], combT[:, c * W:(c + 1) * W], start=True, stop=True)\
                            .then_inc(weight_made, 1)
                def up():
                    if s:
                        pe.wait_ge(act_ready, s)
                    pair(bank[4][:, :], [wu[:, h, e, :] for h in range(2)], data).then_inc(up_made, 1)

                if ends_chunk(t, 3):
                    f = (s - 3) // EX
                    pe.wait_ge(y_copied, f + 1)
                    for k in range(PER):
                        last = pe.transpose(bank[6][:, k * P:(k + 1) * P], ysb[:, k * P:(k + 1) * P], ident[:, :])
                    last.then_inc(y_turned, 1)
                    if t < STEPS:
                        up()
                if 2 <= t < STEPS + 2:
                    d = s - 2
                    pe.wait_ge(act_split, d + 1)
                    if d % EX == 0 and d:
                        pe.wait_ge(out_scaled, d // EX)
                    pair(bank[6][:, :], [wd[:, h, d % EX, :] for h in range(2)],
                         [gp[:, d % 3, h, :] for h in range(2)], start=(d % EX == 0), stop=(d % EX == EX - 1))\
                        .then_inc(down_made, 1)
                if t < STEPS and not ends_chunk(t, 3):
                    up()

            run(inputs, attention, route, step)

        @block.vector
        def _(dve):
            chain = Chain(dve, dve_step)
            step, settle = chain.step, chain.settle
            dve.wait_ge(consts_ready, 1)
            dve.wait_ge(set_pe, 1)
            step(dve.tensor_copy(sc[:, :], bank[1][:, E + 2:E + 2 + NB]))
            settle()
            for b in range(NB):
                last = dve.tensor_scalar(scb[:, b, :], ones[:, :], sc[:, b:b + 1], None, ALU.mult)
            last.then_inc(set_dve, 1)
            dve.wait_ge(small_loaded, 16 * (SMALL))
            dve.wait_ge(set_pe, 2)
            step(dve.tensor_scalar(wT[:, 0:2, :], bank[0][:, 0:2 * P], QK_UP, None, ALU.mult))
            step(dve.tensor_scalar(colu[:, :], cols[:, 0:2], QK_UP, None, ALU.mult))
            step(dve.tensor_copy(wT[:, 2, :], bank[0][:, 2 * P:3 * P]))
            step(dve.tensor_copy(rT[:, :], bank[1][:, 0:E]))
            step(dve.tensor_copy(tqT[:, :], bank[1][:, E:E + 2]))
            step(dve.tensor_copy(md[:, :, :], bank[2][:, 0:6 * NB]))
            settle()
            step(dve.tensor_scalar(md[:, 1, :], md[:, 1, :], 1.0, None, ALU.add))
            step(dve.tensor_scalar(md[:, 4, :], md[:, 4, :], 1.0, None, ALU.add))
            settle()
            dve.sem_inc(set_dve, 1)
            dve.wait_ge(set_pe, 3)
            step(dve.tensor_scalar(gsgn, bank[3][:, :], 0.0, 2.0, ALU.is_ge, ALU.mult))
            step(dve.tensor_copy(graw, bank[3][:, :]))
            settle()
            step(dve.scalar_tensor_tensor(out=gmag, in0=graw, scalar=-1.0, in1=graw, op0=ALU.mult, op1=ALU.max))
            settle()
            step(dve.tensor_scalar(gmag, gmag, NEAR, None, ALU.max))
            settle()
            step(dve.scalar_tensor_tensor(out=gbc[:, :, :, :].rearrange("p b g d -> p (b g d)"),
                                          in0=gsgn, scalar=-1.0, in1=gmag,
                                          op0=ALU.add, op1=ALU.mult))
            settle()
            dve.wait_ge(set_pe, 4)
            for b in range(NB):
                step(dve.tensor_tensor(vh[:, b, 0, :], bank[4][:, 0:P], gbc[:, b, 0, :], ALU.mult))
                step(dve.tensor_tensor(vh[:, b, 1, :], ident[:, :], gbc[:, b, 0, :], ALU.mult))
            step(dve.tensor_scalar(x3[:, 0:2], wfq[:, :], 0.1, None, ALU.mult))
            step(dve.scalar_tensor_tensor(out=x3[:, 2:3], in0=cols[:, 4:5], scalar=0.1, in1=cols[:, 3:4],
                                          op0=ALU.mult, op1=ALU.add))
            settle()
            step(dve.tensor_tensor(x3[:, 2:3], bank[4][:, P:P + 1], x3[:, 2:3], ALU.add))
            settle()
            dve.sem_inc(set_dve, 1)
            dve.wait_ge(set_pe, 5)
            for b in range(NB):
                step(dve.tensor_tensor(qw[:, b, :], bank[5][0:3, 0:P], gbc[0:3, b, 0, :], ALU.mult))
            settle()
            dve.sem_inc(set_dve, 1)

            def stats(b, i):
                step(dve.bn_stats(st[:, i, :], x[:, b * BLK + i, :])); settle()
                step(dve.bn_aggr(mv[:, i, :], st[:, i, :]))

            def ask_root(lot):
                settle()
                dve.tensor_scalar(ve[:, lot], mv[:, lot, 1], EPS, None, ALU.add).then_inc(root_asked, 1)

            def layer_norm(b, which, g):
                if g >= 2:
                    dve.wait_ge(norm_turned, 2 * CH * b + which * CH + g - 1)
                for k in range(PER):
                    i = g * PER + k
                    dve.tensor_scalar(xn[:, g % 2 * PER + k, :], x[:, b * BLK + i, :], mv[:, i, 0:1], rs[:, i:i + 1],
                                      ALU.subtract, ALU.mult).then_inc(norm_ready, 1)

            def inputs(b, k):
                if k == 0:
                    dve.wait_ge(x_loaded, 16 * (b + 1))
                    for i in range(BLK):
                        step(dve.bn_stats(st[:, i, :], x[:, b * BLK + i, :]))
                    settle()
                    for i in range(BLK):
                        step(dve.bn_aggr(mv[:, i, :], st[:, i, :]))
                    ask_root(slice(0, BLK))
                elif k <= CH:
                    if k == 1:
                        dve.wait_ge(root_ready, ROOTS * b + 1)
                    layer_norm(b, 0, k - 1)
                if k == 5:
                    dve.wait_ge(pos_ready, b + 1)
                    step(dve.tensor_tensor(qp[:, :, :], bank[2][:, 0:2 * BLK].rearrange("p (i k) -> p i k", k=2),
                                           btq_bc[:, :].unsqueeze(1).broadcast_to([P, BLK, 2]), ALU.add))
                    settle()
                    step(dve.tensor_tensor(sq[:, :, :], qp[:, :, :], qp[:, :, :], ALU.mult))
                    dve.tensor_reduce(part[:, :], qp[:, :, :].rearrange("p i k -> p k i"), X, ALU.add)\
                       .then_inc(part_ready, 1)
                    settle()
                    step(dve.tensor_tensor(nrm[:, :], sq[:, :, 0], sq[:, :, 1], ALU.add)); settle()
                    dve.tensor_scalar(nrm[:, :], nrm[:, :], 1e-24, None, ALU.max).then_inc(root_asked, 1)
                if k == 6:
                    dve.wait_ge(part_summed, 2 * b + 1)
                    step(dve.tensor_scalar(mean[:, :], bank[2][:, 0:2], 1.0 / N, None, ALU.mult)); settle()
                    step(dve.tensor_tensor(qc[:, :, :], qp[:, :, :],
                                           mean[:, :].unsqueeze(1).broadcast_to([P, BLK, 2]), ALU.subtract))
                    settle()
                    step(dve.tensor_tensor(mom[:, 0, :], qc[:, :, 0], qc[:, :, 0], ALU.mult))
                    step(dve.tensor_tensor(mom[:, 1, :], qc[:, :, 0], qc[:, :, 1], ALU.mult))
                    step(dve.tensor_tensor(mom[:, 2, :], qc[:, :, 1], qc[:, :, 1], ALU.mult))
                    settle()
                    step(dve.tensor_tensor(mom[:, 3, :], mom[:, 0, :], mom[:, 2, :], ALU.add)); settle()
                    step(dve.tensor_tensor(mom[:, 4, :], mom[:, 3, :], mom[:, 3, :], ALU.mult)); settle()
                    dve.tensor_reduce(mpart[:, :], mom[:, :, :], X, ALU.add).then_inc(part_ready, 1)
                if k == 7:
                    dve.wait_ge(root_ready, ROOTS * b + 2)
                    dve.tensor_tensor(rea[:, :, 0:2], qp[:, :, :], runit[:, :].unsqueeze(2).broadcast_to([P, BLK, 2]),
                                      ALU.mult).then_inc(unit_ready, 1)
                    dve.wait_ge(part_summed, 2 * b + 2)
                    step(dve.tensor_copy(msum[:, :], bank[2][:, 0:5])); settle()
                    step(dve.tensor_tensor(m2[:, 0:4], msum[:, 0:4], msum[:, 0:4], ALU.mult))
                    step(dve.tensor_copy(m2[:, 4:5], msum[:, 4:5])); settle()
                    step(dve.tensor_tensor(m2[:, :], m2[:, :], vw[:, :], ALU.mult)); settle()
                    step(dve.tensor_reduce(var[:, :], m2[:, :], X, ALU.add)); settle()
                    dve.tensor_scalar(var[:, :], var[:, :], TINY, None, ALU.max).then_inc(root_asked, 1)
                    step(dve.tensor_copy(quant[:, :, 0:2], qc[:, :, :]))
                    step(dve.tensor_scalar(quant[:, :, 2], qc[:, :, 1], 1.0 / WEDGE, None, ALU.mult))
                    step(dve.tensor_scalar(quant[:, :, 3], mom[:, 3, :], -1.0, None, ALU.mult))
                    settle()
                    step(dve.tensor_scalar(xi[:, :], quant[:, :, 0], HUGE, None, ALU.mult))
                    step(dve.tensor_scalar(nyi[:, :], quant[:, :, 2], -HUGE, None, ALU.mult))
                if k == 8:
                    dve.wait_ge(root_ready, ROOTS * b + 3)
                    step(dve.tensor_scalar(sdv[:, :], sdv[:, :], 1.25, None, ALU.mult)); settle()
                    step(dve.scalar_tensor_tensor(out=thr[:, :], in0=msum[:, 3:4], scalar=2.0 / N, in1=sdv[:, :],
                                                  op0=ALU.mult, op1=ALU.add))
                    settle()
                    step(dve.tensor_scalar(quant[:, :, 4], quant[:, :, 3], thr[:, 0:1], None, ALU.add)); settle()
                    step(dve.tensor_copy(parts[:, 0, :, :], quant[:, :, :])); settle()
                    step(dve.tensor_tensor(rest[:, :, :], quant[:, :, :], parts[:, 0, :, :], ALU.subtract)); settle()
                    step(dve.tensor_copy(parts[:, 1, :, :], rest[:, :, :])); settle()
                    step(dve.tensor_tensor(rest[:, :, :], rest[:, :, :], parts[:, 1, :, :], ALU.subtract)); settle()
                    step(dve.tensor_copy(parts[:, 2, :, :], rest[:, :, :])); settle()

                    def by_part(a):
                        return parts[:, :, :, a].rearrange("p s i -> p i s")

                    for a in range(2):
                        o = 9 * a
                        step(dve.tensor_scalar(fl[:, :, o:o + 9].rearrange("p i (s t) -> p i s t", t=3),
                                               by_part(a).unsqueeze(3).broadcast_to([P, BLK, 3, 3]),
                                               2 * HUGE, None, ALU.mult))
                        step(dve.tensor_copy(fr[:, :, o:o + 9].rearrange("p i (s t) -> p i s t", s=3),
                                             by_part(a).unsqueeze(2).broadcast_to([P, BLK, 3, 3])))
                    step(dve.tensor_scalar(fl[:, :, 18:21], by_part(4), HUGE, None, ALU.mult))
                    step(dve.tensor_copy(fr[:, :, 21:24], by_part(3)))
                    step(dve.tensor_copy(fr[:, :, 24:27], by_part(2)))
                    settle()
                    dve.sem_inc(feat_ready, 1)
                if 5 <= k <= 8:
                    for m in (2 * (k - 5), 2 * (k - 5) + 1):
                        q, n, lot = (qT, kT)[m // CH], m // CH, slice(m % CH * W, (m % CH + 1) * W)
                        dve.wait_ge(high_ready, 2 * CH * b + m + 1)
                        dve.scalar_tensor_tensor(out=q[:, 1, lot], in0=bank[m % 2][:, :], scalar=colu[:, n:n + 1],
                                                 in1=q[:, 0, lot], op0=ALU.add, op1=ALU.subtract)\
                           .then_inc(q_ready, 1)
                if k == 9:
                    for g in range(CH):
                        dve.wait_ge(unit_turned, CH * b + g + 1)
                        dve.tensor_copy(reT[:, g * W:(g + 1) * W], bank[g % 2][0:3, :]).then_inc(unit_copied, 1)
                    for n in range(4):
                        dve.wait_ge(feat_turned, 4 * b + n + 1)
                        dve.tensor_copy((flT, frT)[n // 2][:, (n % 2) * 8 * P:(n % 2 + 1) * 8 * P],
                                        bank[n % 2][0:FEAT, :].bitcast(BF16)).then_inc(feat_copied, 1)
                if k in (10, 11):
                    for g in (2 * (k - 10), 2 * (k - 10) + 1):
                        dve.wait_ge(base_made, CH * b + g + 1)
                        blocks = x[:, b * BLK + g * PER:b * BLK + (g + 1) * PER, :]
                        dve.tensor_tensor(blocks, bank[2][:, :].rearrange("p (i d) -> p i d", d=P), blocks, ALU.add)\
                           .then_inc(base_ready, 1)

            def split_input(b, g):
                lot = slice(g * W, (g + 1) * W)
                dve.wait_ge(mix_high, CH * b + g + 1)
                dve.scalar_tensor_tensor(out=h2[:, 1, lot], in0=hT[:, lot], scalar=H_UP, in1=h2[:, 0, lot],
                                         op0=ALU.mult, op1=ALU.subtract).then_inc(mix_split, 1)

            def attention(b, n):
                if n == 0:
                    dve.wait_ge(spread_ready, 2 * CH * (b + 1))
                    dve.wait_ge(base_ready, CH * (b + 1))
                if n < NCH:
                    i, c = CHUNKS[n]
                    L = (i + 1) * P
                    o = row[:, i % ROWS, :]
                    if c == 0:
                        dve.wait_ge(rise_ready, BLK * b + i + 1)
                        step(dve.scalar_tensor_tensor(out=o[:, 0:L], in0=xb[:, 0:L], scalar=xi[:, i:i + 1],
                                                      in1=o[:, 0:L], op0=ALU.subtract, op1=ALU.subtract, reverse1=True))
                        settle()
                    w = min(W, L - c * W)
                    dve.wait_ge(dist_made, NCH * b + n + 1)
                    dve.scalar_tensor_tensor(out=pen[:, n % 2, 0:w], in0=ring(b, 1, n)[:, 0:w], scalar=0.0,
                                             in1=o[:, c * W:c * W + w], op0=ALU.min, op1=ALU.min)\
                       .then_inc(dist_used, 1)
                    dve.wait_ge(dist_used, NCH * b + n + 1)
                    dve.wait_ge(scores_made, NCH * b + n + 1)
                    dve.tensor_tensor_reduce(o[:, c * W:c * W + w], ring(b, 0, n)[:, 0:w], pen[:, n % 2, 0:w],
                                             float(P) ** -0.5 / QK_UP ** 2, -3.0e38, ALU.add, ALU.max,
                                             mx[:, i, c:c + 1]).then_inc(scores_masked, 1)
                    if c == CHUNKS_ROW[i] - 1:
                        dve.wait_ge(scores_masked, NCH * b + n + 1)
                        dve.tensor_reduce(nmx[:, i:i + 1], mx[:, i, 0:c + 1], X, ALU.max, negate=True)\
                           .then_inc(max_ready, 1)
                if n in FINISH_AT:
                    i = FINISH_AT[n]
                    dve.wait_ge(probs_ready, BLK * b + i + 1)
                    step(dve.reciprocal(rinv[:, i:i + 1], rsum[:, i:i + 1])); settle()
                    dve.wait_ge(turned_used, NCH * b + CHUNKS_BEFORE[i + 1])
                    own = x[:, b * BLK + i, :]
                    dve.scalar_tensor_tensor(out=own, in0=ring(b, 3, i)[:, 0:P], scalar=rinv[:, i:i + 1],
                                             in1=own, op0=ALU.mult, op1=ALU.add).then_inc(row_ready, 1)
                    dve.wait_ge(row_ready, BLK * b + i + 1)
                    stats(b, i)
                if n in ROOT_AT:
                    ask_root(slice(ROOT_AT[n] * PER, (ROOT_AT[n] + 1) * PER))
                if n in NORM_AT and NORM_AT[n] not in LATE:
                    dve.wait_ge(root_ready, ROOTS * b + 4 + NORM_AT[n])
                    layer_norm(b, 1, NORM_AT[n])
                if n in SPLIT_AT:
                    split_input(b, SPLIT_AT[n])

            def route(b):
                for g in LATE:
                    dve.wait_ge(root_ready, ROOTS * b + 4 + g)
                    layer_norm(b, 1, g)
                    split_input(b, g)
                dve.wait_ge(sig_ready, b + 1)
                step(dve.tensor_scalar(sig[:, :, :], sig[:, :, :], 1.0, 0.5, ALU.add, ALU.mult)); settle()
                step(dve.tensor_tensor(score[:, :, :], sig[:, :, :],
                                       rb_bc[:, :].unsqueeze(1).broadcast_to([P, BLK, E]), ALU.add))
                settle()
                pair = score[:, :, :].rearrange("p i (g a c) -> p (i g) a c", g=GRP, a=2)
                for n, op in enumerate((ALU.max, ALU.min)):
                    step(dve.tensor_tensor(pm[:, :, :, :, n].rearrange("p i g a -> p (i g) a"),
                                           pair[:, :, :, 0], pair[:, :, :, 1], op))
                settle()
                step(dve.tensor_tensor(ps2[:, :, :, 0], pm[:, :, :, 0, 0], pm[:, :, :, 1, 0], ALU.max))
                step(dve.tensor_tensor(ps3[:, :, :, 0], pm[:, :, :, 0, 0], pm[:, :, :, 1, 0], ALU.min))
                step(dve.tensor_tensor(ps3[:, :, :, 1], pm[:, :, :, 0, 1], pm[:, :, :, 1, 1], ALU.max))
                settle()
                step(dve.tensor_tensor(ps2[:, :, :, 1], ps3[:, :, :, 0], ps3[:, :, :, 1], ALU.max)); settle()
                step(dve.tensor_tensor(gs[:, :, :], ps2[:, :, :, 0], ps2[:, :, :, 1], ALU.add)); settle()
                mine = gs[:, :, :].unsqueeze(3).broadcast_to([P, BLK, GRP, GRP])
                other = gs[:, :, :].unsqueeze(2).broadcast_to([P, BLK, GRP, GRP])
                step(dve.tensor_tensor(gcmp[:, :, :, :], other, mine, ALU.is_gt))
                step(dve.tensor_tensor(geq[:, :, :, :], other, mine, ALU.is_equal))
                settle()
                step(dve.tensor_tensor(geq[:, :, :, :].rearrange("p i g o -> p i (g o)"),
                                       geq[:, :, :, :].rearrange("p i g o -> p i (g o)"),
                                       tri[:, :, :].rearrange("p g o -> p (g o)").unsqueeze(1)
                                       .broadcast_to([P, BLK, GRP * GRP]), ALU.mult))
                settle()
                step(dve.tensor_tensor(gcmp[:, :, :, :], gcmp[:, :, :, :], geq[:, :, :, :], ALU.add)); settle()
                step(dve.tensor_reduce(grank[:, :, :], gcmp[:, :, :, :], X, ALU.add)); settle()
                step(dve.tensor_scalar(gsel[:, :, :], grank[:, :, :], 2.0, None, ALU.is_lt)); settle()
                chosen = gsel[:, :, :].unsqueeze(3).broadcast_to([P, BLK, GRP, EPG])
                wide = lambda t: t[:, :, :].rearrange("p i (g m) -> p i g m", g=GRP)
                step(dve.tensor_tensor(wide(score), wide(score), chosen, ALU.mult)); settle()
                step(dve.tensor_tensor(wide(score), wide(score), chosen, ALU.add)); settle()
                step(dve.tensor_scalar(score[:, :, :], score[:, :, :], -1.0, None, ALU.add)); settle()
                for i in range(BLK):
                    step(dve.max(best[:, i, :], score[:, i, :]))
                settle()
                for i in range(BLK):
                    step(dve.max_index(bidx[:, i, :], best[:, i, :], score[:, i, :]))
                settle()
                step(dve.tensor_copy(bf[:, :, :], bidx[:, :, :])); settle()
                every = iota[:, :].unsqueeze(1).broadcast_to([P, BLK, E])
                for k in range(TOP):
                    step(dve.tensor_tensor((hit if k else hits)[:, :, :], every,
                                           bf[:, :, k:k + 1].broadcast_to([P, BLK, E]), ALU.is_equal))
                    settle()
                    if k:
                        step(dve.tensor_tensor(hits[:, :, :], hits[:, :, :], hit[:, :, :], ALU.add)); settle()
                step(dve.tensor_tensor(comb[:, :, :], hits[:, :, :], sig[:, :, :], ALU.mult)); settle()
                step(dve.tensor_reduce(wsum[:, :], comb[:, :, :], X, ALU.add)); settle()
                step(dve.tensor_scalar(wsum[:, :], wsum[:, :], 1e-20, None, ALU.add)); settle()
                step(dve.reciprocal(wsum[:, :], wsum[:, :])); settle()
                up = SCALE if smooth(b) else SCALE * 2 * H_UP * W_UP
                step(dve.tensor_scalar(wsum[:, :], wsum[:, :], up, None, ALU.mult)); settle()
                step(dve.tensor_tensor(comb[:, :, :], comb[:, :, :],
                                       wsum[:, :].unsqueeze(2).broadcast_to([P, BLK, E]), ALU.mult))
                settle()
                step(dve.tensor_copy(cpart[:, :, 0, :], comb[:, :, :])); settle()
                step(dve.tensor_tensor(crest[:, :, :], comb[:, :, :], cpart[:, :, 0, :], ALU.subtract)); settle()
                step(dve.tensor_copy(cpart[:, :, 1, :], crest[:, :, :])); settle()
                step(dve.tensor_tensor(crest[:, :, :], crest[:, :, :], cpart[:, :, 1, :], ALU.subtract)); settle()
                dve.tensor_copy(cpart[:, :, 2, :], crest[:, :, :]).then_inc(comb_ready, 1)
                for n in range(2):
                    dve.wait_ge(comb_turned, 2 * b + n + 1)
                    dve.tensor_copy(combT[:, n * 8 * P:(n + 1) * 8 * P],
                                    bank[1 + n][0:3 * E, :].bitcast(BF16)).then_inc(comb_copied, 1)

            def mix(b, t):
                s = STEPS * b + t
                e = t % EX
                if t < STEPS:
                    n = E * (s // EX) + e
                    dve.wait_ge(silu_ready, s + 1)
                    if s >= 2:
                        dve.wait_ge(act_ready, s - 1)
                        dve.wait_ge(act_split, s - 1)
                    src = sg[:, s % 2, :]
                    if smooth(b):
                        dve.scalar_tensor_tensor(out=hid[:, s % 2, :], in0=src, scalar=1.0, in1=bank[3][:, :],
                                                 op0=ALU.add, op1=ALU.mult).then_inc(hidden_ready, 1)
                        dve.wait_ge(hidden_ready, s + 1)
                        src = hid[:, s % 2, :]
                    if e < E:
                        dve.wait_ge(weight_made, n + 1)
                        dve.tensor_tensor(sw[:, s % 2, :], bank[5][:, :], src, ALU.mult)\
                           .then_inc(silu_weighted, 1)
                        dve.wait_ge(silu_weighted, n + 1)
                        dve.wait_ge(up_made, s + 1)
                        dve.tensor_tensor(act_g[:, s % 2, :], bank[4][:, :], sw[:, s % 2, :], ALU.mult)\
                           .then_inc(act_ready, 1)
                    else:
                        dve.wait_ge(up_made, s + 1)
                        up = G_UP / (H_UP * W_UP) / (2 * H_UP * W_UP if smooth(b) else 1)
                        dve.scalar_tensor_tensor(out=act_g[:, s % 2, :], in0=bank[4][:, :], scalar=up, in1=src,
                                                 op0=ALU.mult, op1=ALU.mult).then_inc(act_ready, 1)
                if ends_chunk(t, 3):
                    f = (s - 3) // EX
                    dve.wait_ge(y_turned, f + 1)
                    dve.tensor_tensor(scaled[:, :, :], bank[6][:, :].rearrange("p (k d) -> p k d", d=P),
                                      gbc[:, b, 1:2, :].broadcast_to([P, PER, P]), ALU.mult)\
                       .then_inc(out_scaled, 1)
                    dve.wait_ge(out_scaled, f + 1)
                    o = x[:, f * PER:(f + 1) * PER, :]
                    dve.tensor_tensor(o, o, scaled[:, :, :], ALU.add).then_inc(out_ready, 1)

            run(inputs, attention, route, mix)

_INS = ["L0_attn_hidden_states", "L0_attn_Wq", "L0_attn_bq", "L0_attn_Wk", "L0_attn_bk", "L0_attn_Wv",
        "L0_attn_bv", "L0_attn_Wo", "L0_attn_bo", "L0_attn_Wtq", "L0_attn_btq", "L0_attn_Wfq", "L0_attn_bfq",
        "L0_ffn_router_w", "L0_ffn_bias", "L0_ffn_gate_w", "L0_ffn_up_w", "L0_ffn_down_w", "L0_ffn_sh_gate_w",
        "L0_ffn_sh_up_w", "L0_ffn_sh_down_w", "L0_c", "L0_wmod"]


def kernel(**inputs):
    import concourse.bacc as _bacc
    from concourse.bass_utils import run_bass_kernel_spmd as _run

    nc = _bacc.Bacc("TRN2", target_bir_lowering=False, num_devices=1)
    arrays, args = {}, []
    for name in _INS:
        a = np.ascontiguousarray(inputs[name])
        arrays[f"in_{name}"] = a
        args.append(nc.dram_tensor(f"in_{name}", a.shape, mybir.dt.from_np(a.dtype), kind="ExternalInput").ap())
    args.append(nc.dram_tensor("out_x", (NB, N, P), F32, kind="ExternalOutput").ap())
    build(nc, *args)
    r = _run(nc, [arrays], core_ids=[0])
    return r.results[0]["out_x"]
```

```python
from contextlib import ExitStack

import numpy as np

import concourse.bass as bass
from concourse import mybir

F32 = mybir.dt.float32
BF16 = mybir.dt.bfloat16
F16 = mybir.dt.float16
U32 = mybir.dt.uint32
ALU = mybir.AluOpType
ACT = mybir.ActivationFunctionType
X = mybir.AxisListType.X

P = 128
NB = 2
N = 2048
BLK = N // P
W = 512
CH = N // W
PER = W // P
E = 16
NS = 2
EX = E + NS
GRP = 4
EPG = E // GRP
TOP = 4
SCALE = 2.5
EPS = 1e-5
NEAR = 0.25

WEDGE = 2.4417243e-4
HUGE = float(2.0 ** 90)
HUGER = float(2.0 ** 110)
FEAT = 27
TINY = 1e-30

QK_UP = 16.0
H_UP = 32.0
W_UP = 64.0
G_UP = 32.0
ROWS = 3
PIECE = EX // 2
STEPS = EX * CH

STATS = 0
NORM = STATS + CH
QUERIES = 9
POSITIONS = 10
FEATURES = 17
SPREAD = 19
VALUES = ({14: (0,), 15: (1,), 16: (2,), 20: (3,)}, {21: (0,), 22: (1,), 23: (2,), 24: (3,)})
BASE = 18
PIECES = 25

CHUNKS_ROW = [i // PER + 1 for i in range(BLK)]
CHUNKS_BEFORE = [sum(CHUNKS_ROW[:i]) for i in range(BLK + 1)]
NCH = CHUNKS_BEFORE[BLK]
CHUNKS = [(i, c) for i in range(BLK) for c in range(CHUNKS_ROW[i])]
EXP_AT = {n + CHUNKS_ROW[i]: n for n, (i, c) in enumerate(CHUNKS)}
TURN_AT = {n + CHUNKS_ROW[i] + 1: n for n, (i, c) in enumerate(CHUNKS)}
RISE_AT = {CHUNKS_BEFORE[i - ROWS + 1] + CHUNKS_ROW[i - ROWS]: i for i in range(ROWS, BLK)}
MEASURES_AT = {0: [2]}
for slot, i in RISE_AT.items():
    for c in range(CHUNKS_ROW[i]):
        MEASURES_AT.setdefault(slot + c, []).append(CHUNKS_BEFORE[i] + c)
PRODUCT_AT = {slot + 1: n for slot, n in TURN_AT.items()}
FINISH_AT = {slot + 1: CHUNKS[n][0] for slot, n in PRODUCT_AT.items() if CHUNKS[n][1] == CHUNKS_ROW[CHUNKS[n][0]] - 1}
SLOTS = max(FINISH_AT) + 1
ROOT_AT = {slot: i // PER for slot, i in FINISH_AT.items() if i % PER == PER - 1}
NORM_AT = {slot + 1: g for slot, g in ROOT_AT.items() if g < CH - 1}
SHIFT_AT = {slot + 1: g for slot, g in NORM_AT.items()}
SPLIT_AT = {slot + 1: g for slot, g in SHIFT_AT.items()}
BASE_AT = {first + every * n: (g, n) for g, first, every in ((1, 0, 1), (2, 6, 2), (3, 17, 3)) for n in range(5)}
WEIGHTS_AT = {8: 2, 17: 3, 30: 4, 34: 5}
ROOTS = 3 + CH
EARLY = (0, (CH - 1) * PER)
LAST = ((CH - 1) * PER, BLK)
ROUTE_PARTS = 6
POOL_FROM = CHUNKS_BEFORE[14]
LOGITS_AT = max(SPLIT_AT) + 1
ROUTE_AT = {SLOTS - 4 - ROUTE_PARTS + n: n for n in range(ROUTE_PARTS)}
HALVES = ((0, 6), (6, 12))
COMB_AT = {SLOTS - 2 + n: n for n in range(len(HALVES))}
PART_EVERY = 1
LATE_STEPS = 5 + PART_EVERY * ROUTE_PARTS


class Chain:

    def __init__(self, engine, semaphore):
        self.engine, self.semaphore, self.n = engine, semaphore, 0

    def step(self, instruction):
        instruction.then_inc(self.semaphore, 1)
        self.n += 1

    def settle(self):
        self.engine.wait_ge(self.semaphore, self.n)


def build(nc, hs, Wq, bq, Wk, bk, Wv, bv, Wo, bo, Wtq, btq, Wfq, bfq, router_w, router_b,
          gate_w, up_w, down_w, sh_gate_w, sh_up_w, sh_down_w, cvec, wmod, out):
    ctx = ExitStack()
    with ctx:
        def sb(name, shape, dt=F32):
            return ctx.enter_context(nc.sbuf_tensor(name, shape, dt))

        def sem(name):
            return ctx.enter_context(nc.semaphore(name))

        bank = [ctx.enter_context(nc.psum_tensor(f"bank{i}", [P, W], F32)) for i in range(8)]

        wv = sb("wv", [P, P])
        wT = sb("wT", [P, 3, P])
        rT = sb("rT", [P, 2, E], F16); colu = sb("colu", [P, 2])
        tqT = sb("tqT", [P, 2])
        wfq = sb("wfq", [P, 2])
        cols = sb("cols", [P, 5])
        btq_bc = sb("btq_bc", [P, 2])
        rb_bc = sb("rb_bc", [P, E])
        sc = sb("sc", [P, NB])
        md = sb("md", [P, 6, NB])
        gbc = sb("gbc", [P, NB, 2, P])
        vh = sb("vh", [P, NB, P])
        x3 = sb("x3", [P, 3])
        terms = sb("terms", [P, NB, 4, P])
        share = sb("share", [P, PER, P])
        stage = sb("stage", [P, 2, PIECE, P])
        wg = sb("wg", [P, 2, EX, P], F16); wu = sb("wu", [P, 2, EX, P], F16); wd = sb("wd", [P, 2, EX, P], F16)
        ident = sb("ident", [P, P]); identb = sb("identb", [P, P], BF16)
        minus = sb("minus", [P, P], BF16)
        causal = sb("causal", [P, P], BF16)
        ones = sb("ones", [P, P])
        selw = sb("selw", [3 * E, E, P], BF16)
        selx = sb("selx", [FEAT, P], BF16); sely = sb("sely", [FEAT, P], BF16)
        vw = sb("vw", [P, 5])

        x = sb("x", [P, NB * BLK, P])
        hT = sb("hT", [P, N])
        qT = sb("qT", [P, 2, N], F16); kT = sb("kT", [P, 2, N], F16)
        h2 = sb("h2", [P, 2, N], F16)
        v = sb("v", [P, BLK, P])
        xb = sb("xb", [P, N]); yb = sb("yb", [P, N])
        pen = sb("pen", [P, 2, W], BF16); dx = sb("dx", [P, 2, W])
        row = sb("row", [P, ROWS, N])
        gsgn, gmag, graw = (row[:, 0, k * W:(k + 1) * W] for k in range(3))
        wm = row[:, 1, 0:6 * P]
        wq, wk, wo = (row[:, 1, k * P:(k + 1) * P] for k in range(6, 9))
        scb = row[:, 1, 9 * P:11 * P].rearrange("p (b k) -> p b k", b=NB)
        x3b = row[:, 1, 11 * P:14 * P].rearrange("p (n k) -> p n k", n=3)
        rw, wtq, c2, sc2 = (row[0:m, 2, k * P:(k + 1) * P] for k, m in enumerate((E, 2, NB, NB)))
        xn = sb("xn", [P, 2 * PER, P])
        ptr = sb("ptr", [P, 2, W])
        st = sb("st", [P, BLK, 6]); mv = sb("mv", [P, BLK, 2])
        ve = sb("ve", [P, BLK]); rs = sb("rs", [P, BLK]); runit = sb("runit", [P, BLK])
        minus_half = sb("minus_half", [P, BLK]); half = sb("half", [P, 1])
        w_up = sb("w_up", [P, 1])
        warm = sb("warm", [P, 1])
        qp = sb("qp", [P, BLK, 2]); qc = sb("qc", [P, BLK, 2]); sq = sb("sq", [P, BLK, 2])
        nrm = sb("nrm", [P, BLK]); unit = sb("unit", [P, BLK, 2])
        part = sb("part", [P, 2]); mean = sb("mean", [P, 2])
        mom = sb("mom", [P, 5, BLK]); mpart = sb("mpart", [P, 5]); msum = sb("msum", [P, 5])
        m2 = sb("m2", [P, 5]); var = sb("var", [P, 1]); sdv = sb("sdv", [P, 1])
        thr = sb("thr", [P, 1])
        quant = sb("quant", [P, BLK, 5])
        rest = sb("rest", [P, BLK, 5])
        parts = sb("parts", [P, 3, BLK, 5], BF16)
        fl = sb("fl", [P, BLK, FEAT], BF16); fr = sb("fr", [P, BLK, FEAT], BF16)
        flT = sb("flT", [FEAT, N], BF16); frT = sb("frT", [FEAT, N], BF16)
        nxi = sb("nxi", [P, BLK]); nyi = sb("nyi", [P, BLK])
        mx = sb("mx", [P, BLK, CH]); nmx = sb("nmx", [P, BLK])
        rsum = sb("rsum", [P, BLK, CH]); rinv = sb("rinv", [P, BLK])
        sig = sb("sig", [P, BLK, E]); score = sb("score", [P, BLK, E])
        pm = sb("pm", [P, BLK, GRP, 2, 2]); ps2 = sb("ps2", [P, BLK, GRP, 2]); ps3 = sb("ps3", [P, BLK, GRP, 2])
        gs = sb("gs", [P, BLK, GRP])
        gcmp = pm[:, :, :, :, :].rearrange("p i g a n -> p i g (a n)")
        geq = sb("geq", [P, BLK, GRP, GRP])
        hits = pm[:, :, :, :, :].rearrange("p i g a n -> p i (g a n)")
        hit = crest = geq[:, :, :, :].rearrange("p i g o -> p i (g o)")
        tri = sb("tri", [P, GRP, GRP])
        grank = sb("grank", [P, BLK, GRP]); gsel = sb("gsel", [P, BLK, GRP])
        best = sb("best", [P, BLK, 8]); bidx = sb("bidx", [P, BLK, 8], U32); bf = sb("bf", [P, BLK, 8])
        iota = sb("iota", [P, E]); iotai = sb("iotai", [P, E], mybir.dt.int32)
        wsum = sb("wsum", [P, BLK]); comb = sb("comb", [P, BLK, E])
        cpart = sb("cpart", [P, BLK, 3, E], BF16); combT = sb("combT", [3 * E, N], BF16)
        sg = stage[:, 0, 0:2 * PER, :].rearrange("p (n k) d -> p n (k d)", n=2)
        act_g = stage[:, 1, 0:2 * PER, :].rearrange("p (n k) d -> p n (k d)", n=2)
        sw = sb("sw", [P, 2, W]); hid = sb("hid", [P, 2, W])
        gp = sb("gp", [P, 3, 2, W], F16)
        ysb = sb("ysb", [P, W]); scaled = ysb[:, :].rearrange("p (k d) -> p k d", k=PER)

        small_loaded = sem("small_loaded"); x_loaded = sem("x_loaded")
        consts_ready = sem("consts_ready"); pool_step = sem("pool_step")
        set_pe = sem("set_pe")
        set_act = sem("set_act")
        set_dve = sem("set_dve")
        dve_step = sem("dve_step")
        root_asked = sem("root_asked"); root_ready = sem("root_ready")
        stage_loaded = [sem(f"stage_loaded{n}") for n in range(2)]; stage_used = sem("stage_used")
        high_ready = sem("high_ready")
        mix_high = sem("mix_high"); mix_split = sem("mix_split")
        act_high = sem("act_high"); act_split = sem("act_split")
        norm_ready = sem("norm_ready"); norm_turned = sem("norm_turned"); h_ready = sem("h_ready")
        pos_ready = sem("pos_ready")
        part_ready = sem("part_ready"); part_summed = sem("part_summed")
        q_made = sem("q_made"); q_ready = sem("q_ready")
        unit_ready = sem("unit_ready"); base_ready = sem("base_ready")
        feat_ready = sem("feat_ready"); feat_turned = sem("feat_turned")
        feat_copied = [sem(f"feat_copied{n}") for n in range(2)]
        v_made = sem("v_made"); v_ready = sem("v_ready")
        spread_made = [sem(f"spread_made{n}") for n in range(2)]
        spread_ready = [sem(f"spread_ready{n}") for n in range(2)]
        dist_made = sem("dist_made"); dist_used = sem("dist_used")
        scores_made = sem("scores_made"); scores_masked = sem("scores_masked")
        rise_ready = sem("rise_ready")
        dx_ready = sem("dx_ready")
        measure_ready = sem("measure_ready")
        max_ready = sem("max_ready"); probs_ready = sem("probs_ready")
        probs_turned = sem("probs_turned"); turned_copied = sem("turned_copied")
        turned_used = sem("turned_used"); row_ready = sem("row_ready")
        logits_made = sem("logits_made"); sig_ready = sem("sig_ready")
        comb_ready = sem("comb_ready"); comb_turned = sem("comb_turned"); comb_copied = sem("comb_copied")
        gate_made = sem("gate_made"); up_made = sem("up_made"); down_made = sem("down_made")
        weight_made = sem("weight_made")
        silu_ready = sem("silu_ready")
        hidden_ready = sem("hidden_ready"); silu_weighted = sem("silu_weighted"); act_ready = sem("act_ready")
        y_copied = sem("y_copied"); y_turned = sem("y_turned"); out_scaled = sem("out_scaled")
        expert_added = sem("expert_added"); out_ready = sem("out_ready"); stored = sem("stored")

        block = ctx.enter_context(nc.Block())
        SMALL = 16

        def batch_view(t):
            return t.rearrange("b (n p) d -> p (b n) d", p=P)

        def run(inputs, attention, step, late, finish=None):
            for k in range(PIECES):
                inputs(0, k)
            for n in range(SLOTS):
                if finish:
                    finish(0, n)
                attention(0, n)
            for s in range(NB * STEPS + 3):
                b, t = divmod(s, STEPS)
                if finish and b + 1 < NB and 0 <= t - PIECES < SLOTS:
                    finish(b + 1, t - PIECES)
                step(s)
                if b < NB and t < LATE_STEPS:
                    late(b, t)
                if b + 1 < NB:
                    n = t - PIECES
                    if n < 0:
                        inputs(b + 1, t)
                    if 0 <= n < SLOTS:
                        attention(b + 1, n)

        def ring(b, which, n):
            first, second = ((0, 3), (1, 4), (2, 5), (7, 6))[which]
            return bank[second if b == 0 and n % 2 else first]

        def by_pool(b, m):
            return b > 0 or m >= POOL_FROM

        def pooled(b, m):
            return b * NCH + m - POOL_FROM + 1

        def gate_bank(s):
            return bank[3 if smooth(s) else (3, 2)[s % 2]]

        def up_bank(s):
            return bank[4 if smooth(s) else (4, 5)[s % 2]]

        def down_bank(s):
            return bank[6 if smooth(s) else s % 2]

        def norm_bank(which, g):
            if which == 0:
                return bank[g % 2]
            return bank[7 if g == CH - 1 else 2]

        def value_bank(b, g):
            return bank[g % 2 + (3 if b == 0 else 0)]

        def turned_features(n):
            return (frT, flT)[n // 2][:, (n % 2) * 8 * P:(n % 2 + 1) * 8 * P]

        FEAT_BANK = (2, 0, 1, 2)

        def behind(b):
            return 2 if b == 0 else 1

        def smooth(s):
            return s < (NB - 1) * STEPS

        def ends_chunk(s, lag):
            return s >= lag and (s - lag) % EX == EX - 1

        @block.sync
        def _(sp):
            sp.dma_start(x[:, 0:BLK, :], batch_view(hs)[:, 0:BLK, :]).then_inc(x_loaded, 16)
            sp.dma_start(c2[:, :], cvec).then_inc(small_loaded, 16)
            sp.dma_start(wm[:, :], wmod).then_inc(small_loaded, 16)
            for dst, src in ((wq, Wq), (wk, Wk), (wv, Wv), (wo, Wo), (rw, router_w), (wtq, Wtq), (wfq, Wfq)):
                sp.dma_start(dst[:, :], src).then_inc(small_loaded, 16)
            for n, src in enumerate((bq, bk, bv, bo, bfq)):
                sp.dma_start(cols[:, n:n + 1], src.rearrange("(d o) -> d o", o=1)).then_inc(small_loaded, 16)
            for dst, src in ((btq_bc, btq), (rb_bc, router_b)):
                sp.dma_start(dst[:, :], src.rearrange("(o d) -> o d", o=1).broadcast_to([P, dst.shape[1]]))\
                  .then_inc(small_loaded, 16)
            sp.wait_ge(x_loaded, 16)
            sp.dma_start(x[:, BLK:, :], batch_view(hs)[:, BLK:NB * BLK, :]).then_inc(x_loaded, 16)
            for n in range(6):
                routed, shared = ((gate_w.rearrange("e d f -> d e f"), sh_gate_w.rearrange("d (s f) -> d s f", s=NS)),
                                  (up_w.rearrange("e d f -> d e f"), sh_up_w.rearrange("d (s f) -> d s f", s=NS)),
                                  (down_w.rearrange("e f d -> f e d"),
                                   sh_down_w.rearrange("(s f) d -> f s d", s=NS)))[n // 2]
                if n >= 2:
                    sp.wait_ge(stage_used, n - 1)
                dst = stage[:, n % 2, :, :]
                if n % 2 == 0:
                    sp.dma_start(dst, routed[:, 0:PIECE, :]).then_inc(stage_loaded[0], 16)
                else:
                    sp.dma_start(dst[:, 0:E - PIECE, :], routed[:, PIECE:E, :]).then_inc(stage_loaded[1], 16)
                    sp.dma_start(dst[:, E - PIECE:PIECE, :], shared).then_inc(stage_loaded[1], 16)
            with sp.Fori(0, NB * CH) as it:
                sp.wait_ge(out_ready, it + 1)
                sp.dma_start(batch_view(out)[:, bass.ds(it * PER, PER), :],
                             x[:, bass.ds(it * PER, PER), :]).then_inc(stored, 16)
            sp.wait_ge(stored, 16 * NB * CH)

        @block.gpsimd
        def _(pool):
            chain = Chain(pool, pool_step)
            chain.step(pool.memset(ident[:, :], 0.0))
            chain.step(pool.memset(ones[:, :], 1.0))
            chain.step(pool.memset(causal[:, :], 0.0))
            chain.step(pool.memset(selw[:, :, :], 0.0))
            chain.step(pool.memset(selx[:, :], 0.0))
            chain.step(pool.memset(sely[:, :], HUGE))
            chain.step(pool.memset(tri[:, :, :], 0.0))
            chain.step(pool.memset(fl[:, :, :], 0.0))
            chain.step(pool.memset(minus_half[:, :], -0.5))
            chain.step(pool.memset(half[:, :], 0.5))
            chain.step(pool.memset(w_up[:, :], W_UP))
            chain.step(pool.memset(fr[:, :, :], 0.0))
            chain.step(pool.memset(minus[:, :], 0.0))
            chain.step(pool.memset(identb[:, :], 0.0))
            chain.step(pool.iota(iotai[:, :], pattern=[[1, E]], base=0, channel_multiplier=0))
            w_den = float(N) * N - 1
            for n, wgt in enumerate((4.0, 8.0, 4.0, -2.0, 2.0 * N)):
                chain.step(pool.memset(vw[:, n:n + 1], wgt / w_den))
            chain.settle()
            chain.step(pool.affine_select(out=ident[:, :], in_=ident[:, :], compare_op=ALU.not_equal, fill=1.0,
                                          base=0, pattern=[[-1, P]], channel_multiplier=1))
            chain.step(pool.affine_select(out=identb[:, :], in_=identb[:, :], compare_op=ALU.not_equal, fill=1.0,
                                          base=0, pattern=[[-1, P]], channel_multiplier=1))
            chain.step(pool.affine_select(out=minus[:, :], in_=minus[:, :], compare_op=ALU.not_equal, fill=-HUGER,
                                          base=0, pattern=[[-1, P]], channel_multiplier=1))
            chain.step(pool.affine_select(out=causal[:, :], in_=causal[:, :], compare_op=ALU.is_ge, fill=1.0,
                                          base=0, pattern=[[-1, P]], channel_multiplier=1))
            for k in range(3):
                chain.settle()
                chain.step(pool.affine_select(out=selw[:, :, :], in_=selw[:, :, :], compare_op=ALU.not_equal,
                                              fill=G_UP / (H_UP * W_UP) ** 2 / 2, base=-E * k, pattern=[[-1, E], [0, P]],
                                              channel_multiplier=1))
            chain.step(pool.affine_select(out=tri[:, :, :], in_=tri[:, :, :], compare_op=ALU.is_ge, fill=1.0,
                                          base=0, pattern=[[-1, GRP], [1, GRP]], channel_multiplier=0))
            chain.step(pool.memset(selx[0:3, :], HUGE))
            chain.step(pool.affine_select(out=sely[:, :], in_=sely[:, :], compare_op=ALU.is_ge, fill=0.0,
                                          base=-(FEAT - 3), pattern=[[0, P]], channel_multiplier=1))
            chain.step(pool.tensor_copy(iota[:, :], iotai[:, :]))
            chain.step(pool.memset(fr[:, :, 18:21], 1.0))
            chain.step(pool.memset(fl[:, :, 21:24], HUGE))
            chain.settle()
            pool.sem_inc(consts_ready, 1)

            def power(dst, src, exponent, count):
                pool.wait_ge(root_asked, count)
                pool.tensor_tensor(dst, src, exponent, ALU.pow).then_inc(root_ready, 1)

            def split(n):
                pool.wait_ge(stage_loaded[n % 2], (n // 2 + 1) * (16, 32)[n % 2])
                w, dst = stage[:, n % 2, :, :], (wg, wu, wd)[n // 2]
                lot = slice(n % 2 * PIECE, (n % 2 + 1) * PIECE)
                up = w_up[:, :].unsqueeze(2).broadcast_to([P, PIECE, P])
                chain.step(pool.tensor_tensor(dst[:, 0, lot, :], w, up, ALU.mult)); chain.settle()
                chain.step(pool.tensor_tensor(w, w, up, ALU.mult)); chain.settle()
                pool.tensor_tensor(dst[:, 1, lot, :], w, dst[:, 0, lot, :], ALU.subtract).then_inc(stage_used, 1)

            def base(b, g, part_of):
                if g == 0 and part_of == 0:
                    pool.wait_ge(set_dve, 4)
                    pool.wait_ge(unit_ready, b + 1)
                    pool.wait_ge(norm_ready, 2 * BLK * b + BLK)
                own = x[:, b * BLK + g * PER:b * BLK + (g + 1) * PER, :]

                def add_to_x():
                    return pool.tensor_tensor(own, own, share[:, :, :], ALU.add)

                def spread(n):
                    return terms[:, b, n:n + 1, :].broadcast_to([P, PER, P])

                def spread_token(column):
                    return column.broadcast_to([P, PER, P])

                def change(other, op):
                    chain.step(pool.tensor_tensor(share[:, :, :], share[:, :, :], other, op)); chain.settle()

                lot = slice(g * PER, (g + 1) * PER)
                if part_of == 0:
                    chain.step(pool.tensor_tensor(share[:, :, :], own, spread_token(mv[:, lot, 0:1]), ALU.subtract))
                    chain.settle()
                    change(spread_token(rs[:, lot].unsqueeze(2)), ALU.mult)
                if part_of == 1:
                    change(spread(3), ALU.mult)
                    change(spread(2), ALU.add)
                if part_of in (2, 3):
                    n = part_of - 2
                    chain.step(add_to_x()); chain.settle()
                    chain.step(pool.tensor_tensor(share[:, :, :], spread(n),
                                                  spread_token(unit[:, lot, n:n + 1]), ALU.mult))
                    chain.settle()
                if part_of == 4:
                    add_to_x().then_inc(base_ready, 1)
                    pool.wait_ge(base_ready, CH * b + g + 1)

            def measure(b, m):
                i, c = CHUNKS[m]
                w = min(W, (i + 1) * P - c * W)
                pool.wait_ge(dx_ready, pooled(b, m))
                o = row[:, i % ROWS, c * W:c * W + w]
                pool.tensor_tensor(o, o, dx[:, pooled(b, m) % 2, 0:w], ALU.subtract).then_inc(measure_ready, 1)

            def inputs(b, k):
                if k == STATS + CH - 1:
                    power(rs[:, :], ve[:, :], minus_half[:, :], ROOTS * b + 1)
                if b == 0 and k in (NORM, POSITIONS + 5):
                    split(0 if k == NORM else 1)
                if k == POSITIONS:
                    power(runit[:, :], nrm[:, :], minus_half[:, :], ROOTS * b + 2)
                if k == POSITIONS + 4:
                    power(sdv[:, :], var[:, :], half[:, :], ROOTS * b + 3)
                if BASE <= k < BASE + 5:
                    base(b, 0, k - BASE)
                if k == PIECES - 1 and b:
                    for m in range(2):
                        measure(b, m)

            def attention(b, n):
                for m in MEASURES_AT.get(n, ()):
                    if by_pool(b, m):
                        measure(b, m)
                if n in ROOT_AT:
                    lot = slice(ROOT_AT[n] * PER, (ROOT_AT[n] + 1) * PER)
                    power(rs[:, lot], ve[:, lot], minus_half[:, lot], ROOTS * b + 4 + ROOT_AT[n])
                if n in BASE_AT:
                    base(b, *BASE_AT[n])
                if b == 0 and n in WEIGHTS_AT:
                    split(WEIGHTS_AT[n])

            def step(s):
                if s < NB * STEPS:
                    pool.wait_ge(act_high, s + 1)
                    if s >= 3:
                        pool.wait_ge(down_made, s - 2)
                    pool.tensor_tensor(gp[:, s % 3, 1, :], act_g[:, s % 2, :], gp[:, s % 3, 0, :], ALU.subtract)\
                        .then_inc(act_split, 1)

            def late(b, t):
                pass

            run(inputs, attention, step, late)

        @block.scalar
        def _(act):
            act.wait_ge(small_loaded, 16 * SMALL)
            act.activation(sc2[:, :], c2[:, :], ACT.Silu).then_inc(set_act, 1)
            act.wait_ge(set_dve, 2)

            def shift(b, which, g):
                act.wait_ge(norm_turned, 2 * CH * b + which * CH + g + 1)
                src = norm_bank(which, g)
                act.activation(hT[:, g * W:(g + 1) * W], src[:, :], ACT.Identity,
                               bias=md[:, 3 * which, b:b + 1], scale=md[:, 3 * which + 1, b:b + 1])\
                   .then_inc(h_ready, 1)

            def rise(b, m):
                i, c = CHUNKS[m]
                w = min(W, (i + 1) * P - c * W)
                lot = slice(c * W, c * W + w)
                if i >= ROWS:
                    act.wait_ge(probs_turned, NCH * b + CHUNKS_BEFORE[i - ROWS] + min(c + 1, CHUNKS_ROW[i - ROWS]))
                act.activation(row[:, i % ROWS, lot], yb[:, lot], ACT.Abs, bias=nyi[:, i:i + 1]).then_inc(rise_ready, 1)
                if by_pool(b, m):
                    if pooled(b, m) > 2:
                        act.wait_ge(measure_ready, pooled(b, m) - 2)
                    act.wait_ge(rise_ready, NCH * b + m + 1)
                    act.activation(dx[:, pooled(b, m) % 2, 0:w], xb[:, lot], ACT.Identity, bias=nxi[:, i:i + 1])\
                       .then_inc(dx_ready, 1)

            def mixture_input(b, g):
                shift(b, 1, g)
                act.wait_ge(h_ready, 2 * CH * b + CH + g + 1)
                if b:
                    act.wait_ge(up_made, STEPS * (b - 1) + EX * (g + 1))
                lot = slice(g * W, (g + 1) * W)
                act.mul(h2[:, 0, lot], hT[:, lot], H_UP).then_inc(mix_high, 1)

            def inputs(b, k):
                if NORM < k <= NORM + CH:
                    shift(b, 0, k - NORM - 1)
                if k == QUERIES and b == 0:
                    act.activation(warm[:, :], colu[:, 0:1], ACT.Exp, scale=0.0)
                if QUERIES <= k < QUERIES + 2 * CH:
                    m = k - QUERIES
                    act.wait_ge(q_made, 2 * CH * b + m + 1)
                    act.activation((qT, kT)[m // CH][:, 0, m % CH * W:(m % CH + 1) * W], bank[m % 2][:, :],
                                   ACT.Identity, bias=colu[:, m // CH:m // CH + 1]).then_inc(high_ready, 1)
                if k in VALUES[b]:
                    for g in VALUES[b][k]:
                        act.wait_ge(v_made, CH * b + g + 1)
                        act.copy(v[:, g * PER:(g + 1) * PER, :], value_bank(b, g)[:, :]).then_inc(v_ready, 1)
                if k in (FEATURES, FEATURES + 1):
                    n = 2 * (k - FEATURES)
                    act.wait_ge(feat_turned, 4 * b + n + 1)
                    act.copy(turned_features(n), bank[FEAT_BANK[n]][0:FEAT, :].bitcast(BF16))\
                       .then_inc(feat_copied[0], 1)
                if k in (SPREAD, SPREAD + 1):
                    for g in (2 * (k - SPREAD), 2 * (k - SPREAD) + 1):
                        act.wait_ge(spread_made[1], CH * b + g + 1)
                        act.copy(yb[:, g * W:(g + 1) * W], bank[g % 2][:, :]).then_inc(spread_ready[1], 1)
                if k == PIECES - 1:
                    for m in range(2):
                        act.wait_ge(spread_ready[m], CH * (b + 1))
                    for m in range(2):
                        rise(b, m)

            def attention(b, n):
                if n in TURN_AT:
                    m = TURN_AT[n]
                    i, g = CHUNKS[m]
                    w = min(W, (i + 1) * P - g * W)
                    act.wait_ge(probs_turned, NCH * b + m + 1)
                    if m >= 2:
                        act.wait_ge(turned_used, NCH * b + m - 1)
                    act.copy(ptr[:, m % 2, 0:w], ring(b, 2, m)[:, 0:w]).then_inc(turned_copied, 1)
                if n in EXP_AT:
                    m = EXP_AT[n]
                    i, c = CHUNKS[m]
                    lot = slice(c * W, min((c + 1) * W, (i + 1) * P))
                    act.wait_ge(max_ready, BLK * b + i + 1)
                    act.activation(row[:, i % ROWS, lot], row[:, i % ROWS, lot], ACT.Exp, bias=nmx[:, i:i + 1],
                                   accum_out=rsum[:, i, c:c + 1]).then_inc(probs_ready, 1)
                for m in MEASURES_AT.get(n, ()):
                    rise(b, m)
                if n in SHIFT_AT:
                    mixture_input(b, SHIFT_AT[n])
                if n == LOGITS_AT:
                    sigmoid(b, EARLY, bank[2], 0)

            def sigmoid(b, lot, src, n):
                act.wait_ge(logits_made, 2 * b + n + 1)
                act.activation(sig[:, lot[0]:lot[1], :], src[:, 0:(lot[1] - lot[0]) * E], ACT.Tanh,
                               scale=0.5 / (H_UP * W_UP)).then_inc(sig_ready, 1)

            def late(b, t):
                if t == 1:
                    mixture_input(b, CH - 1)
                if t == 3:
                    sigmoid(b, LAST, bank[7], 1)

            def silu(s):
                act.wait_ge(gate_made, s + 1)
                if s >= 2:
                    act.wait_ge(act_ready, s - 1)
                func, half_of = (ACT.Tanh, 0.5) if smooth(s) else (ACT.Silu, 1.0)
                act.activation(sg[:, s % 2, :], gate_bank(s)[:, :], func, scale=half_of / (H_UP * W_UP))\
                   .then_inc(silu_ready, 1)

            def step(s):
                if s == 0:
                    silu(0)
                if smooth(s + 1):
                    silu(s + 1)
                if 1 <= s <= NB * STEPS:
                    act.wait_ge(act_ready, s)
                    if s >= 4:
                        act.wait_ge(down_made, s - 3)
                    act.copy(gp[:, (s - 1) % 3, 0, :], act_g[:, (s - 1) % 2, :]).then_inc(act_high, 1)
                if not smooth(s + 1) and s + 1 < NB * STEPS:
                    silu(s + 1)
                if ends_chunk(s, 2) and smooth(s - 2):
                    f = (s - 2) // EX
                    act.wait_ge(down_made, EX * (f + 1))
                    if f:
                        act.wait_ge(out_ready, f)
                    act.mul(ysb[:, :], bank[6][:, :], 1 / (G_UP * W_UP)).then_inc(y_copied, 1)

            run(inputs, attention, step, late)

        @block.tensor
        def _(pe):
            mm = pe.matmul
            pe.wait_ge(small_loaded, 16 * SMALL)
            pe.wait_ge(consts_ready, 1)
            for n, w in enumerate((wq, wk, wo)):
                pe.transpose(bank[0][:, n * P:(n + 1) * P], w[:, :], ident[:, :])
            pe.transpose(bank[1][:, 0:E], rw[:, :], ident[0:E, 0:E])
            pe.transpose(bank[1][:, E:E + 2], wtq[:, :], ident[0:2, 0:2])
            pe.wait_ge(set_act, 1)
            pe.transpose(bank[1][:, E + 2:E + 2 + NB], sc2[:, :], ident[0:NB, 0:NB]).then_inc(set_pe, 1)
            pe.wait_ge(set_dve, 1)
            for j in range(6):
                last = mm(bank[2][:, NB * j:NB * (j + 1)], wm[:, j * P:(j + 1) * P], sc[:, :], start=True, stop=True)
            last.then_inc(set_pe, 1)
            def spread_modulation(columns, dst):
                for b in range(NB):
                    for n, j in enumerate(columns):
                        o = (2 * b + n) * P
                        last = mm(dst[:, o:o + P], scb[:, b, :], wm[:, j * P:(j + 1) * P], start=True, stop=True)
                return last

            spread_modulation((2, 5), bank[3]).then_inc(set_pe, 1)

            def pair(out_bank, weights, data, start=True, stop=True):
                mm(out_bank, weights[0], data[0], start=start, stop=False)
                mm(out_bank, weights[0], data[1], start=False, stop=False)
                return mm(out_bank, weights[1], data[0], start=False, stop=stop)

            def turn_norm(b, which, g):
                if which == 0 and g >= 2:
                    pe.wait_ge(h_ready, 2 * CH * b + g - 1)
                pe.wait_ge(norm_ready, 2 * BLK * b + which * BLK + (g + 1) * PER)
                dst = norm_bank(which, g)
                for k in range(PER):
                    last = pe.transpose(dst[:, k * P:(k + 1) * P], xn[:, g % 2 * PER + k, :], ident[:, :])
                last.then_inc(norm_turned, 1)

            def inputs(b, k):
                if NORM < k <= NORM + CH:
                    turn_norm(b, 0, k - NORM - 1)
                if NORM + 2 <= k < NORM + 2 + CH:
                    g = k - NORM - 2
                    pe.wait_ge(h_ready, 2 * CH * b + g + 1)
                    for i in range(g * PER, (g + 1) * PER):
                        last = mm(bank[2][:, 2 * i:2 * i + 2], hT[:, i * P:(i + 1) * P], tqT[:, :],
                                  start=True, stop=True)
                    if g == CH - 1:
                        last.then_inc(pos_ready, 1)
                if k == POSITIONS + 1:
                    pe.wait_ge(part_ready, 2 * b + 1)
                    mm(bank[2][:, 0:2], ones[:, :], part[:, :], start=True, stop=True).then_inc(part_summed, 1)
                if k == POSITIONS + 3:
                    pe.wait_ge(part_ready, 2 * b + 2)
                    mm(bank[2][:, 0:5], ones[:, :], mpart[:, :], start=True, stop=True).then_inc(part_summed, 1)
                if QUERIES <= k < QUERIES + 2 * CH:
                    m = k - QUERIES
                    if m >= 2:
                        pe.wait_ge(q_ready, 2 * CH * b + m - 1)
                    mm(bank[m % 2][:, :], wT[:, m // CH, :], hT[:, m % CH * W:(m % CH + 1) * W],
                       start=True, stop=True).then_inc(q_made, 1)
                if k == POSITIONS + 1 and b == 0:
                    spread_modulation((1, 0), bank[5])
                    pe.wait_ge(set_dve, 2)
                    mm(bank[4][:, 0:P], wv[:, :], wT[:, 2, :], start=True, stop=True)
                    mm(bank[4][:, P:P + 1], wT[:, 2, :], cols[:, 2:3], start=True, stop=True).then_inc(set_pe, 1)
                if k == POSITIONS + 3 and b == 0:
                    pe.wait_ge(set_dve, 3)
                    for n in range(3):
                        last = mm(bank[6][:, n * P:(n + 1) * P], x3b[:, n, :], ident[:, :], start=True, stop=True)
                    last.then_inc(set_pe, 1)
                if k in VALUES[b]:
                    if b == 0:
                        pe.wait_ge(set_dve, 3)
                    if b and VALUES[b][k][0] == 0:
                        pe.wait_ge(spread_ready[1], CH * (b + 1))
                    for g in VALUES[b][k]:
                        if g >= 2:
                            pe.wait_ge(v_ready, CH * b + g - 1)
                        for j, i in enumerate(range(g * PER, (g + 1) * PER)):
                            last = mm(value_bank(b, g)[:, j * P:(j + 1) * P], hT[:, i * P:(i + 1) * P], vh[:, b, :],
                                      start=True, stop=True)
                        last.then_inc(v_made, 1)
                if k in (FEATURES, FEATURES + 1):
                    pe.wait_ge(feat_ready, b + 1)
                    for n in (2 * (k - FEATURES), 2 * (k - FEATURES) + 1):
                        if n == 1:
                            pe.wait_ge(q_ready, 2 * CH * b + 2 * CH - 1)
                        if n == 2:
                            pe.wait_ge(q_ready, 2 * CH * (b + 1))
                        if n == 3:
                            pe.wait_ge(feat_copied[0], 2 * b + 1)
                        for j in range(8):
                            last = pe.transpose(bank[FEAT_BANK[n]][0:FEAT, :].bitcast(BF16)[:, j * P:(j + 1) * P],
                                                (fr, fl)[n // 2][:, (n % 2) * 8 + j, :], identb[:, :])
                        last.then_inc(feat_turned, 1)
                if k in (SPREAD, SPREAD + 1):
                    for m in range(2):
                        pe.wait_ge(feat_copied[m], 2 * (b + 1))
                    for g in (2 * (k - SPREAD), 2 * (k - SPREAD) + 1):
                        lot = frT[:, g * W:(g + 1) * W]
                        if g >= 2:
                            pe.wait_ge(spread_ready[1], CH * b + g - 1)
                        mm(bank[g % 2][:, :], sely[:, :], lot, start=True, stop=True).then_inc(spread_made[1], 1)
                        if g:
                            pe.wait_ge(spread_ready[0], CH * b + g)
                        mm(bank[2][:, :], selx[:, :], lot, start=True, stop=True).then_inc(spread_made[0], 1)

            def attention(b, n):
                lag = behind(b)
                if n == 0:
                    pe.wait_ge(spread_ready[0], CH * (b + 1))
                    pe.wait_ge(spread_ready[1], CH * (b + 1))
                    pe.wait_ge(v_ready, CH * (b + 1))
                if n < NCH:
                    i, c = CHUNKS[n]
                    w = min(W, (i + 1) * P - c * W)
                    if n >= lag:
                        pe.wait_ge(dist_used, NCH * b + n - lag + 1)
                    d = ring(b, 1, n)
                    diag = c == CHUNKS_ROW[i] - 1
                    last = mm(d[:, 0:w], flT[:, i * P:(i + 1) * P], frT[:, c * W:c * W + w], start=True, stop=not diag)
                    if diag:
                        last = mm(d[:, w - P:w], minus[:, :], causal[:, :], start=False, stop=True)
                    last.then_inc(dist_made, 1)
                    if n >= lag:
                        pe.wait_ge(scores_masked, NCH * b + n - lag + 1)
                    pair(ring(b, 0, n)[:, 0:w], [qT[:, h, i * P:(i + 1) * P] for h in range(2)],
                         [kT[:, h, c * W:c * W + w] for h in range(2)]).then_inc(scores_made, 1)
                if n in TURN_AT:
                    m = TURN_AT[n]
                    i, g = CHUNKS[m]
                    pe.wait_ge(probs_ready, NCH * b + m + 1)
                    if m >= lag:
                        pe.wait_ge(turned_copied, NCH * b + m - lag + 1)
                    norms, combs = sum(at < n for at in SHIFT_AT), sum(at < n for at in COMB_AT)
                    if norms:
                        pe.wait_ge(h_ready, 2 * CH * b + CH + norms)
                    if n > LOGITS_AT:
                        pe.wait_ge(sig_ready, 2 * b + 1)
                    if combs and b == 0:
                        pe.wait_ge(comb_copied, combs)
                    for k in range(min(PER, i + 1 - g * PER)):
                        j = g * PER + k
                        last = pe.transpose(ring(b, 2, m)[:, k * P:(k + 1) * P],
                                            row[:, i % ROWS, j * P:(j + 1) * P], ident[:, :])
                    last.then_inc(probs_turned, 1)
                if n in PRODUCT_AT:
                    m = PRODUCT_AT[n]
                    i, g = CHUNKS[m]
                    pe.wait_ge(turned_copied, NCH * b + m + 1)
                    if i == 0 and b:
                        pe.wait_ge(comb_copied, 3)
                    if g == 0 and i >= lag:
                        pe.wait_ge(row_ready, BLK * b + i - lag + 1)
                    for k in range(min(PER, i + 1 - g * PER)):
                        j = g * PER + k
                        last = mm(ring(b, 3, i)[:, 0:P], ptr[:, m % 2, k * P:(k + 1) * P], v[:, j, :],
                                  start=(j == 0), stop=(j == i))
                    last.then_inc(turned_used, 1)
                if n in SHIFT_AT or n == LOGITS_AT or (n in COMB_AT and b == 0):
                    turned = sum(at <= n for at in TURN_AT)
                    pe.wait_ge(turned_copied, NCH * b + turned)
                if n in SHIFT_AT:
                    turn_norm(b, 1, SHIFT_AT[n])
                if n == LOGITS_AT:
                    logits(b, EARLY, bank[2])
                if n in COMB_AT and b == 0:
                    if COMB_AT[n] == 0:
                        pe.wait_ge(comb_ready, 1)
                    else:
                        pe.wait_ge(comb_copied, COMB_AT[n])
                    turn_weights(HALVES[COMB_AT[n]], bank[2])

            def logits(b, lot, dst):
                pe.wait_ge(mix_split, CH * b + lot[1] // PER)
                for i in range(*lot):
                    last = pair(dst[:, (i - lot[0]) * E:(i - lot[0] + 1) * E],
                                [h2[:, h, i * P:(i + 1) * P] for h in range(2)], [rT[:, h, :] for h in range(2)])
                last.then_inc(logits_made, 1)

            def turn_weights(lot, dst):
                for i in range(*lot):
                    last = pe.transpose(dst[0:3 * E, :].bitcast(BF16)[:, (i - lot[0]) * P:(i - lot[0] + 1) * P],
                                        cpart[:, i, :, :], identb[:, :])
                last.then_inc(comb_turned, 1)

            def late(b, t):
                if t == 1:
                    pe.wait_ge(row_ready, BLK * (b + 1))
                    turn_norm(b, 1, CH - 1)
                if t == 3:
                    logits(b, LAST, bank[7])
                if t == LATE_STEPS - 1 and b == 0:
                    pe.wait_ge(comb_ready, 2)
                    turn_weights(LAST, bank[7])

            def step(s):
                b, e, c = s // STEPS, s % EX, s // EX % CH
                data = [h2[:, h, c * W:(c + 1) * W] for h in range(2)]
                if s == 0:
                    pe.wait_ge(scores_masked, NCH)
                    pe.wait_ge(turned_copied, NCH)
                    pe.wait_ge(row_ready, BLK)
                    pe.wait_ge(stage_used, 6)
                def gate(s):
                    e, c = s % EX, s // EX % CH
                    if e == 0 and c in (0, CH - 1):
                        pe.wait_ge(mix_split, CH * (s // STEPS) + (CH if c else CH - 1))
                    if s and smooth(s - 1):
                        pe.wait_ge(hidden_ready, s)
                    elif s and smooth(s - 2):
                        pe.wait_ge(turned_copied, NB * NCH)
                    elif s:
                        pe.wait_ge(silu_ready, s - 1)
                    pair(gate_bank(s)[:, :], [wg[:, h, e, :] for h in range(2)],
                         [h2[:, h, c * W:(c + 1) * W] for h in range(2)]).then_inc(gate_made, 1)

                if s == 0:
                    gate(0)
                if s + 1 < NB * STEPS:
                    gate(s + 1)
                if smooth(s) and e < E:
                    if e == 0 and c in (0, CH - 1):
                        pe.wait_ge(comb_copied, 3 if c else 2)
                    if E * (s // EX) + e:
                        pe.wait_ge(silu_weighted, E * (s // EX) + e)
                    mm(bank[5][:, :], selw[:, e, :], combT[:, c * W:(c + 1) * W], start=True, stop=True)\
                        .then_inc(weight_made, 1)

                def up():
                    if s and smooth(s - 1):
                        pe.wait_ge(act_ready, s)
                    elif s and smooth(s - 2):
                        pe.wait_ge(silu_weighted, E * (s // EX))
                    elif s:
                        pe.wait_ge(act_ready, s - 1)
                    pair(up_bank(s)[:, :], [wu[:, h, e, :] for h in range(2)], data).then_inc(up_made, 1)

                if ends_chunk(s, 3) and smooth(s - 3):
                    f = (s - 3) // EX
                    pe.wait_ge(y_copied, f + 1)
                    for k in range(PER):
                        last = pe.transpose(bank[6][:, k * P:(k + 1) * P], ysb[:, k * P:(k + 1) * P], ident[:, :])
                    last.then_inc(y_turned, 1)
                    if s < NB * STEPS:
                        up()
                if 2 <= s < NB * STEPS + 2:
                    d = s - 2
                    pe.wait_ge(act_split, d + 1)
                    if smooth(d):
                        if d % EX == 0 and d:
                            pe.wait_ge(out_scaled, d // EX)
                        pair(bank[6][:, :], [wd[:, h, d % EX, :] for h in range(2)],
                             [gp[:, d % 3, h, :] for h in range(2)], start=(d % EX == 0), stop=(d % EX == EX - 1))\
                            .then_inc(down_made, 1)
                    else:
                        n = d - (NB - 1) * STEPS
                        if n == 0:
                            pe.wait_ge(scores_masked, NB * NCH)
                            pe.wait_ge(dist_used, NB * NCH)
                        if n >= 2:
                            pe.wait_ge(expert_added, n - 1)
                        for k in range(PER):
                            last = pair(down_bank(d)[:, k * P:(k + 1) * P],
                                        [gp[:, d % 3, h, k * P:(k + 1) * P] for h in range(2)],
                                        [wd[:, h, d % EX, :] for h in range(2)])
                        last.then_inc(down_made, 1)
                if s < NB * STEPS and not (ends_chunk(s, 3) and smooth(s - 3)):
                    up()

            run(inputs, attention, step, late)

        @block.vector
        def _(dve):
            chain = Chain(dve, dve_step)
            step, settle = chain.step, chain.settle

            def ask_root(lot):
                settle()
                dve.tensor_scalar(ve[:, lot], mv[:, lot, 1], EPS, None, ALU.add).then_inc(root_asked, 1)

            def input_stats(b, g):
                if g == 0:
                    dve.wait_ge(x_loaded, 16 * (b + 1))
                blocks = range(g * PER, (g + 1) * PER)
                for i in blocks:
                    step(dve.bn_stats(st[:, i, :], x[:, b * BLK + i, :]))
                settle()
                for i in blocks:
                    step(dve.bn_aggr(mv[:, i, :], st[:, i, :]))
                if g == CH - 1:
                    ask_root(slice(0, BLK))

            for g in range(CH):
                input_stats(0, g)
            dve.wait_ge(consts_ready, 1)
            dve.wait_ge(set_pe, 1)
            step(dve.tensor_copy(sc[:, :], bank[1][:, E + 2:E + 2 + NB]))
            settle()
            for b in range(NB):
                last = dve.tensor_scalar(scb[:, b, :], ones[:, :], sc[:, b:b + 1], None, ALU.mult)
            last.then_inc(set_dve, 1)
            dve.wait_ge(small_loaded, 16 * (SMALL))
            dve.wait_ge(set_pe, 2)
            step(dve.tensor_scalar(wT[:, 0:2, :], bank[0][:, 0:2 * P], QK_UP, None, ALU.mult))
            step(dve.tensor_scalar(colu[:, :], cols[:, 0:2], QK_UP, None, ALU.mult))
            step(dve.tensor_copy(wT[:, 2, :], bank[0][:, 2 * P:3 * P]))
            step(dve.tensor_scalar(rT[:, 0, :], bank[1][:, 0:E], W_UP, None, ALU.mult))
            step(dve.tensor_copy(tqT[:, :], bank[1][:, E:E + 2]))
            step(dve.tensor_copy(md[:, :, :], bank[2][:, 0:6 * NB]))
            settle()
            step(dve.tensor_scalar(md[:, 1, :], md[:, 1, :], 1.0, None, ALU.add))
            step(dve.tensor_scalar(md[:, 4, :], md[:, 4, :], 1.0, None, ALU.add))
            step(dve.scalar_tensor_tensor(out=rT[:, 1, :], in0=bank[1][:, 0:E], scalar=W_UP, in1=rT[:, 0, :],
                                          op0=ALU.mult, op1=ALU.subtract))
            settle()
            dve.sem_inc(set_dve, 1)

            def gates():
                dve.wait_ge(set_pe, 3)
                step(dve.tensor_scalar(gsgn, bank[3][:, :], 0.0, 2.0, ALU.is_ge, ALU.mult))
                step(dve.tensor_copy(graw, bank[3][:, :]))
                settle()
                step(dve.scalar_tensor_tensor(out=gmag, in0=graw, scalar=-1.0, in1=graw, op0=ALU.mult, op1=ALU.max))
                settle()
                step(dve.tensor_scalar(gmag, gmag, NEAR, None, ALU.max))
                settle()
                step(dve.scalar_tensor_tensor(out=gbc[:, :, :, :].rearrange("p b g d -> p (b g d)"),
                                              in0=gsgn, scalar=-1.0, in1=gmag,
                                              op0=ALU.add, op1=ALU.mult))

            def value_weights():
                dve.wait_ge(set_pe, 4)
                step(dve.tensor_scalar(x3[:, 0:2], wfq[:, :], 0.1, None, ALU.mult))
                step(dve.scalar_tensor_tensor(out=x3[:, 2:3], in0=cols[:, 4:5], scalar=0.1, in1=cols[:, 3:4],
                                              op0=ALU.mult, op1=ALU.add))
                settle()
                step(dve.tensor_tensor(x3[:, 2:3], bank[4][:, P:P + 1], x3[:, 2:3], ALU.add))
                for b in range(NB):
                    step(dve.tensor_tensor(vh[:, b, :], bank[4][:, 0:P], gbc[:, b, 0, :], ALU.mult))
                settle()
                for n in range(3):
                    step(dve.tensor_scalar(x3b[:, n, :], ones[:, :], x3[:, n:n + 1], None, ALU.mult))
                settle()
                dve.sem_inc(set_dve, 1)

            def spread_terms():
                dve.wait_ge(set_pe, 5)
                step(dve.tensor_copy(x3b[:, :, :], bank[6][:, 0:3 * P])); settle()
                for b in range(NB):
                    gate = gbc[:, b, 0:1, :]
                    ca, sa = (bank[5][:, (2 * b + n) * P:(2 * b + n + 1) * P] for n in range(2))
                    step(dve.scalar_tensor_tensor(out=terms[:, b, 3, :], in0=ca, scalar=1.0, in1=gate[:, 0, :],
                                                  op0=ALU.add, op1=ALU.mult))
                    step(dve.tensor_tensor(terms[:, b, 2, :], sa, x3b[:, 2, :], ALU.add))
                    step(dve.tensor_tensor(terms[:, b, 0:2, :], x3b[:, 0:2, :], gate.broadcast_to([P, 2, P]), ALU.mult))
                settle()
                for b in range(NB):
                    step(dve.tensor_tensor(terms[:, b, 2, :], terms[:, b, 2, :], gbc[:, b, 0, :], ALU.mult))
                settle()
                dve.sem_inc(set_dve, 1)

            def stats(b, i):
                step(dve.bn_stats(st[:, i, :], x[:, b * BLK + i, :])); settle()
                step(dve.bn_aggr(mv[:, i, :], st[:, i, :]))

            def layer_norm(b, which, g):
                if g >= 2 or which or b:
                    dve.wait_ge(norm_turned, 2 * CH * b + which * CH + g - 1)
                for k in range(PER):
                    i = g * PER + k
                    dve.tensor_scalar(xn[:, g % 2 * PER + k, :], x[:, b * BLK + i, :], mv[:, i, 0:1], rs[:, i:i + 1],
                                      ALU.subtract, ALU.mult).then_inc(norm_ready, 1)

            def inputs(b, k):
                if STATS <= k < STATS + CH and b:
                    input_stats(b, k - STATS)
                if NORM <= k < NORM + CH:
                    if k == NORM:
                        dve.wait_ge(root_ready, ROOTS * b + 1)
                    layer_norm(b, 0, k - NORM)
                if k == NORM + 1 and b == 0:
                    gates()
                if k == POSITIONS:
                    dve.wait_ge(pos_ready, b + 1)
                    step(dve.tensor_tensor(qp[:, :, :], bank[2][:, 0:2 * BLK].rearrange("p (i k) -> p i k", k=2),
                                           btq_bc[:, :].unsqueeze(1).broadcast_to([P, BLK, 2]), ALU.add))
                    settle()
                    step(dve.tensor_tensor(sq[:, :, :], qp[:, :, :], qp[:, :, :], ALU.mult))
                    dve.tensor_reduce(part[:, :], qp[:, :, :].rearrange("p i k -> p k i"), X, ALU.add)\
                       .then_inc(part_ready, 1)
                    settle()
                    step(dve.tensor_tensor(nrm[:, :], sq[:, :, 0], sq[:, :, 1], ALU.add)); settle()
                    dve.tensor_scalar(nrm[:, :], nrm[:, :], 1e-24, None, ALU.max).then_inc(root_asked, 1)
                if k == POSITIONS + 2:
                    dve.wait_ge(part_summed, 2 * b + 1)
                    step(dve.tensor_scalar(mean[:, :], bank[2][:, 0:2], 1.0 / N, None, ALU.mult)); settle()
                    step(dve.tensor_tensor(qc[:, :, :], qp[:, :, :],
                                           mean[:, :].unsqueeze(1).broadcast_to([P, BLK, 2]), ALU.subtract))
                    settle()
                    step(dve.tensor_tensor(mom[:, 0, :], qc[:, :, 0], qc[:, :, 0], ALU.mult))
                    step(dve.tensor_tensor(mom[:, 1, :], qc[:, :, 0], qc[:, :, 1], ALU.mult))
                    step(dve.tensor_tensor(mom[:, 2, :], qc[:, :, 1], qc[:, :, 1], ALU.mult))
                    settle()
                    step(dve.tensor_tensor(mom[:, 3, :], mom[:, 0, :], mom[:, 2, :], ALU.add)); settle()
                    step(dve.tensor_tensor(mom[:, 4, :], mom[:, 3, :], mom[:, 3, :], ALU.mult)); settle()
                    dve.tensor_reduce(mpart[:, :], mom[:, :, :], X, ALU.add).then_inc(part_ready, 1)
                    if b == 0:
                        value_weights()
                if k == POSITIONS + 4:
                    dve.wait_ge(part_summed, 2 * b + 2)
                    step(dve.tensor_copy(msum[:, :], bank[2][:, 0:5])); settle()
                    step(dve.tensor_tensor(m2[:, 0:4], msum[:, 0:4], msum[:, 0:4], ALU.mult))
                    step(dve.tensor_copy(m2[:, 4:5], msum[:, 4:5])); settle()
                    step(dve.tensor_tensor(m2[:, :], m2[:, :], vw[:, :], ALU.mult)); settle()
                    step(dve.tensor_reduce(var[:, :], m2[:, :], X, ALU.add)); settle()
                    dve.tensor_scalar(var[:, :], var[:, :], TINY, None, ALU.max).then_inc(root_asked, 1)
                    step(dve.tensor_copy(quant[:, :, 0:2], qc[:, :, :]))
                    step(dve.tensor_scalar(quant[:, :, 2], qc[:, :, 1], 1.0 / WEDGE, None, ALU.mult))
                    step(dve.tensor_scalar(quant[:, :, 3], mom[:, 3, :], -1.0, None, ALU.mult))
                    settle()
                    step(dve.tensor_scalar(nxi[:, :], quant[:, :, 0], -HUGE, None, ALU.mult))
                    step(dve.tensor_scalar(nyi[:, :], quant[:, :, 2], -HUGE, None, ALU.mult))
                    dve.wait_ge(root_ready, ROOTS * b + 2)
                    if b:
                        dve.wait_ge(base_ready, CH * b)
                    dve.tensor_tensor(unit[:, :, :], qp[:, :, :], runit[:, :].unsqueeze(2).broadcast_to([P, BLK, 2]),
                                      ALU.mult).then_inc(unit_ready, 1)
                if k == POSITIONS + 5:
                    dve.wait_ge(root_ready, ROOTS * b + 3)
                    step(dve.tensor_scalar(sdv[:, :], sdv[:, :], 1.25, None, ALU.mult)); settle()
                    step(dve.scalar_tensor_tensor(out=thr[:, :], in0=msum[:, 3:4], scalar=2.0 / N, in1=sdv[:, :],
                                                  op0=ALU.mult, op1=ALU.add))
                    settle()
                    step(dve.tensor_scalar(quant[:, :, 4], quant[:, :, 3], thr[:, 0:1], None, ALU.add)); settle()
                    step(dve.tensor_copy(parts[:, 0, :, :], quant[:, :, :])); settle()
                    step(dve.tensor_tensor(rest[:, :, :], quant[:, :, :], parts[:, 0, :, :], ALU.subtract)); settle()
                    step(dve.tensor_copy(parts[:, 1, :, :], rest[:, :, :])); settle()
                    step(dve.tensor_tensor(rest[:, :, :], rest[:, :, :], parts[:, 1, :, :], ALU.subtract)); settle()
                    step(dve.tensor_copy(parts[:, 2, :, :], rest[:, :, :])); settle()

                if k == POSITIONS + 6:
                    def by_part(a):
                        return parts[:, :, :, a].rearrange("p s i -> p i s")

                    for a in range(2):
                        o = 9 * a
                        step(dve.tensor_scalar(fl[:, :, o:o + 9].rearrange("p i (s t) -> p i s t", t=3),
                                               by_part(a).unsqueeze(3).broadcast_to([P, BLK, 3, 3]),
                                               2 * HUGE, None, ALU.mult))
                        step(dve.tensor_copy(fr[:, :, o:o + 9].rearrange("p i (s t) -> p i s t", s=3),
                                             by_part(a).unsqueeze(2).broadcast_to([P, BLK, 3, 3])))
                    step(dve.tensor_scalar(fl[:, :, 18:21], by_part(4), HUGE, None, ALU.mult))
                    step(dve.tensor_copy(fr[:, :, 21:24], by_part(3)))
                    step(dve.tensor_copy(fr[:, :, 24:27], by_part(2)))
                    settle()
                    dve.sem_inc(feat_ready, 1)
                if k == POSITIONS + 4 and b == 0:
                    spread_terms()
                if QUERIES + 1 <= k <= QUERIES + 2 * CH:
                    m = k - QUERIES - 1
                    q, n, lot = (qT, kT)[m // CH], m // CH, slice(m % CH * W, (m % CH + 1) * W)
                    dve.wait_ge(high_ready, 2 * CH * b + m + 1)
                    dve.scalar_tensor_tensor(out=q[:, 1, lot], in0=bank[m % 2][:, :], scalar=colu[:, n:n + 1],
                                             in1=q[:, 0, lot], op0=ALU.add, op1=ALU.subtract)\
                       .then_inc(q_ready, 1)
                if k in (FEATURES, FEATURES + 1):
                    n = 2 * (k - FEATURES) + 1
                    dve.wait_ge(feat_turned, 4 * b + n + 1)
                    dve.tensor_copy(turned_features(n), bank[FEAT_BANK[n]][0:FEAT, :].bitcast(BF16))\
                       .then_inc(feat_copied[1], 1)
                if k in (SPREAD, SPREAD + 1):
                    for g in (2 * (k - SPREAD), 2 * (k - SPREAD) + 1):
                        dve.wait_ge(spread_made[0], CH * b + g + 1)
                        dve.tensor_copy(xb[:, g * W:(g + 1) * W], bank[2][:, :])\
                           .then_inc(spread_ready[0], 1)

            def split_input(b, g):
                lot = slice(g * W, (g + 1) * W)
                dve.wait_ge(mix_high, CH * b + g + 1)
                dve.scalar_tensor_tensor(out=h2[:, 1, lot], in0=hT[:, lot], scalar=H_UP, in1=h2[:, 0, lot],
                                         op0=ALU.mult, op1=ALU.subtract).then_inc(mix_split, 1)

            def finish(b, n):
                if n in FINISH_AT:
                    i = FINISH_AT[n]
                    dve.wait_ge(probs_ready, NCH * b + CHUNKS_BEFORE[i + 1])
                    step(dve.tensor_reduce(rinv[:, i:i + 1], rsum[:, i, 0:CHUNKS_ROW[i]], X, ALU.add)); settle()
                    step(dve.reciprocal(rinv[:, i:i + 1], rinv[:, i:i + 1])); settle()
                    dve.wait_ge(turned_used, NCH * b + CHUNKS_BEFORE[i + 1])
                    dve.wait_ge(base_ready, CH * b + i // PER + 1)
                    own = x[:, b * BLK + i, :]
                    dve.scalar_tensor_tensor(out=own, in0=ring(b, 3, i)[:, 0:P], scalar=rinv[:, i:i + 1],
                                             in1=own, op0=ALU.mult, op1=ALU.add).then_inc(row_ready, 1)

            def attention(b, n):
                if n < NCH:
                    i, c = CHUNKS[n]
                    L = (i + 1) * P
                    o = row[:, i % ROWS, :]
                    if by_pool(b, n):
                        dve.wait_ge(measure_ready, pooled(b, n))
                    else:
                        lot = slice(c * W, min((c + 1) * W, L))
                        dve.wait_ge(rise_ready, NCH * b + n + 1)
                        step(dve.scalar_tensor_tensor(out=o[:, lot], in0=xb[:, lot], scalar=nxi[:, i:i + 1],
                                                      in1=o[:, lot], op0=ALU.add, op1=ALU.subtract, reverse1=True))
                        settle()
                    w = min(W, L - c * W)
                    dve.wait_ge(dist_made, NCH * b + n + 1)
                    dve.scalar_tensor_tensor(out=pen[:, n % 2, 0:w], in0=ring(b, 1, n)[:, 0:w], scalar=0.0,
                                             in1=o[:, c * W:c * W + w], op0=ALU.min, op1=ALU.min)\
                       .then_inc(dist_used, 1)
                    dve.wait_ge(dist_used, NCH * b + n + 1)
                    dve.wait_ge(scores_made, NCH * b + n + 1)
                    dve.tensor_tensor_reduce(o[:, c * W:c * W + w], ring(b, 0, n)[:, 0:w], pen[:, n % 2, 0:w],
                                             float(P) ** -0.5 / QK_UP ** 2, -3.0e38, ALU.add, ALU.max,
                                             mx[:, i, c:c + 1]).then_inc(scores_masked, 1)
                    if c == CHUNKS_ROW[i] - 1:
                        dve.wait_ge(scores_masked, NCH * b + n + 1)
                        dve.tensor_reduce(nmx[:, i:i + 1], mx[:, i, 0:c + 1], X, ALU.max, negate=True)\
                           .then_inc(max_ready, 1)
                if n in FINISH_AT:
                    i = FINISH_AT[n]
                    dve.wait_ge(row_ready, BLK * b + i + 1)
                    stats(b, i)
                if n in ROOT_AT:
                    ask_root(slice(ROOT_AT[n] * PER, (ROOT_AT[n] + 1) * PER))
                if n in NORM_AT:
                    dve.wait_ge(root_ready, ROOTS * b + 4 + NORM_AT[n])
                    layer_norm(b, 1, NORM_AT[n])
                if n in SPLIT_AT:
                    split_input(b, SPLIT_AT[n])
                if n in ROUTE_AT:
                    routing(b, EARLY, ROUTE_AT[n])
                if n in COMB_AT and b == 0:
                    copy_weights(HALVES[COMB_AT[n]], COMB_AT[n], bank[2])

            def late(b, t):
                if t == 0:
                    dve.wait_ge(root_ready, ROOTS * (b + 1))
                    layer_norm(b, 1, CH - 1)
                if t == 2:
                    split_input(b, CH - 1)
                if 4 <= t < LATE_STEPS - 1 and t % PART_EVERY == 0:
                    routing(b, LAST, (t - 4) // PART_EVERY)
                if t == LATE_STEPS - 1 and b == 0:
                    copy_weights(LAST, 2, bank[7])

            def copy_weights(lot, n, src):
                dve.wait_ge(comb_turned, n + 1)
                dve.tensor_copy(combT[:, lot[0] * P:lot[1] * P],
                                src[0:3 * E, :].bitcast(BF16)[:, 0:(lot[1] - lot[0]) * P]).then_inc(comb_copied, 1)

            def routing(b, lot, part_of):
                cut = slice(*lot)
                count = lot[1] - lot[0]
                sig_, score_, pm_, ps2_, ps3_, gs_ = (t[:, cut] for t in (sig, score, pm, ps2, ps3, gs))
                gcmp_, geq_, grank_, gsel_ = (t[:, cut] for t in (gcmp, geq, grank, gsel))
                hits_, hit_, crest_, comb_ = (t[:, cut] for t in (hits, hit, crest, comb))
                wsum_ = wsum[:, cut]
                if part_of == 0:
                    dve.wait_ge(sig_ready, 2 * b + (1 if lot == EARLY else 2))
                    step(dve.tensor_scalar(sig_, sig_, 1.0, 0.5, ALU.add, ALU.mult)); settle()
                    step(dve.tensor_tensor(score_, sig_, rb_bc[:, :].unsqueeze(1).broadcast_to([P, count, E]), ALU.add))
                    settle()
                    pairs = score_.rearrange("p i (g a c) -> p (i g) a c", g=GRP, a=2)
                    for n, op in enumerate((ALU.max, ALU.min)):
                        step(dve.tensor_tensor(pm_[:, :, :, :, n].rearrange("p i g a -> p (i g) a"),
                                               pairs[:, :, :, 0], pairs[:, :, :, 1], op))
                    settle()
                    step(dve.tensor_tensor(ps2_[:, :, :, 0], pm_[:, :, :, 0, 0], pm_[:, :, :, 1, 0], ALU.max))
                    step(dve.tensor_tensor(ps3_[:, :, :, 0], pm_[:, :, :, 0, 0], pm_[:, :, :, 1, 0], ALU.min))
                    step(dve.tensor_tensor(ps3_[:, :, :, 1], pm_[:, :, :, 0, 1], pm_[:, :, :, 1, 1], ALU.max))
                    settle()
                    step(dve.tensor_tensor(ps2_[:, :, :, 1], ps3_[:, :, :, 0], ps3_[:, :, :, 1], ALU.max)); settle()
                    step(dve.tensor_tensor(gs_, ps2_[:, :, :, 0], ps2_[:, :, :, 1], ALU.add)); settle()
                if part_of == 1:
                    mine = gs_.unsqueeze(3).broadcast_to([P, count, GRP, GRP])
                    other = gs_.unsqueeze(2).broadcast_to([P, count, GRP, GRP])
                    step(dve.tensor_tensor(gcmp_, other, mine, ALU.is_gt))
                    step(dve.tensor_tensor(geq_, other, mine, ALU.is_equal))
                    settle()
                    equal = geq_.rearrange("p i g o -> p i (g o)")
                    step(dve.tensor_tensor(equal, equal,
                                           tri[:, :, :].rearrange("p g o -> p (g o)").unsqueeze(1)
                                           .broadcast_to([P, count, GRP * GRP]), ALU.mult))
                    settle()
                    step(dve.tensor_tensor(gcmp_, gcmp_, geq_, ALU.add)); settle()
                    step(dve.tensor_reduce(grank_, gcmp_, X, ALU.add)); settle()
                    step(dve.tensor_scalar(gsel_, grank_, 2.0, None, ALU.is_lt)); settle()
                if part_of == 2:
                    chosen = gsel_.unsqueeze(3).broadcast_to([P, count, GRP, EPG])
                    wide = score_.rearrange("p i (g m) -> p i g m", g=GRP)
                    step(dve.tensor_tensor(wide, wide, chosen, ALU.mult)); settle()
                    step(dve.tensor_tensor(wide, wide, chosen, ALU.add)); settle()
                    step(dve.tensor_scalar(score_, score_, -1.0, None, ALU.add)); settle()
                    for i in range(*lot):
                        step(dve.max(best[:, i, :], score[:, i, :]))
                    settle()
                if part_of == 3:
                    for i in range(*lot):
                        step(dve.max_index(bidx[:, i, :], best[:, i, :], score[:, i, :]))
                    settle()
                    step(dve.tensor_copy(bf[:, cut], bidx[:, cut])); settle()
                if part_of == 4:
                    every = iota[:, :].unsqueeze(1).broadcast_to([P, count, E])
                    for m in range(TOP):
                        step(dve.tensor_tensor(hit_ if m else hits_, every,
                                               bf[:, cut, m:m + 1].broadcast_to([P, count, E]), ALU.is_equal))
                        settle()
                        if m:
                            step(dve.tensor_tensor(hits_, hits_, hit_, ALU.add)); settle()
                if part_of == 5:
                    step(dve.tensor_tensor(comb_, hits_, sig_, ALU.mult)); settle()
                    step(dve.tensor_reduce(wsum_, comb_, X, ALU.add)); settle()
                    step(dve.tensor_scalar(wsum_, wsum_, 1e-20, None, ALU.add)); settle()
                    step(dve.reciprocal(wsum_, wsum_)); settle()
                    up = SCALE if b + 1 < NB else SCALE / (G_UP * W_UP)
                    step(dve.tensor_scalar(wsum_, wsum_, up, None, ALU.mult)); settle()
                    step(dve.tensor_tensor(comb_, comb_, wsum_.unsqueeze(2).broadcast_to([P, count, E]), ALU.mult))
                    settle()
                    if b + 1 == NB:
                        return
                    high, mid, low = (cpart[:, cut, n, :] for n in range(3))
                    step(dve.tensor_copy(high, comb_)); settle()
                    step(dve.tensor_tensor(crest_, comb_, high, ALU.subtract)); settle()
                    step(dve.tensor_copy(mid, crest_)); settle()
                    step(dve.tensor_tensor(crest_, crest_, mid, ALU.subtract)); settle()
                    dve.tensor_copy(low, crest_).then_inc(comb_ready, 1)

            def hidden(s):
                dve.wait_ge(silu_ready, s + 1)
                if s >= 2:
                    dve.wait_ge(act_ready, s - 1)
                dve.scalar_tensor_tensor(out=hid[:, s % 2, :], in0=sg[:, s % 2, :], scalar=1.0, in1=bank[3][:, :],
                                         op0=ALU.add, op1=ALU.mult).then_inc(hidden_ready, 1)

            def output(f, src):
                dve.tensor_tensor(scaled[:, :, :], src[:, :].rearrange("p (k d) -> p k d", d=P),
                                  gbc[:, f // CH, 1:2, :].broadcast_to([P, PER, P]), ALU.mult)\
                   .then_inc(out_scaled, 1)
                dve.wait_ge(out_scaled, f + 1)
                o = x[:, f * PER:(f + 1) * PER, :]
                dve.tensor_tensor(o, o, scaled[:, :, :], ALU.add).then_inc(out_ready, 1)

            def mix_beside(s):
                e = s % EX
                n = E * (s // EX) + e
                if s == 0:
                    hidden(0)
                dve.wait_ge(hidden_ready, s + 1)
                src = hid[:, s % 2, :]
                if s >= 2:
                    dve.wait_ge(act_ready, s - 1)
                    dve.wait_ge(act_split, s - 1)
                if e < E:
                    dve.wait_ge(weight_made, n + 1)
                    dve.tensor_tensor(sw[:, s % 2, :], bank[5][:, :], src, ALU.mult).then_inc(silu_weighted, 1)
                if smooth(s + 1):
                    hidden(s + 1)
                if ends_chunk(s, 3):
                    dve.wait_ge(y_turned, (s - 3) // EX + 1)
                    output((s - 3) // EX, bank[6])
                dve.wait_ge(up_made, s + 1)
                if e < E:
                    dve.wait_ge(silu_weighted, n + 1)
                    dve.tensor_tensor(act_g[:, s % 2, :], up_bank(s)[:, :], sw[:, s % 2, :], ALU.mult)\
                       .then_inc(act_ready, 1)
                else:
                    dve.scalar_tensor_tensor(out=act_g[:, s % 2, :], in0=up_bank(s)[:, :],
                                             scalar=G_UP / (H_UP * W_UP) ** 2 / 2, in1=src,
                                             op0=ALU.mult, op1=ALU.mult).then_inc(act_ready, 1)

            def add_expert(d):
                e, c = d % EX, d // EX % CH
                n = d - (NB - 1) * STEPS
                dve.wait_ge(down_made, d + 1)
                if e == 0:
                    dve.wait_ge(out_ready, d // EX)
                if n:
                    dve.wait_ge(expert_added, n)
                for k in range(PER):
                    y = down_bank(d)[:, k * P:(k + 1) * P]
                    own = scaled[:, k, :]
                    weight = comb[:, c * PER + k, e:e + 1] if e < E else 1 / (G_UP * W_UP)
                    if e:
                        last = dve.scalar_tensor_tensor(out=own, in0=y, scalar=weight, in1=own,
                                                        op0=ALU.mult, op1=ALU.add)
                    else:
                        last = dve.tensor_scalar(own, y, weight, None, ALU.mult)
                last.then_inc(expert_added, 1)

            def mix(s):
                if smooth(s):
                    mix_beside(s)
                    return
                if ends_chunk(s, 3) and smooth(s - 3):
                    dve.wait_ge(y_turned, (s - 3) // EX + 1)
                    output((s - 3) // EX, bank[6])
                if s < NB * STEPS:
                    dve.wait_ge(silu_ready, s + 1)
                    dve.wait_ge(up_made, s + 1)
                    dve.wait_ge(act_split, s - 1)
                    dve.scalar_tensor_tensor(out=act_g[:, s % 2, :], in0=up_bank(s)[:, :], scalar=G_UP / (H_UP * W_UP),
                                             in1=sg[:, s % 2, :], op0=ALU.mult, op1=ALU.mult).then_inc(act_ready, 1)
                if not smooth(s - 2) and s < NB * STEPS + 2:
                    add_expert(s - 2)
                    if ends_chunk(s, 2):
                        dve.wait_ge(expert_added, s - 1 - (NB - 1) * STEPS)
                        output((s - 2) // EX, ysb)

            run(inputs, attention, mix, late, finish)

_INS = ["L0_attn_hidden_states", "L0_attn_Wq", "L0_attn_bq", "L0_attn_Wk", "L0_attn_bk", "L0_attn_Wv",
        "L0_attn_bv", "L0_attn_Wo", "L0_attn_bo", "L0_attn_Wtq", "L0_attn_btq", "L0_attn_Wfq", "L0_attn_bfq",
        "L0_ffn_router_w", "L0_ffn_bias", "L0_ffn_gate_w", "L0_ffn_up_w", "L0_ffn_down_w", "L0_ffn_sh_gate_w",
        "L0_ffn_sh_up_w", "L0_ffn_sh_down_w", "L0_c", "L0_wmod"]


def kernel(**inputs):
    import concourse.bacc as _bacc
    from concourse.bass_utils import run_bass_kernel_spmd as _run

    nc = _bacc.Bacc("TRN2", target_bir_lowering=False, num_devices=1)
    arrays, args = {}, []
    for name in _INS:
        a = np.ascontiguousarray(inputs[name])
        arrays[f"in_{name}"] = a
        args.append(nc.dram_tensor(f"in_{name}", a.shape, mybir.dt.from_np(a.dtype), kind="ExternalInput").ap())
    args.append(nc.dram_tensor("out_x", (NB, N, P), F32, kind="ExternalOutput").ap())
    build(nc, *args)
    r = _run(nc, [arrays], core_ids=[0])
    return r.results[0]["out_x"]
```
